# Optimizing a Trainium2 kernel written in Bass

```python
import numpy as np
import jax
import jax.numpy as jnp

def _softmax(x, axis=-1):
    return jax.nn.softmax(x, axis=axis)

def _gelu(x):
    return jax.nn.gelu(x, approximate=True)

def _silu(x):
    return jax.nn.silu(x)

def _sigmoid(x):
    return jax.nn.sigmoid(x)

def _layernorm(x, axis=-1, eps=1e-05):
    m = jnp.mean(x, axis=axis, keepdims=True)
    v = jnp.var(x, axis=axis, keepdims=True)
    return (x - m) / jnp.sqrt(v + eps)

def _scatter_add(tgt, idx, src, axis=0):
    return tgt.at[idx].add(src)

def _segment_sum(src, seg, n):
    return jax.ops.segment_sum(src, seg, n)
kernel_name = 'mk_decoder_postln_d1_seqx_r4_678064'

def setup_inputs(seed: int=0):
    np.random.seed(seed)
    _w = jnp.asarray

    def _rec_inputs():
        import jax
        import jax.numpy as jnp
        _rk = jax.random.key(seed)
        x = -0.0002928 + 1 * jax.random.normal(jax.random.fold_in(_rk, 1), (16, 100, 512), jnp.float32)
        _lenS = 100 - jax.random.randint(jax.random.fold_in(_rk, 7), (16,), 0, max(1, 100 // 4) + 1, jnp.int32)
        _lenS2 = 361 - jax.random.randint(jax.random.fold_in(_rk, 8), (16,), 0, max(1, 361 // 4) + 1, jnp.int32)
        _ctx_2048P = jax.random.normal(jax.random.fold_in(_rk, 11), (16, 16, 512), jnp.float32)
        _ctx_2048c = jax.random.dirichlet(jax.random.fold_in(_rk, 511), 0.3 * jnp.ones((16,), jnp.float32), (16, 361))
        _ctx_2048t = jnp.einsum('bsk,bkd->bsd', _ctx_2048c, _ctx_2048P)
        _ctx_2048t = _ctx_2048t * jax.lax.rsqrt(jnp.mean(jnp.square(_ctx_2048t)) + 1e-12) * 0.953939
        ctx_2048 = 4.13588e-05 + 0.999923 * (_ctx_2048t + 0.3 * jax.random.normal(jax.random.fold_in(_rk, 611), (16, 361, 512), jnp.float32))
        _validS = jnp.arange(100)[None, :] < _lenS[:, None]
        _validS2 = jnp.arange(361)[None, :] < _lenS2[:, None]
        _causal = jnp.tril(jnp.ones((100, 100), dtype=bool))
        mask_1xSxS2_ff0 = jnp.where(jnp.ones((1, 100, 361), dtype=bool), 0.0, -1000000000.0).astype(jnp.float32)
        return (x, ctx_2048, mask_1xSxS2_ff0)
    x, ctx_2048, mask_1xSxS2_ff0 = _rec_inputs()

    def _L0_attn_setup():
        import jax, jax.numpy as jnp
        import numpy as np
        B, S, H, NH = (4, 512, 512, 16)
        HD = H // NH
        CAUSAL = True
        key = jax.random.key(seed)
        ks = jax.random.split(key, 5)
        mk = lambda k: jax.random.normal(k, (H, H), dtype=jnp.float32) * 0.02
        return {'x': jax.random.normal(ks[0], (B, S, H), dtype=jnp.float32), 'w_q': mk(ks[1]), 'w_k': mk(ks[2]), 'w_v': mk(ks[3]), 'w_o': mk(ks[4])}
    _L0_attn_all = _L0_attn_setup()
    _L0_attn_in = {k: v for k, v in _L0_attn_all.items() if k in ('w_q', 'w_k', 'w_v', 'w_o')}
    del _L0_attn_all

    def _L0_xattn_setup():
        import jax, jax.numpy as jnp
        import numpy as np
        H = 512
        NH = 16
        NKV = 4
        HD = 128
        GROUPS = NH // NKV
        EPS = 1e-06
        B, S, SE = (1, 512, 1024)

        def _rmsnorm(x, w, eps=EPS):
            xf = x.astype(jnp.float32)
            var = jnp.mean(xf * xf, axis=-1, keepdims=True)
            return (xf * jax.lax.rsqrt(var + eps)).astype(x.dtype) * w
        key = jax.random.key(seed)
        ks = jax.random.split(key, 12)
        sc = 0.02
        return {'hidden_states': jax.random.normal(ks[0], (B, S, H), jnp.float32), 'encoder_hidden_states': jax.random.normal(ks[1], (B, SE, H), jnp.float32), 'attention_mask': jnp.zeros((B, S, SE), jnp.float32), 'Wq': jax.random.normal(ks[2], (H, NH * HD), jnp.float32) * sc, 'bq': jax.random.normal(ks[3], (NH * HD,), jnp.float32) * sc, 'Wk': jax.random.normal(ks[4], (H, NKV * HD), jnp.float32) * sc, 'bk': jax.random.normal(ks[5], (NKV * HD,), jnp.float32) * sc, 'Wv': jax.random.normal(ks[6], (H, NKV * HD), jnp.float32) * sc, 'bv': jax.random.normal(ks[7], (NKV * HD,), jnp.float32) * sc, 'Wo': jax.random.normal(ks[8], (NH * HD, H), jnp.float32) * sc, 'qn_w': jnp.ones((HD,), jnp.float32), 'kn_w': jnp.ones((HD,), jnp.float32)}
    _L0_xattn_all = _L0_xattn_setup()
    _L0_xattn_in = {k: v for k, v in _L0_xattn_all.items() if k in ('Wq', 'bq', 'Wk', 'bk', 'Wv', 'bv', 'Wo', 'qn_w', 'kn_w')}
    del _L0_xattn_all

    def _L0_ffn_setup():
        import jax, jax.numpy as jnp
        import numpy as np
        TOP_K = 2
        EPS = 1e-06
        key = jax.random.key(seed)
        ks = jax.random.split(key, 5)
        B, S, D, E = (4, 512, 512, 8)
        sd = 1.0 / np.sqrt(D)
        return {'x': jax.random.normal(ks[0], (B, S, D), jnp.float32), 'router_w': jax.random.normal(ks[1], (D, E), jnp.float32) * sd, 'router_b': jnp.zeros((E,), jnp.float32), 'expert_w': jax.random.normal(ks[2], (E, D, D), jnp.float32) * sd, 'expert_b': jnp.zeros((E, D), jnp.float32), 'proj_w': jax.random.normal(ks[3], (D, D), jnp.float32) * sd, 'proj_b': jnp.zeros((D,), jnp.float32), 'norm_w': jnp.ones((D,), jnp.float32)}
    _L0_ffn_all = _L0_ffn_setup()
    _L0_ffn_in = {k: v for k, v in _L0_ffn_all.items() if k in ('router_w', 'router_b', 'expert_w', 'expert_b', 'proj_w', 'proj_b', 'norm_w')}
    del _L0_ffn_all
    return {'x': x, 'ctx_2048': ctx_2048, 'mask_1xSxS2_ff0': mask_1xSxS2_ff0, 'L0_attn_w_q': _L0_attn_in['w_q'], 'L0_attn_w_k': _L0_attn_in['w_k'], 'L0_attn_w_v': _L0_attn_in['w_v'], 'L0_attn_w_o': _L0_attn_in['w_o'], 'L0_xattn_Wq': _L0_xattn_in['Wq'], 'L0_xattn_bq': _L0_xattn_in['bq'], 'L0_xattn_Wk': _L0_xattn_in['Wk'], 'L0_xattn_bk': _L0_xattn_in['bk'], 'L0_xattn_Wv': _L0_xattn_in['Wv'], 'L0_xattn_bv': _L0_xattn_in['bv'], 'L0_xattn_Wo': _L0_xattn_in['Wo'], 'L0_xattn_qn_w': _L0_xattn_in['qn_w'], 'L0_xattn_kn_w': _L0_xattn_in['kn_w'], 'L0_ffn_router_w': _L0_ffn_in['router_w'], 'L0_ffn_router_b': _L0_ffn_in['router_b'], 'L0_ffn_expert_w': _L0_ffn_in['expert_w'], 'L0_ffn_expert_b': _L0_ffn_in['expert_b'], 'L0_ffn_proj_w': _L0_ffn_in['proj_w'], 'L0_ffn_proj_b': _L0_ffn_in['proj_b'], 'L0_ffn_norm_w': _L0_ffn_in['norm_w']}

def reference(x, ctx_2048, mask_1xSxS2_ff0, L0_attn_w_q, L0_attn_w_k, L0_attn_w_v, L0_attn_w_o, L0_xattn_Wq, L0_xattn_bq, L0_xattn_Wk, L0_xattn_bk, L0_xattn_Wv, L0_xattn_bv, L0_xattn_Wo, L0_xattn_qn_w, L0_xattn_kn_w, L0_ffn_router_w, L0_ffn_router_b, L0_ffn_expert_w, L0_ffn_expert_b, L0_ffn_proj_w, L0_ffn_proj_b, L0_ffn_norm_w):
    import jax
    import jax.numpy as jnp

    def _L0_attn_ref(x, w_q, w_k, w_v, w_o):
        import jax, jax.numpy as jnp
        import numpy as np
        B, S, H, NH = (4, 512, 512, 16)
        HD = H // NH
        CAUSAL = True
        b, s, _ = x.shape
        q = (x @ w_q.T).reshape(b, s, NH, HD).transpose(0, 2, 1, 3)
        k = (x @ w_k.T).reshape(b, s, NH, HD).transpose(0, 2, 1, 3)
        v = (x @ w_v.T).reshape(b, s, NH, HD).transpose(0, 2, 1, 3)
        scale = 1.0 / jnp.sqrt(jnp.asarray(HD, dtype=x.dtype))
        score = jnp.einsum('bhqd,bhkd->bhqk', q, k) * scale
        if CAUSAL:
            mask = jnp.triu(jnp.ones((s, s), dtype=bool), k=1)
            score = jnp.where(mask, -jnp.inf, score)
        attn = jax.nn.softmax(score, axis=-1)
        o = jnp.einsum('bhqk,bhkd->bhqd', attn, v)
        o = o.transpose(0, 2, 1, 3).reshape(b, s, H)
        return o @ w_o.T

    def _L0_xattn_ref(hidden_states, encoder_hidden_states, attention_mask, Wq, bq, Wk, bk, Wv, bv, Wo, qn_w, kn_w):
        import jax, jax.numpy as jnp
        import numpy as np
        H = 512
        NH = 16
        NKV = 4
        HD = 128
        GROUPS = NH // NKV
        EPS = 1e-06
        B, S, SE = (1, 512, 1024)

        def _rmsnorm(x, w, eps=EPS):
            xf = x.astype(jnp.float32)
            var = jnp.mean(xf * xf, axis=-1, keepdims=True)
            return (xf * jax.lax.rsqrt(var + eps)).astype(x.dtype) * w
        b, s, _ = hidden_states.shape
        se = encoder_hidden_states.shape[1]
        q = (hidden_states @ Wq + bq).reshape(b, s, NH, HD).transpose(0, 2, 1, 3)
        k = (encoder_hidden_states @ Wk + bk).reshape(b, se, NKV, HD).transpose(0, 2, 1, 3)
        v = (encoder_hidden_states @ Wv + bv).reshape(b, se, NKV, HD).transpose(0, 2, 1, 3)
        k = jnp.repeat(k, GROUPS, axis=1)
        v = jnp.repeat(v, GROUPS, axis=1)
        q = _rmsnorm(q, qn_w)
        k = _rmsnorm(k, kn_w)
        scale = 1.0 / np.sqrt(HD).astype(np.float32)
        scores = jnp.einsum('bhsd,bhed->bhse', q, k) * scale
        scores = scores + attention_mask[:, None, :, :]
        probs = jax.nn.softmax(scores.astype(jnp.float32), axis=-1).astype(q.dtype)
        out = jnp.einsum('bhse,bhed->bhsd', probs, v)
        out = out.transpose(0, 2, 1, 3).reshape(b, s, NH * HD)
        return out @ Wo

    def _L0_ffn_ref(x, router_w, router_b, expert_w, expert_b, proj_w, proj_b, norm_w):
        import jax, jax.numpy as jnp
        import numpy as np
        TOP_K = 2
        EPS = 1e-06
        B, S, D = x.shape
        E = router_b.shape[0]
        logits = jnp.einsum('bsd,de->bse', x, router_w) + router_b
        topk_vals, topk_idx = jax.lax.top_k(logits, TOP_K)
        topk_w = jax.nn.softmax(topk_vals, axis=-1)
        full_w = jnp.sum(jax.nn.one_hot(topk_idx, E, dtype=x.dtype) * topk_w[..., None], axis=-2)
        xf = x.reshape(-1, D)
        h = jnp.einsum('td,edf->etf', xf, expert_w) + expert_b[:, None, :]
        expert_out = jax.nn.silu(h)
        combined = jnp.einsum('etf,te->tf', expert_out, full_w.reshape(-1, E)).reshape(B, S, D)
        out = jnp.einsum('bsd,df->bsf', combined, proj_w) + proj_b
        y = x + out
        rms = jnp.sqrt(jnp.mean(y * y, axis=-1, keepdims=True) + EPS)
        return norm_w * (y / rms)
    x = _layernorm(x + _L0_attn_ref(x, L0_attn_w_q, L0_attn_w_k, L0_attn_w_v, L0_attn_w_o), axis=-1)
    x = _layernorm(x + _L0_xattn_ref(x, ctx_2048, mask_1xSxS2_ff0, L0_xattn_Wq, L0_xattn_bq, L0_xattn_Wk, L0_xattn_bk, L0_xattn_Wv, L0_xattn_bv, L0_xattn_Wo, L0_xattn_qn_w, L0_xattn_kn_w), axis=-1)
    x = _layernorm(x + _L0_ffn_ref(x, L0_ffn_router_w, L0_ffn_router_b, L0_ffn_expert_w, L0_ffn_expert_b, L0_ffn_proj_w, L0_ffn_proj_b, L0_ffn_norm_w), axis=-1)
    return x

_drawn_inputs = setup_inputs


def setup_inputs(seed=0):
    import zlib

    import numpy as np

    out = dict(_drawn_inputs(seed))
    spreads = {'L0_xattn_qn_w': (1.0, 0.583),
     'L0_xattn_kn_w': (1.0, 0.6),
     'L0_ffn_router_b': (0.0, 0.1),
     'L0_ffn_expert_b': (0.0, 0.368),
     'L0_ffn_proj_b': (0.0, 0.1),
     'L0_ffn_norm_w': (1.0, 0.2)}
    factors = {'L0_attn_w_q': 3.359, 'L0_attn_w_k': 3.48, 'L0_xattn_bq': 6.482, 'L0_xattn_bk': 8.0}
    for name, (base, spread) in spreads.items():
        noise = np.random.default_rng([zlib.crc32(name.encode()), seed]).standard_normal(out[name].shape)
        drawn = base * np.exp(spread * noise) if base else spread * noise
        out[name] = jnp.asarray(drawn.astype(out[name].dtype))
    for name, factor in factors.items():
        out[name] = (out[name] * factor).astype(out[name].dtype)
    return out
```

```python
from contextlib import ExitStack

import concourse.bass as bass
from concourse import mybir

F32 = mybir.dt.float32
F32R = mybir.dt.float32r
ALU = mybir.AluOpType
ACT = mybir.ActivationFunctionType
AX = mybir.AxisListType

P = 128
B, S, D = 16, 100, 512
DC = D // P
BIG = 3.0e38
LN_EPS = 1e-5
RMS_EPS = 1e-6

SH, SHD = 16, 32
SR = P // SHD
XH, XKV, XHD = 16, 4, 128
XG = XH // XKV
SE = 361
KC, KT = 3, 121
SEP = KC * KT
SEQ = SE + 1
E = 8
GB = 4
GT = GB * S
G = B // GB


def wait(eng, sem, value):
    if not isinstance(value, int) or value > 0:
        eng.wait_ge(sem, value)


def product3(eng, out, lhi, llo, rhi, rlo, terms, first=True, last=True):
    mm = None
    n = 3 * len(terms)
    k = 0
    for c in terms:
        for l, r in ((lhi, rhi), (lhi, rlo), (llo, rhi)):
            mm = eng.matmul(out, lhsT=l(c), rhs=r(c), start=first and k == 0, stop=last and k == n - 1)
            k += 1
    return mm


def self_attention_phase(nc, sem, x_nat, xT, w_q, w_k, w_v, w_o, Wq, bq, qn_w, kn_w, causal, ident, x1_d, q_d):
    with ExitStack() as ctx:
        def sb(name, shape, dt=F32):
            return ctx.enter_context(nc.sbuf_tensor(name, shape, dt))

        ident_s = sb("a_ident", [P, P])
        causal_s = sb("a_causal", [S, S])
        half_s = sb("a_half", [P, XG])
        rms_eps_s = sb("a_rms_eps", [P, XG])
        ln_eps_s = sb("a_ln_eps", [P, 1])
        carry = sb("a_carry", [S, SR + 1])
        qkw_s = sb("a_qkw", [P, 4])
        bq_s = sb("a_bq", [S, XH * XHD])
        wq_s = sb("a_wq", [P, DC, D])
        wk_s = sb("a_wk", [P, DC, D])
        stage = sb("a_stage", [P, 2, DC, D])
        wvh, wvl = sb("a_wvh", [P, DC, D], F32R), sb("a_wvl", [P, DC, D], F32R)
        woh, wol = sb("a_woh", [P, DC, D], F32R), sb("a_wol", [P, DC, D], F32R)
        Wqh, Wql = sb("a_Wqh", [P, 4, DC, D], F32R), sb("a_Wql", [P, 4, DC, D], F32R)
        xTr = sb("a_xTr", [P, DC, S])
        xTh, xTl = sb("a_xTh", [P, DC, S], F32R), sb("a_xTl", [P, DC, S], F32R)
        xs = sb("a_xs", [S, D])
        qTs, kTs = sb("a_qTs", [P, DC, S]), sb("a_kTs", [P, DC, S])
        v_s = sb("a_v", [S, D])
        probs = sb("a_probs", [S, SR, DC, S])
        nmax = sb("a_nmax", [S, SH])
        psums = sb("a_psums", [S, SR, DC])
        rinv = sb("a_rinv", [S, SR, DC])
        pT = sb("a_pT", [S, SR, DC, S])
        o_s = sb("a_o", [S, D])
        oTh, oTl = sb("a_oTh", [P, DC, S], F32R), sb("a_oTl", [P, DC, S], F32R)
        x1_s = sb("a_x1", [S, D])
        stat = sb("a_stat", [S, 6])
        mv = sb("a_mv", [S, 2])
        rstd = sb("a_rstd", [S, 1])
        x1Th, x1Tl = sb("a_x1Th", [P, DC, S], F32R), sb("a_x1Tl", [P, DC, S], F32R)
        qn = sb("a_qn", [S, XKV, XG * XHD])
        junk = sb("a_junk", [S, XG * XHD])
        qss = sb("a_qss", [S, XH])
        qrs = sb("a_qrs", [S, XH])
        qo = sb("a_qo", [P, 2, 2, XG * S], F32R)

        bank = [ctx.enter_context(nc.psum_tensor(f"a_bank{k}", [P, 512], F32)) for k in range(8)]
        s_bank = bank[0:SR]

        consts, w_raw, w_hi, w_lo = sem("a_consts"), [sem("a_w_raw0"), sem("a_w_raw1")], sem("a_w_hi"), sem("a_w_lo")
        wqk_in, half_set, qkw_set = sem("a_wqk_in"), sem("a_half_set"), sem("a_qkw_set")
        xT_in, x_in, xT_hi, xT_lo = sem("xT_in"), sem("x_in"), sem("xT_hi"), sem("xT_lo")
        qs_done, ks_done, qs_ev, ks_ev = sem("qs_done"), sem("ks_done"), sem("qs_ev"), sem("ks_ev")
        sc_done, t_rdy, p_rdy = sem("sc_done"), sem("t_rdy"), sem("p_rdy")
        pt_done, pt_ev, v_done, v_ev = sem("pt_done"), sem("pt_ev"), sem("v_done"), sem("v_ev")
        pv_done, rinv_set, o_rdy = sem("pv_done"), sem("rinv_set"), sem("o_rdy")
        oT_done, oT_hi, oT_lo, y_done = sem("oT_done"), sem("oT_hi"), sem("oT_lo"), sem("y_done")
        ysum, stat_set, mv_set, rstd_set, x1_rdy = sem("ysum"), sem("stat_set"), sem("mv_set"), sem("rstd_set"), sem("x1_rdy")
        x1T_done, x1T_hi, x1T_lo = sem("x1T_done"), sem("x1T_hi"), sem("x1T_lo")
        qx_done, q_ev, q_ss, q_rs, q_rdy = sem("qx_done"), sem("q_ev"), sem("q_ss"), sem("q_rs"), sem("q_rdy")
        qT_done, qT_hi, qT_lo = sem("qT_done"), sem("qT_hi"), sem("qT_lo")
        x1_out, q_out = sem("x1_out"), [sem("q_out0"), sem("q_out1")]

        pieces = [(w_v, wvh[:], wvl[:]), (w_o, woh[:], wol[:])]
        pieces += [(Wq[n], Wqh[:, n], Wql[:, n]) for n in range(4)]

        def over_batches(eng, body):
            body(0)
            body(1)
            with eng.Fori(2, B - 1) as i:
                body(i)
            body(B - 1)
            body(B)

        block = ctx.enter_context(nc.Block())

        @block.sync
        def _(sp):
            sp.dma_start(xTr[:], xT[0]).then_inc(xT_in, 16)
            sp.dma_start(wq_s[:], w_q).then_inc(wqk_in, 16)
            sp.dma_start(wk_s[:], w_k).then_inc(wqk_in, 16)
            sp.dma_start(ident_s[:], ident).then_inc(consts, 16)
            sp.dma_start(causal_s[:], causal).then_inc(consts, 16)
            sp.dma_start(qkw_s[:, 0:1], qn_w).then_inc(consts, 16)
            sp.dma_start(qkw_s[:, 1:2], kn_w).then_inc(consts, 16)
            sp.dma_start(stage[:, 0], pieces[0][0]).then_inc(w_raw[0], 16)
            sp.dma_start(xs[:], x_nat[0]).then_inc(x_in, 16)
            sp.dma_start(stage[:, 1], pieces[1][0]).then_inc(w_raw[1], 16)
            sp.dma_start(bq_s[:], bq.partition_broadcast(S)).then_inc(consts, 16)
            for n in range(2, len(pieces)):
                sp.wait_ge(w_lo, n - 1)
                sp.dma_start(stage[:, n % 2], pieces[n][0]).then_inc(w_raw[n % 2], 16)
            def body(i):
                is_int = isinstance(i, int)
                back, front = not (is_int and i == 0), not (is_int and i == B)
                if front and not (is_int and i == B - 1):
                    wait(sp, xT_lo, i + 1)
                    wait(sp, ks_done, i + 1)
                    sp.dma_start(xTr[:], xT[bass.ds(i + 1, 1)].rearrange("a p c t -> p (a c) t")).then_inc(xT_in, 16)
                if back:
                    wait(sp, x1_rdy, i)
                    sp.dma_start(x1_d[bass.ds(i - 1, 1)].rearrange("a t d -> t (a d)"), x1_s[:]).then_inc(x1_out, 16)
                    if front:
                        wait(sp, ysum, i)
                        sp.dma_start(xs[:], x_nat[bass.ds(i, 1)].rearrange("a t d -> t (a d)")).then_inc(x_in, 16)
                    for n in range(4):
                        wait(sp, qT_lo, 4 * (i - 1) + n + 1)
                        dst = q_d[bass.ds(4 * (i - 1) + n, 1)].rearrange("a p h t -> p (a h) t")
                        sp.dma_start(dst, qo[:, n % 2].bitcast(F32)).then_inc(q_out[n % 2], 16)
            over_batches(sp, body)
            sp.wait_ge(x1_out, 16 * B)
            for slot in q_out:
                sp.wait_ge(slot, 16 * 2 * B)

        @block.tensor
        def _(pe):
            def project_q(i):
                wait(pe, xT_in, 16 * (i + 1))
                for m in range(DC):
                    for c in range(DC):
                        mm = pe.matmul(bank[6][:, m * S:(m + 1) * S], lhsT=wq_s[:, c, m * P:(m + 1) * P],
                                       rhs=xTr[:, c, :], start=c == 0, stop=c == DC - 1)
                mm.then_inc(qs_done, 1)

            def project_k(i):
                for m in range(DC):
                    for c in range(DC):
                        mm = pe.matmul(bank[4][:, m * S:(m + 1) * S], lhsT=wk_s[:, c, m * P:(m + 1) * P],
                                       rhs=xTr[:, c, :], start=c == 0, stop=c == DC - 1)
                mm.then_inc(ks_done, 1)

            pe.wait_ge(wqk_in, 32)
            pe.wait_ge(consts, 80)
            project_q(0)
            project_k(0)

            def body(i):
                is_int = isinstance(i, int)
                back, front = not (is_int and i == 0), not (is_int and i == B)
                if front:
                    pe.wait_ge(qs_ev, i + 1)
                    pe.wait_ge(ks_ev, i + 1)
                    for r in range(SR):
                        for c in range(DC):
                            mm = pe.matmul(s_bank[r][0:S, c * S:(c + 1) * S], lhsT=qTs[r * SHD:(r + 1) * SHD, c, :],
                                           rhs=kTs[r * SHD:(r + 1) * SHD, c, :], start=True, stop=True)
                        mm.then_inc(sc_done, 1)
                if back:
                    wait(pe, x1_rdy, i)
                    for c in range(DC):
                        mm = pe.transpose(bank[6][:, c * S:(c + 1) * S], x1_s[:, c * P:(c + 1) * P], ident_s[0:S, 0:S])
                    mm.then_inc(x1T_done, 1)
                if front:
                    wait(pe, xT_lo, i + 1)
                    if is_int and i == 0:
                        pe.wait_ge(w_lo, 1)
                    product3(pe, bank[7][0:S, :], lambda c: xTh[:, c, :], lambda c: xTl[:, c, :],
                             lambda c: wvh[:, c, :], lambda c: wvl[:, c, :], range(DC)).then_inc(v_done, 1)
                if back:
                    wait(pe, x1T_lo, i)
                    for n in range(4):
                        if n >= 2:
                            wait(pe, q_ev, 4 * (i - 1) + n - 1)
                        if is_int and i == 1:
                            pe.wait_ge(w_lo, 3 + n)
                        product3(pe, bank[4 + n % 2][0:S, :], lambda c: x1Th[:, c, :], lambda c: x1Tl[:, c, :],
                                 lambda c: Wqh[:, n, c, :], lambda c: Wql[:, n, c, :], range(DC)).then_inc(qx_done, 1)
                if front:
                    for r in range(SR):
                        pe.wait_ge(p_rdy, 4 * i + r + 1)
                        for c in range(DC):
                            mm = pe.transpose(s_bank[r][0:S, c * S:(c + 1) * S], probs[:, r, c, :], ident_s[0:S, 0:S])
                        mm.then_inc(pt_done, 1)
                if back:
                    for n in range(4):
                        pe.wait_ge(q_rdy, 4 * (i - 1) + n + 1)
                        if n < 2:
                            pe.wait_ge(q_ev, 4 * (i - 1) + 3 + n)
                        else:
                            pe.wait_ge(qT_lo, 4 * (i - 1) + n - 1)
                        for h in range(XG):
                            mm = pe.transpose(bank[4 + n % 2][:, h * S:(h + 1) * S],
                                              qn[:, n, h * XHD:(h + 1) * XHD], ident_s[0:S, 0:S])
                        mm.then_inc(qT_done, 1)
                if front:
                    pe.wait_ge(v_ev, i + 1)
                    for r in range(SR):
                        pe.wait_ge(pt_ev, 4 * i + r + 1)
                        for c in range(DC):
                            h = SR * c + r
                            mm = pe.matmul(bank[7][0:S, h * SHD:(h + 1) * SHD], lhsT=pT[:, r, c, :],
                                           rhs=v_s[:, h * SHD:(h + 1) * SHD], start=True, stop=True)
                    mm.then_inc(pv_done, 1)
                    last = is_int and i == B - 1
                    if not last:
                        project_q(i + 1)
                    pe.wait_ge(o_rdy, i + 1)
                    if back:
                        wait(pe, qT_lo, 4 * i)
                    for c in range(DC):
                        mm = pe.transpose(bank[5][:, c * S:(c + 1) * S], o_s[:, c * P:(c + 1) * P], ident_s[0:S, 0:S])
                    mm.then_inc(oT_done, 1)
                    if not last:
                        project_k(i + 1)
                    pe.wait_ge(oT_lo, i + 1)
                    if is_int and i == 0:
                        pe.wait_ge(w_lo, 2)
                    product3(pe, bank[7][0:S, :], lambda c: oTh[:, c, :], lambda c: oTl[:, c, :],
                             lambda c: woh[:, c, :], lambda c: wol[:, c, :], range(DC)).then_inc(y_done, 1)
            over_batches(pe, body)

        @block.scalar
        def _(act):
            def split_hi(n):
                act.wait_ge(w_raw[n % 2], 16 * (n // 2 + 1))
                act.activation(pieces[n][1], stage[:, n % 2], ACT.Copy).then_inc(w_hi, 1)

            def scaled_q(i):
                wait(act, qs_done, i + 1)
                act.activation(qTs[:].rearrange("p c t -> p (c t)"), bank[6][:, 0:DC * S], ACT.Copy,
                               scale=float(SHD) ** -0.5).then_inc(qs_ev, 1)

            def split_xT(i):
                wait(act, xT_in, 16 * (i + 1))
                act.activation(xTh[:], xTr[:], ACT.Copy).then_inc(xT_hi, 1)

            split_xT(0)
            scaled_q(0)
            split_hi(0)
            split_hi(1)

            def body(i):
                is_int = isinstance(i, int)
                back, front = not (is_int and i == 0), not (is_int and i == B)
                if back:
                    wait(act, x1T_done, i)
                    act.activation(x1Th[:].rearrange("p c t -> p (c t)"), bank[6][:, 0:DC * S],
                                   ACT.Copy).then_inc(x1T_hi, 1)
                if front:
                    for r in range(SR):
                        act.wait_ge(t_rdy, 4 * i + r + 1)
                        for c in range(DC):
                            h = r * DC + c
                            e = act.activation(probs[:, r, c, :], probs[:, r, c, :], ACT.Exp, scale=-1.0,
                                               bias=nmax[:, h:h + 1], accum_out=psums[:, r, c:c + 1])
                        e.then_inc(p_rdy, 1)
                    act.wait_ge(v_done, i + 1)
                    act.activation(v_s[:], bank[7][0:S, :], ACT.Copy).then_inc(v_ev, 1)
                    for r in range(SR):
                        act.wait_ge(pt_done, 4 * i + r + 1)
                        act.activation(pT[:, r].rearrange("k c t -> k (c t)"), s_bank[r][0:S, 0:DC * S],
                                       ACT.Copy).then_inc(pt_ev, 1)
                if is_int and i == 0:
                    for n in range(2, 6):
                        split_hi(n)
                if back:
                    for n in range(4):
                        act.wait_ge(qT_done, 4 * (i - 1) + n + 1)
                        wait(act, q_out[n % 2], 16 * (2 * (i - 1) + n // 2))
                        act.activation(qo[:, n % 2, 0, :], bank[4 + n % 2][:, 0:XG * S], ACT.Copy,
                                       scale=qkw_s[:, 3:4]).then_inc(qT_hi, 1)
                if front:
                    last = is_int and i == B - 1
                    if not last:
                        scaled_q(i + 1)
                    act.wait_ge(oT_done, i + 1)
                    act.activation(oTh[:].rearrange("p c t -> p (c t)"), bank[5][:, 0:DC * S],
                                   ACT.Copy).then_inc(oT_hi, 1)
                    if not last:
                        split_xT(i + 1)
            over_batches(act, body)

        @block.vector
        def _(dve):
            def split_lo(n):
                dve.wait_ge(w_hi, n + 1)
                dve.tensor_tensor(pieces[n][2], stage[:, n % 2], pieces[n][1].bitcast(F32),
                                  ALU.subtract).then_inc(w_lo, 1)

            def copy_k(i):
                wait(dve, ks_done, i + 1)
                dve.tensor_copy(kTs[:].rearrange("p c t -> p (c t)"), bank[4][:, 0:DC * S]).then_inc(ks_ev, 1)

            def split_xT(i):
                wait(dve, xT_hi, i + 1)
                dve.tensor_tensor(xTl[:], xTr[:], xTh[:].bitcast(F32), ALU.subtract).then_inc(xT_lo, 1)

            dve.memset(half_s[:], -0.5).then_inc(half_set, 1)
            dve.memset(rms_eps_s[:], XHD * RMS_EPS).then_inc(half_set, 1)
            dve.memset(ln_eps_s[:], LN_EPS).then_inc(half_set, 1)
            split_xT(0)
            copy_k(0)
            dve.wait_ge(consts, 80)
            dve.tensor_tensor(qkw_s[:, 2:3], qkw_s[:, 0:1], qkw_s[:, 1:2], ALU.mult).then_inc(qkw_set, 1)
            dve.wait_ge(qkw_set, 1)
            dve.tensor_scalar(qkw_s[:, 3:4], qkw_s[:, 2:3], float(XHD) ** 0.5, None, ALU.mult).then_inc(qkw_set, 1)
            split_lo(0)
            split_lo(1)

            def masked(i, r):
                dve.wait_ge(sc_done, 4 * i + r + 1)
                dve.memset(carry[:, r:r + 1], 0.0)
                for c in range(DC):
                    h = r * DC + c
                    t = dve.tensor_tensor_reduce(out=probs[:, r, c, :], in0=s_bank[r][0:S, c * S:(c + 1) * S],
                                                 in1=causal_s[:], scale=-1.0, scalar=BIG, op0=ALU.add,
                                                 op1=ALU.min, accum_out=nmax[:, h:h + 1])
                t.then_inc(t_rdy, 1)

            def apply_rms(i, n):
                dve.wait_ge(q_rs, 2 * (4 * (i - 1) + n + 1))
                q4 = qn[:, n].rearrange("t (h d) -> t h d", h=XG)
                dve.tensor_tensor(q4, q4, qrs[:, XG * n:XG * (n + 1)].unsqueeze(2).to_broadcast([S, XG, XHD]),
                                  ALU.mult).then_inc(q_rdy, 1)

            def body(i):
                is_int = isinstance(i, int)
                back, front = not (is_int and i == 0), not (is_int and i == B)
                if front:
                    masked(i, 0)
                    masked(i, 1)
                if back:
                    wait(dve, x1T_hi, i)
                    dve.tensor_tensor(x1Tl[:].rearrange("p c t -> p (c t)"), bank[6][:, 0:DC * S],
                                      x1Th[:].bitcast(F32).rearrange("p c t -> p (c t)"),
                                      ALU.subtract).then_inc(x1T_lo, 1)
                if front:
                    masked(i, 2)
                    masked(i, 3)
                if is_int and i == 0:
                    for n in range(2, 6):
                        split_lo(n)
                if back:
                    for n in range(4):
                        dve.wait_ge(qx_done, 4 * (i - 1) + n + 1)
                        dve.tensor_tensor(qn[:, n], bank[4 + n % 2][0:S, :], bq_s[:, n * D:(n + 1) * D],
                                          ALU.add).then_inc(q_ev, 1)
                        if n:
                            dve.wait_ge(q_ss, 4 * (i - 1) + n)
                        dve.wait_ge(q_ev, 4 * (i - 1) + n + 1)
                        for h in range(XG):
                            q = qn[:, n, h * XHD:(h + 1) * XHD]
                            t = dve.tensor_tensor_reduce(out=junk[:, h * XHD:(h + 1) * XHD], in0=q, in1=q, scale=1.0,
                                                         scalar=0.0, op0=ALU.mult, op1=ALU.add,
                                                         accum_out=qss[:, XG * n + h:XG * n + h + 1])
                        t.then_inc(q_ss, 1)
                        if n:
                            apply_rms(i, n - 1)
                    apply_rms(i, 3)
                    for n in range(4):
                        dve.wait_ge(qT_hi, 4 * (i - 1) + n + 1)
                        dve.scalar_tensor_tensor(out=qo[:, n % 2, 1, :], in0=bank[4 + n % 2][:, 0:XG * S],
                                                 scalar=qkw_s[:, 3:4], in1=qo[:, n % 2, 0, :].bitcast(F32),
                                                 op0=ALU.mult, op1=ALU.subtract).then_inc(qT_lo, 1)
                if front:
                    last = is_int and i == B - 1
                    dve.wait_ge(p_rdy, 4 * i + 4)
                    dve.reciprocal(rinv[:], psums[:]).then_inc(rinv_set, 1)
                    dve.wait_ge(rinv_set, i + 1)
                    dve.wait_ge(pv_done, i + 1)
                    dve.tensor_tensor(o_s[:].rearrange("t (c r d) -> t c r d", c=DC, r=SR),
                                      bank[7][0:S, :].rearrange("t (c r d) -> t c r d", c=DC, r=SR),
                                      rinv[:].rearrange("t r c -> t c r").unsqueeze(3).to_broadcast([S, DC, SR, SHD]),
                                      ALU.mult).then_inc(o_rdy, 1)
                    dve.wait_ge(oT_hi, i + 1)
                    dve.tensor_tensor(oTl[:].rearrange("p c t -> p (c t)"), bank[5][:, 0:DC * S],
                                      oTh[:].bitcast(F32).rearrange("p c t -> p (c t)"),
                                      ALU.subtract).then_inc(oT_lo, 1)
                    if not last:
                        copy_k(i + 1)
                        split_xT(i + 1)
                    wait(dve, x1_out, 16 * i)
                    dve.wait_ge(x_in, 16 * (i + 1))
                    dve.wait_ge(y_done, i + 1)
                    dve.tensor_tensor(x1_s[:], bank[7][0:S, :], xs[:], ALU.add).then_inc(ysum, 1)
                    dve.wait_ge(ysum, i + 1)
                    dve.bn_stats(stat[:], x1_s[:]).then_inc(stat_set, 1)
                    dve.wait_ge(stat_set, i + 1)
                    dve.memset(carry[:, SR:SR + 1], 0.0)
                    dve.bn_aggr(mv[:], stat[:]).then_inc(mv_set, 1)
                    dve.wait_ge(rstd_set, 2 * (i + 1))
                    dve.tensor_scalar(x1_s[:], x1_s[:], mv[:, 0:1], rstd[:, 0:1], ALU.subtract,
                                      ALU.mult).then_inc(x1_rdy, 1)
            over_batches(dve, body)

        @block.gpsimd
        def _(pool):
            pool.wait_ge(half_set, 3)

            def body(i):
                is_int = isinstance(i, int)
                back, front = not (is_int and i == 0), not (is_int and i == B)
                if back:
                    for n in range(4):
                        k = 4 * (i - 1) + n
                        rs = qrs[:, XG * n:XG * (n + 1)]
                        pool.wait_ge(q_ss, k + 1)
                        pool.tensor_tensor(rs, qss[:, XG * n:XG * (n + 1)], rms_eps_s[0:S, :], ALU.add).then_inc(q_rs, 1)
                        pool.wait_ge(q_rs, 2 * k + 1)
                        pool.tensor_tensor(rs, rs, half_s[0:S, 0:XG], ALU.pow).then_inc(q_rs, 1)
                if front:
                    pool.wait_ge(mv_set, i + 1)
                    pool.tensor_tensor(rstd[:], mv[:, 1:2], ln_eps_s[0:S, :], ALU.add).then_inc(rstd_set, 1)
                    pool.wait_ge(rstd_set, 2 * i + 1)
                    pool.tensor_tensor(rstd[:], rstd[:], half_s[0:S, 0:1], ALU.pow).then_inc(rstd_set, 1)
            over_batches(pool, body)



def cross_attention_phase(nc, sem, ctxT, Wk, Wv, Wo, bk, bv, mask, ident, x1_d, q_d, x2_d):
    with ExitStack() as ctx:
        def sb(name, shape, dt=F32):
            return ctx.enter_context(nc.sbuf_tensor(name, shape, dt))

        ident_s = sb("b_ident", [P, P])
        mask_s = sb("b_mask", [S, SE])
        bk_s = sb("b_bk", [KT, XKV * XHD])
        bv_s = sb("b_bv", [P, XKV])
        half_s = sb("b_half", [P, XG])
        rms_eps_s = sb("b_rms_eps", [P, XG])
        ln_eps_s = sb("b_ln_eps", [P, 1])
        carry = sb("b_carry", [S, XG + 1])
        pcarry = sb("b_pcarry", [P, 16])
        stage = sb("b_stage", [P, 2, 2, D])
        Wkh, Wkl = sb("b_Wkh", [P, DC, D], F32R), sb("b_Wkl", [P, DC, D], F32R)
        Wvh, Wvl = sb("b_Wvh", [P, DC, D], F32R), sb("b_Wvl", [P, DC, D], F32R)
        Woh, Wol = sb("b_Woh", [P, XH, D], F32R), sb("b_Wol", [P, XH, D], F32R)
        q_s = sb("b_q", [P, 2, 2, XG * S], F32R)
        ctxr = sb("b_ctxr", [P, 2, DC, KT])
        ctxh, ctxl = sb("b_ctxh", [P, KC, DC, KT], F32R), sb("b_ctxl", [P, KC, DC, KT], F32R)
        kn = sb("b_kn", [KT, 2, XKV * XHD])
        junk = sb("b_junk", [KT, XKV * XHD])
        kss, krs = sb("b_kss", [KT, KC, XKV]), sb("b_krs", [KT, KC, XKV])
        kTh, kTl = sb("b_kTh", [P, 2, XKV, SEP + 1], F32R), sb("b_kTl", [P, 2, XKV, SEP + 1], F32R)
        Vh, Vl = sb("b_Vh", [KT, KC, XKV * XHD], F32R), sb("b_Vl", [KT, KC, XKV * XHD], F32R)
        probs = sb("b_probs", [S, 2, XG, SEP])
        nmax, psums, rinv = sb("b_nmax", [S, 2, XG]), sb("b_psums", [S, 2, XG]), sb("b_rinv", [S, 2, XG])
        pTh, pTl = sb("b_pTh", [KT, KC, XG * S], F32R), sb("b_pTl", [KT, KC, XG * S], F32R)
        oTh, oTl = sb("b_oTh", [P, XKV, XG * S], F32R), sb("b_oTl", [P, XKV, XG * S], F32R)
        x1_s, y_s = sb("b_x1", [S, D]), sb("b_y", [S, D])
        stat, mv, rstd = sb("b_stat", [S, 6]), sb("b_mv", [S, 2]), sb("b_rstd", [S, 1])

        bank = [ctx.enter_context(nc.psum_tensor(f"b_bank{k}", [P, 512], F32)) for k in range(8)]
        s_bank, t_bank, o_bank, kv_bank, y_bank = bank[0:2], bank[2:4], bank[4], bank[5:7], bank[7]

        consts, set_up = sem("b_consts"), sem("b_set_up")
        w_raw, w_hi, w_lo = [sem("b_w_raw0"), sem("b_w_raw1")], sem("b_w_hi"), sem("b_w_lo")
        q_in, ctx_in = [sem("b_q_in0"), sem("b_q_in1")], [sem("ctx_in0"), sem("ctx_in1")]
        ctx_hi, ctx_lo = sem("ctx_hi"), sem("ctx_lo")
        s_done, t_rdy, e_rdy, ri_set, p_rdy = sem("b_s_done"), sem("b_t_rdy"), sem("b_e_rdy"), sem("b_ri_set"), sem("b_p_rdy")
        pt_done, pt_hi, pt_lo = sem("b_pt_done"), sem("b_pt_hi"), sem("b_pt_lo")
        o_done, o_hi, o_lo = sem("b_o_done"), sem("b_o_hi"), sem("b_o_lo")
        v_done, v_hi, v_lo = sem("b_v_done"), sem("b_v_hi"), sem("b_v_lo")
        k_done, k_ev, k_ss, k_rs, k_rdy = sem("k_done"), sem("k_ev"), sem("k_ss"), sem("k_rs"), sem("k_rdy")
        kt_done, kt_hi, kt_lo = sem("kt_done"), sem("kt_hi"), sem("kt_lo")
        y_done, ysum, stat_set, mv_set = sem("b_y_done"), sem("b_ysum"), sem("b_stat_set"), sem("b_mv_set")
        rstd_set, x2_rdy, x1_in, x2_out = sem("b_rstd_set"), sem("x2_rdy"), sem("x1_in"), sem("x2_out")

        pieces = []
        for w, h, l, n in ((Wk, Wkh, Wkl, DC), (Wv, Wvh, Wvl, DC), (Wo, Woh, Wol, XH)):
            pieces += [(w[:, c:c + 2], h[:, c:c + 2], l[:, c:c + 2]) for c in range(0, n, 2)]
        KV_PIECES = 4
        KEY_BANK, KEY_T_BANK = (1, 0, 0), (1, 1, 0)

        def over_batches(eng, body):
            body(0, 0)
            with eng.Fori(0, B // 2 - 1) as pair:
                body(2 * pair + 1, 1)
                body(2 * pair + 2, 0)
            body(B - 1, 1)
            body(B, 0)

        def kinds(j):
            return [isinstance(j, int) and j == k for k in (0, B - 1, B)]

        def ctx_loads(jn, c):
            return 16 * (jn + 1) if c == 1 else 16 * (2 * jn + 1 + c // 2)

        block = ctx.enter_context(nc.Block())

        @block.sync
        def _(sp):
            def load_ctx(jn, c):
                if c == 0:
                    wait(sp, ctx_lo, 3 * jn)
                if c == 2:
                    sp.wait_ge(ctx_lo, 3 * jn + 1)
                src = ctxT[bass.ds(KC * jn + c, 1)].rearrange("a p c t -> p (a c) t")
                sp.dma_start(ctxr[:, c % 2], src).then_inc(ctx_in[c % 2], 16)

            def load_q(n, slot, free):
                wait(sp, s_done, free)
                src = q_d[bass.ds(n, 1)].rearrange("a p h t -> p (a h) t")
                sp.dma_start(q_s[:, slot].bitcast(F32), src).then_inc(q_in[slot], 16)

            def load_weights(n):
                if n >= 2:
                    sp.wait_ge(w_lo, n - 1)
                sp.dma_start(stage[:, n % 2], pieces[n][0]).then_inc(w_raw[n % 2], 16)

            load_ctx(0, 0)
            load_weights(0)
            load_weights(1)
            sp.dma_start(bk_s[:], bk.partition_broadcast(KT)).then_inc(consts, 16)
            sp.dma_start(ident_s[:], ident).then_inc(consts, 16)
            load_ctx(0, 1)
            load_q(0, 0, 0)
            sp.dma_start(mask_s[:], mask).then_inc(consts, 16)
            sp.dma_start(bv_s[:], bv).then_inc(consts, 16)
            load_ctx(0, 2)
            load_weights(2)
            load_weights(3)

            def body(j, par):
                first, last, past = kinds(j)
                if not past:
                    load_q(4 * j + 1, 1, 16 * j)
                    if not last:
                        load_ctx(j + 1, 0)
                        load_ctx(j + 1, 1)
                    if first:
                        for n in range(KV_PIECES, len(pieces)):
                            load_weights(n)
                    load_q(4 * j + 2, 0, 16 * j + 4)
                    if not last:
                        load_ctx(j + 1, 2)
                    load_q(4 * j + 3, 1, 16 * j + 8)
                    wait(sp, ysum, j)
                    sp.dma_start(x1_s[:], x1_d[bass.ds(j, 1)].rearrange("a t d -> t (a d)")).then_inc(x1_in, 16)
                if not first:
                    sp.wait_ge(x2_rdy, j)
                    sp.dma_start(x2_d[bass.ds(j - 1, 1)].rearrange("a t d -> t (a d)"), y_s[:]).then_inc(x2_out, 16)
                if not past and not last:
                    load_q(4 * j + 4, 0, 16 * j + 12)
            over_batches(sp, body)
            sp.wait_ge(x2_out, 16 * B)

        @block.tensor
        def _(pe):
            def scores(j, s, h, par):
                if h == 0:
                    pe.wait_ge(q_in[s % 2], 16 * (2 * j + s // 2 + 1))
                    if s == 0:
                        pe.wait_ge(kt_lo, 3 * (j + 1))
                wait(pe, t_rdy, 16 * j + 4 * s + h - 1)
                q = [q_s[:, s % 2, k, h * S:(h + 1) * S] for k in range(2)]
                k_ = [kTh[:, par, s, 0:SEQ], kTl[:, par, s, 0:SEQ]]
                product3(pe, s_bank[h % 2][0:S, 0:SEQ], lambda c: q[0], lambda c: q[1],
                         lambda c: k_[0], lambda c: k_[1], range(1)).then_inc(s_done, 1)

            def transpose_probs(n, s, c):
                if c == 0:
                    pe.wait_ge(p_rdy, 4 * n + 4)
                    wait(pe, pt_lo, 3 * n)
                if c == 2:
                    pe.wait_ge(pt_lo, 3 * n + 1)
                for h in range(XG):
                    mm = pe.transpose(t_bank[c % 2][0:KT, h * S:(h + 1) * S],
                                      probs[:, s % 2, h, c * KT:(c + 1) * KT], ident_s[0:S, 0:S])
                mm.then_inc(pt_done, 1)

            def values_product(n, kv, j):
                if kv == 0:
                    pe.wait_ge(v_lo, 3 * (j + 1))
                pe.wait_ge(pt_lo, 3 * n + 3)
                wait(pe, o_lo, n)
                cols = slice(kv * XHD, (kv + 1) * XHD)
                product3(pe, o_bank[:, 0:XG * S], lambda c: Vh[:, c, cols], lambda c: Vl[:, c, cols],
                         lambda c: pTh[:, c, :], lambda c: pTl[:, c, :], range(KC)).then_inc(o_done, 1)

            def values(j, c):
                if c == 2:
                    pe.wait_ge(v_lo, 3 * j + 1)
                product3(pe, kv_bank[c % 2][0:KT, :], lambda i: ctxh[:, c, i, :], lambda i: ctxl[:, c, i, :],
                         lambda i: Wvh[:, i, :], lambda i: Wvl[:, i, :], range(DC)).then_inc(v_done, 1)

            def keys(jn, c):
                pe.wait_ge(ctx_lo, 3 * jn + c + 1)
                if c < 2:
                    wait(pe, v_lo, 3 * (jn - 1) + c + 2)
                else:
                    pe.wait_ge(k_ev, 3 * jn + 2)
                product3(pe, kv_bank[KEY_BANK[c]][0:KT, :], lambda i: ctxh[:, c, i, :],
                         lambda i: ctxl[:, c, i, :], lambda i: Wkh[:, i, :], lambda i: Wkl[:, i, :],
                         range(DC)).then_inc(k_done, 1)

            def transpose_keys(jn, c):
                pe.wait_ge(k_rdy, 3 * jn + c + 1)
                if c == 1:
                    pe.wait_ge(kt_lo, 3 * jn + 1)
                for kv in range(XKV):
                    mm = pe.transpose(kv_bank[KEY_T_BANK[c]][:, kv * KT:(kv + 1) * KT],
                                      kn[:, c % 2, kv * XHD:(kv + 1) * XHD], ident_s[0:KT, 0:KT])
                mm.then_inc(kt_done, 1)

            def output(j, kv):
                pe.wait_ge(o_lo, 4 * j + kv + 1)
                if kv == 0:
                    wait(pe, ysum, j)
                mm = product3(pe, y_bank[0:S, :], lambda h: oTh[:, kv, h * S:(h + 1) * S],
                              lambda h: oTl[:, kv, h * S:(h + 1) * S], lambda h: Woh[:, XG * kv + h, :],
                              lambda h: Wol[:, XG * kv + h, :], range(XG), first=kv == 0, last=kv == XKV - 1)
                if kv == XKV - 1:
                    mm.then_inc(y_done, 1)

            pe.wait_ge(consts, 64)
            pe.wait_ge(w_lo, 2)
            keys(0, 0)
            keys(0, 1)
            transpose_keys(0, 0)
            keys(0, 2)
            transpose_keys(0, 1)
            transpose_keys(0, 2)

            def body(j, par):
                first, last, past = kinds(j)
                for s in range(1 if past else 4):
                    n, before = 4 * j + s, not (first and s == 0)
                    now = not past
                    for h in range(3):
                        if now:
                            scores(j, s, h, par)
                        if before:
                            transpose_probs(n - 1, (s + 3) % 4, h)
                    if s == 0 and not first:
                        output(j - 1, 2)
                    if s == 1:
                        values(j, 2)
                    if s in (2, 3) and not last:
                        keys(j + 1, s - 1)
                    if now:
                        scores(j, s, 3, par)
                    if before:
                        values_product(n - 1, (s + 3) % 4, j)
                    if s == 0 and now:
                        if first:
                            pe.wait_ge(w_lo, KV_PIECES)
                        values(j, 0)
                        values(j, 1)
                    if s == 1 and not last:
                        keys(j + 1, 0)
                    if s in (2, 3) and not last:
                        transpose_keys(j + 1, s - 2)
                    if s == 1 and not first:
                        output(j - 1, 3)
                    if s in (2, 3):
                        if first:
                            pe.wait_ge(w_lo, KV_PIECES + 2 * (s - 1))
                        output(j, s - 2)
                    if s == 3 and not last:
                        transpose_keys(j + 1, 2)
                if past:
                    output(j - 1, 3)
                elif first:
                    pe.wait_ge(w_lo, len(pieces))
            over_batches(pe, body)

        @block.scalar
        def _(act):
            def split_hi(n):
                act.wait_ge(w_raw[n % 2], 16 * (n // 2 + 1))
                act.activation(pieces[n][1], stage[:, n % 2], ACT.Copy).then_inc(w_hi, 1)

            def keys_hi(jn, c, par):
                act.wait_ge(kt_done, 3 * jn + c + 1)
                act.activation(kTh[:, par, :, c * KT:(c + 1) * KT],
                               kv_bank[KEY_T_BANK[c]][:, 0:XKV * KT].rearrange("d (k t) -> d k t", k=XKV),
                               ACT.Copy).then_inc(kt_hi, 1)

            def values_hi(j, c):
                act.wait_ge(v_done, 3 * j + c + 1)
                act.activation(Vh[:, c, :], kv_bank[c % 2][0:KT, :], ACT.Copy).then_inc(v_hi, 1)

            def probs_hi(n, c):
                act.wait_ge(pt_done, 3 * n + c + 1)
                act.activation(pTh[:, c, :], t_bank[c % 2][0:KT, 0:XG * S], ACT.Copy).then_inc(pt_hi, 1)

            def exponent(j, s, h):
                act.wait_ge(t_rdy, 16 * j + 4 * s + h + 1)
                p = probs[:, s % 2, h, 0:SE]
                act.activation(p, p, ACT.Exp, scale=-1.0, bias=nmax[:, s % 2, h:h + 1],
                               accum_out=psums[:, s % 2, h:h + 1]).then_inc(e_rdy, 1)

            for n in range(KV_PIECES):
                split_hi(n)
            act.wait_ge(consts, 64)
            for c in range(KC):
                keys_hi(0, c, 0)

            def body(j, par):
                first, last, past = kinds(j)
                for s in range(1 if past else 4):
                    n, before, now = 4 * j + s, not (first and s == 0), not past
                    for h in range(3):
                        if before:
                            probs_hi(n - 1, h)
                        if now:
                            exponent(j, s, h)
                    if s == 1:
                        values_hi(j, 2)
                    if now:
                        exponent(j, s, 3)
                    if before:
                        kv = (s + 3) % 4
                        act.wait_ge(o_done, n)
                        act.activation(oTh[:, kv, :], o_bank[:, 0:XG * S], ACT.Identity,
                                       bias=bv_s[:, kv:kv + 1]).then_inc(o_hi, 1)
                    if s == 0 and now:
                        values_hi(j, 0)
                        values_hi(j, 1)
                    if first and s < 2:
                        for k in range(4):
                            split_hi(KV_PIECES + 4 * s + k)
                    if s in (2, 3) and not last:
                        keys_hi(j + 1, s - 2, 1 - par)
                    if s == 3 and not last:
                        keys_hi(j + 1, 2, 1 - par)
            over_batches(act, body)

        @block.vector
        def _(dve):
            def split_lo(n):
                dve.wait_ge(w_hi, n + 1)
                dve.tensor_tensor(pieces[n][2], stage[:, n % 2], pieces[n][1].bitcast(F32),
                                  ALU.subtract).then_inc(w_lo, 1)

            def key_squares(jn, c):
                if c == 2:
                    dve.wait_ge(kt_done, 3 * jn + 1)
                dve.wait_ge(k_done, 3 * jn + c + 1)
                dve.tensor_tensor(kn[:, c % 2, :], kv_bank[KEY_BANK[c]][0:KT, :], bk_s[:], ALU.add).then_inc(k_ev, 1)
                wait(dve, k_ss, 3 * jn + c)
                dve.wait_ge(k_ev, 3 * jn + c + 1)
                for kv in range(XKV):
                    k_ = kn[:, c % 2, kv * XHD:(kv + 1) * XHD]
                    t = dve.tensor_tensor_reduce(out=junk[:, kv * XHD:(kv + 1) * XHD], in0=k_, in1=k_, scale=1.0,
                                                 scalar=0.0, op0=ALU.mult, op1=ALU.add,
                                                 accum_out=kss[:, c, kv:kv + 1])
                t.then_inc(k_ss, 1)

            def key_norm(jn, c):
                dve.wait_ge(k_rs, 2 * (3 * jn + c + 1))
                k4 = kn[:, c % 2, :].rearrange("t (k d) -> t k d", k=XKV)
                dve.tensor_tensor(k4, k4, krs[:, c, :].unsqueeze(2).to_broadcast([KT, XKV, XHD]),
                                  ALU.mult).then_inc(k_rdy, 1)

            def keys_lo(jn, c, par):
                dve.wait_ge(kt_hi, 3 * jn + c + 1)
                cols = slice(c * KT, (c + 1) * KT)
                dve.tensor_tensor(kTl[:, par, :, cols],
                                  kv_bank[KEY_T_BANK[c]][:, 0:XKV * KT].rearrange("d (k t) -> d k t", k=XKV),
                                  kTh[:, par, :, cols].bitcast(F32), ALU.subtract).then_inc(kt_lo, 1)

            def values_lo(j, c):
                dve.wait_ge(v_hi, 3 * j + c + 1)
                dve.tensor_tensor(Vl[:, c, :], kv_bank[c % 2][0:KT, :], Vh[:, c, :].bitcast(F32),
                                  ALU.subtract).then_inc(v_lo, 1)

            def probs_lo(n, c):
                dve.wait_ge(pt_hi, 3 * n + c + 1)
                dve.tensor_tensor(pTl[:, c, :], t_bank[c % 2][0:KT, 0:XG * S], pTh[:, c, :].bitcast(F32),
                                  ALU.subtract).then_inc(pt_lo, 1)

            def masked(j, s, h):
                dve.wait_ge(s_done, 16 * j + 4 * s + h + 1)
                dve.memset(carry[:, h:h + 1], 0.0)
                dve.tensor_tensor_reduce(out=probs[:, s % 2, h, 0:SE], in0=s_bank[h % 2][0:S, 0:SE], in1=mask_s[:],
                                         scale=-1.0, scalar=BIG, op0=ALU.add, op1=ALU.min,
                                         accum_out=nmax[:, s % 2, h:h + 1]).then_inc(t_rdy, 1)

            def invert_sums(j, s, h):
                dve.wait_ge(e_rdy, 16 * j + 4 * s + h + 2)
                dve.reciprocal(rinv[:, s % 2, h:h + 2], psums[:, s % 2, h:h + 2]).then_inc(ri_set, 1)

            dve.memset(half_s[:], -0.5).then_inc(set_up, 1)
            dve.memset(rms_eps_s[:], XHD * RMS_EPS).then_inc(set_up, 1)
            dve.memset(ln_eps_s[:], LN_EPS).then_inc(set_up, 1)
            dve.memset(probs[:, :, :, SE:SEP], 0.0).then_inc(set_up, 1)
            for n in range(KV_PIECES):
                split_lo(n)
            dve.wait_ge(consts, 64)
            key_squares(0, 0)
            key_squares(0, 1)
            key_norm(0, 0)
            keys_lo(0, 0, 0)
            key_squares(0, 2)
            key_norm(0, 1)
            keys_lo(0, 1, 0)
            key_norm(0, 2)
            keys_lo(0, 2, 0)

            def body(j, par):
                first, last, past = kinds(j)
                for s in range(1 if past else 4):
                    n, before, now = 4 * j + s, not (first and s == 0), not past
                    for h in range(3):
                        if now:
                            masked(j, s, h)
                        if before:
                            probs_lo(n - 1, h)
                    if s == 2 and not first:
                        residual_norm(j - 1)
                    if s == 1:
                        values_lo(j, 2)
                    if s in (2, 3) and not last:
                        key_norm(j + 1, s - 2)
                        key_squares(j + 1, s - 1)
                    if now:
                        masked(j, s, 3)
                        invert_sums(j, s, 0)
                    if before:
                        kv = (s + 3) % 4
                        dve.wait_ge(o_hi, n)
                        dve.scalar_tensor_tensor(out=oTl[:, kv, :], in0=o_bank[:, 0:XG * S], scalar=bv_s[:, kv:kv + 1],
                                                 in1=oTh[:, kv, :].bitcast(F32), op0=ALU.add,
                                                 op1=ALU.subtract).then_inc(o_lo, 1)
                    if now:
                        invert_sums(j, s, 2)
                    if s == 2 and not first:
                        apply_norm(j - 1)
                    if s == 0 and now:
                        values_lo(j, 0)
                        values_lo(j, 1)
                    if s == 1 and not last:
                        key_squares(j + 1, 0)
                    if first and s < 2:
                        for k in range(4):
                            split_lo(KV_PIECES + 4 * s + k)
                    if s in (2, 3) and not last:
                        keys_lo(j + 1, s - 2, 1 - par)
                    if s == 3 and not last:
                        key_norm(j + 1, 2)
                        keys_lo(j + 1, 2, 1 - par)
                if past:
                    residual_norm(j - 1)
                    apply_norm(j - 1)

            def residual_norm(j):
                wait(dve, x2_out, 16 * j)
                dve.wait_ge(x1_in, 16 * (j + 1))
                dve.wait_ge(y_done, j + 1)
                dve.tensor_tensor(y_s[:], y_bank[0:S, :], x1_s[:], ALU.add).then_inc(ysum, 1)
                dve.wait_ge(ysum, j + 1)
                dve.bn_stats(stat[:], y_s[:]).then_inc(stat_set, 1)
                dve.wait_ge(stat_set, j + 1)
                dve.memset(carry[:, XG:XG + 1], 0.0)
                dve.bn_aggr(mv[:], stat[:]).then_inc(mv_set, 1)

            def apply_norm(j):
                dve.wait_ge(rstd_set, 2 * (j + 1))
                dve.tensor_scalar(y_s[:], y_s[:], mv[:, 0:1], rstd[:, 0:1], ALU.subtract,
                                  ALU.mult).then_inc(x2_rdy, 1)
            over_batches(dve, body)

        @block.gpsimd
        def _(pool):
            def carry_wait(k):
                pool.tensor_tensor(pcarry[:, k:k + 1], half_s[:, 0:1], half_s[:, 0:1], ALU.add)

            def split_ctx(jn, c):
                pool.wait_ge(ctx_in[c % 2], ctx_loads(jn, c))
                wait(pool, v_done, 3 * (jn - 1) + c + 1)
                carry_wait(c)
                pool.tensor_scalar(ctxh[:, c], ctxr[:, c % 2], 1.0, 1.0, ALU.mult, ALU.mult).then_inc(ctx_hi, 1)
                pool.wait_ge(ctx_hi, 3 * jn + c + 1)
                pool.tensor_tensor(ctxl[:, c], ctxr[:, c % 2], ctxh[:, c].bitcast(F32),
                                   ALU.subtract).then_inc(ctx_lo, 1)

            def key_rsqrt(jn, c):
                k = 3 * jn + c
                pool.wait_ge(k_ss, k + 1)
                pool.tensor_tensor(krs[:, c, :], kss[:, c, :], rms_eps_s[0:KT, :], ALU.add).then_inc(k_rs, 1)
                pool.wait_ge(k_rs, 2 * k + 1)
                pool.tensor_tensor(krs[:, c, :], krs[:, c, :], half_s[0:KT, :], ALU.pow).then_inc(k_rs, 1)

            def normalise(j, s):
                n = 4 * j + s
                for h in range(XG):
                    if h % 2 == 0:
                        pool.wait_ge(ri_set, 2 * n + 1 + h // 2)
                        carry_wait(4 + 2 * s + h // 2)
                    p = probs[:, s % 2, h, 0:SE]
                    pool.tensor_scalar(p, p, rinv[:, s % 2, h:h + 1], 1.0, ALU.mult, ALU.mult).then_inc(p_rdy, 1)

            pool.wait_ge(set_up, 4)
            for c in range(KC):
                split_ctx(0, c)
            for c in range(KC):
                key_rsqrt(0, c)

            def body(j, par):
                first, last, past = kinds(j)
                if not past:
                    normalise(j, 0)
                    if not last:
                        split_ctx(j + 1, 0)
                        split_ctx(j + 1, 1)
                    normalise(j, 1)
                    if not last:
                        key_rsqrt(j + 1, 0)
                        split_ctx(j + 1, 2)
                        key_rsqrt(j + 1, 1)
                if not first:
                    pool.wait_ge(mv_set, j)
                    pool.tensor_tensor(rstd[:], mv[:, 1:2], ln_eps_s[0:S, :], ALU.add).then_inc(rstd_set, 1)
                    pool.wait_ge(rstd_set, 2 * j - 1)
                    pool.tensor_tensor(rstd[:], rstd[:], half_s[0:S, 0:1], ALU.pow).then_inc(rstd_set, 1)
                if not past:
                    normalise(j, 2)
                    if not last:
                        key_rsqrt(j + 1, 2)
                    normalise(j, 3)
            over_batches(pool, body)



def feed_forward_phase(nc, sem, x2_d, router_w, router_b, expert_w, expert_b, proj_w, proj_b, norm_w, tri, sel, ident, out):
    with ExitStack() as ctx:
        def sb(name, shape, dt=F32):
            return ctx.enter_context(nc.sbuf_tensor(name, shape, dt))

        NST = 2
        ident_s = sb("c_ident", [P, P])
        half_s = sb("c_half", [P, 1])
        rms_eps_s, ln_eps_s = sb("c_rms_eps", [P, 1]), sb("c_ln_eps", [P, 1])
        carry = sb("c_carry", [S, GB])
        rb_s, tri_s = sb("c_rb", [S, E]), sb("c_tri", [S, E, E])
        eb_s = sb("c_eb", [P, E, DC])
        pb_s, nw_s = sb("c_pb", [S, D]), sb("c_nw", [S, D])
        rw_s = sb("c_rw", [P, DC, E])
        rwh, rwl = sb("c_rwh", [P, DC, E], F32R), sb("c_rwl", [P, DC, E], F32R)
        selr = sb("c_selr", [E, E, P], F32R)
        stage = sb("c_stage", [P, NST, D])
        Eh, El = sb("c_Eh", [P, E, DC, D], F32R), sb("c_El", [P, E, DC, D], F32R)
        Ph, Pl = sb("c_Ph", [P, DC, D], F32R), sb("c_Pl", [P, DC, D], F32R)
        x2n = sb("c_x2n", [S, 2, D])
        xTh, xTl = sb("c_xTh", [P, DC, GT], F32R), sb("c_xTl", [P, DC, GT], F32R)
        logit, dlogit, elogit = sb("c_logit", [S, GB, E]), sb("c_dlogit", [S, GB, E]), sb("c_elogit", [S, GB, E])
        lmax, rank, picked = sb("c_lmax", [S, GB]), sb("c_rank", [S, GB, E]), sb("c_picked", [S, GB, E])
        wsum, winv = sb("c_wsum", [S, GB]), sb("c_winv", [S, GB])
        above, equal = sb("c_above", [S, GB, E, E]), sb("c_equal", [S, GB, E, E])
        weight = sb("c_weight", [S, GB, E])
        wTh, wTl = sb("c_wTh", [E, GT], F32R), sb("c_wTl", [E, GT], F32R)
        act_s = sb("c_act", [P, 2, GT])
        acc = sb("c_acc", [P, DC, GT])
        combh, combl = sb("c_combh", [P, 2, DC, S], F32R), sb("c_combl", [P, 2, DC, S], F32R)
        x2r, x2p, u_s = sb("c_x2r", [S, 2, D]), sb("c_x2p", [S, D]), sb("c_u", [S, 2, D])
        ss, rr = sb("c_ss", [S, 2]), sb("c_rr", [S, 2])
        stat, mv, rstd = sb("c_stat", [S, 2, 6]), sb("c_mv", [S, 2, 2]), sb("c_rstd", [S, 2])

        bank = [ctx.enter_context(nc.psum_tensor(f"c_bank{k}", [P, 512], F32)) for k in range(8)]
        h_bank, w_bank, x_bank, l_bank = bank[0:2], bank[2:4], bank[4:6], bank[6]
        p_bank = (bank[7], bank[5])

        consts, set_up, rw_hi, rw_lo = sem("c_consts"), sem("c_set_up"), sem("c_rw_hi"), sem("c_rw_lo")
        w_raw, w_hi, w_lo = [sem(f"c_w_raw{k}") for k in range(NST)], sem("c_w_hi"), sem("c_w_lo")
        x2n_in, xt_done, xt_hi, xt_lo = [sem("x2n_in0"), sem("x2n_in1")], sem("c_xt_done"), sem("c_xt_hi"), sem("c_xt_lo")
        lg_done, route, exp_rdy = sem("lg_done"), sem("route"), sem("exp_rdy")
        wt_done, wt_hi, wt_lo, wb_done = sem("wt_done"), sem("wt_hi"), sem("wt_lo"), sem("wb_done")
        h_done, act_rdy, mul_done, acc_done = sem("h_done"), sem("act_rdy"), sem("mul_done"), sem("acc_done")
        c_hi, c_lo, p_done = sem("c_hi"), sem("c_lo"), sem("p_done")
        x2r_in, x2p_set, u_rdy, sq_done = [sem("x2r_in0"), sem("x2r_in1")], sem("x2p_set"), sem("u_rdy"), sem("sq_done")
        rr_set, v_rdy, z_rdy = sem("rr_set"), sem("v_rdy"), sem("z_rdy")
        stat_set, mv_set, rstd_set = sem("c_stat_set"), sem("c_mv_set"), sem("c_rstd_set")
        o_rdy, out_in = sem("c_out_rdy"), [sem("out_in0"), sem("out_in1")]
        NR = 13

        pieces = [(expert_w[e, :, c], Eh[:, e, c], El[:, e, c]) for e in range(E) for c in range(DC)]
        pieces += [(proj_w[:, c], Ph[:, c], Pl[:, c]) for c in range(DC)]

        def over_groups(eng, body):
            body(0)
            with eng.Fori(1, G - 1) as g:
                body(g)
            body(G - 1)

        def ends(g):
            return [isinstance(g, int) and g == k for k in (0, G - 1)]

        block = ctx.enter_context(nc.Block())

        @block.sync
        def _(sp):
            def load_x2n(g, t):
                wait(sp, xt_done, 4 * g + t - 1)
                src = x2_d[bass.ds(GB * g + t, 1)].rearrange("a t d -> t (a d)")
                sp.dma_start(x2n[:, t % 2], src).then_inc(x2n_in[t % 2], 16)

            def load_x2r(g, t):
                wait(sp, z_rdy, 4 * g + t - 1)
                src = x2_d[bass.ds(GB * g + t, 1)].rearrange("a t d -> t (a d)")
                sp.dma_start(x2r[:, t % 2], src).then_inc(x2r_in[t % 2], 16)

            def store(g, t):
                sp.wait_ge(o_rdy, 4 * g + t + 1)
                dst = out[bass.ds(GB * g + t, 1)].rearrange("a t d -> t (a d)")
                sp.dma_start(dst, u_s[:, t % 2]).then_inc(out_in[t % 2], 16)

            def load_weights(n):
                if n >= NST:
                    sp.wait_ge(w_lo, n - NST + 1)
                sp.dma_start(stage[:, n % NST], pieces[n][0]).then_inc(w_raw[n % NST], 16)

            load_x2n(0, 0)
            load_x2n(0, 1)
            for a, b in ((ident_s, ident), (rw_s, router_w)):
                sp.dma_start(a[:], b).then_inc(consts, 16)
            for n in range(NST):
                load_weights(n)
            for a, b in ((rb_s[:], router_b.partition_broadcast(S)), (tri_s[:], tri), (eb_s[:], expert_b)):
                sp.dma_start(a, b).then_inc(consts, 16)
            sp.dma_start(acc[0:E, 0:2].rearrange("p a b -> p (a b)")[:, 0:E * P // 2], sel[:, 0:E * P // 2]).then_inc(consts, 16)
            sp.dma_start(acc[0:E, 2:4].rearrange("p a b -> p (a b)")[:, 0:E * P // 2], sel[:, E * P // 2:]).then_inc(consts, 16)
            sp.dma_start(pb_s[:], proj_b.partition_broadcast(S)).then_inc(consts, 16)
            sp.dma_start(nw_s[:], norm_w.partition_broadcast(S)).then_inc(consts, 16)
            load_x2n(0, 2)
            load_x2n(0, 3)

            def body(g):
                first, last = ends(g)
                if first:
                    for n in range(NST, len(pieces)):
                        load_weights(n)
                if not last:
                    load_x2n(g + 1, 0)
                    load_x2n(g + 1, 1)
                load_x2r(g, 0)
                load_x2r(g, 1)
                if not last:
                    load_x2n(g + 1, 2)
                    load_x2n(g + 1, 3)
                store(g, 0)
                load_x2r(g, 2)
                store(g, 1)
                load_x2r(g, 3)
                store(g, 2)
                store(g, 3)
            over_groups(sp, body)
            for slot in out_in:
                sp.wait_ge(slot, 16 * 2 * G)

        @block.tensor
        def _(pe):
            def transpose_x2(g, t):
                pe.wait_ge(x2n_in[t % 2], 16 * (2 * g + t // 2 + 1))
                if t >= 2:
                    pe.wait_ge(xt_lo, 4 * g + t - 1)
                for c in range(DC):
                    mm = pe.transpose(x_bank[t % 2][:, c * S:(c + 1) * S], x2n[:, t % 2, c * P:(c + 1) * P],
                                      ident_s[0:S, 0:S])
                mm.then_inc(xt_done, 1)

            def logits(g):
                pe.wait_ge(xt_lo, 4 * g + 4)
                for t in range(GB):
                    cols = slice(t * S, (t + 1) * S)
                    mm = product3(pe, l_bank[0:S, t * E:(t + 1) * E], lambda c: xTh[:, c, cols], lambda c: xTl[:, c, cols],
                                  lambda c: rwh[:, c, :], lambda c: rwl[:, c, :], range(DC))
                mm.then_inc(lg_done, 1)

            def transpose_weights(g):
                pe.wait_ge(route, NR * (g + 1))
                for t in range(GB):
                    mm = pe.transpose(l_bank[0:E, t * S:(t + 1) * S], weight[:, t, :], ident_s[0:S, 0:S])
                mm.then_inc(wt_done, 1)

            def spread_weights(g, e):
                if e == 0:
                    pe.wait_ge(wt_lo, g + 1)
                wait(pe, mul_done, 4 * (E * g + e - 1))
                pe.matmul(w_bank[e % 2][:, 0:GT], lhsT=selr[:, e, :], rhs=wTh[:], start=True, stop=False)
                pe.matmul(w_bank[e % 2][:, 0:GT], lhsT=selr[:, e, :], rhs=wTl[:], start=False,
                          stop=True).then_inc(wb_done, 1)

            def expert(g, e, m):
                k = 32 * g + DC * e + m
                wait(pe, act_rdy, k - 1)
                cols = slice(m * P, (m + 1) * P)
                product3(pe, h_bank[m % 2][:, 0:GT], lambda c: Eh[:, e, c, cols], lambda c: El[:, e, c, cols],
                         lambda c: xTh[:, c, :], lambda c: xTl[:, c, :], range(DC)).then_inc(h_done, 1)

            def project(g, t):
                pe.wait_ge(c_lo, 4 * g + t + 1)
                if t >= 2:
                    pe.wait_ge(sq_done, 4 * g + t - 1)
                product3(pe, p_bank[t % 2][0:S, :], lambda m: combh[:, t % 2, m, :], lambda m: combl[:, t % 2, m, :],
                         lambda m: Ph[:, m, :], lambda m: Pl[:, m, :], range(DC)).then_inc(p_done, 1)

            pe.wait_ge(consts, 16 * 9)
            for t in range(GB):
                transpose_x2(0, t)
            pe.wait_ge(rw_lo, 1)
            logits(0)
            pe.wait_ge(set_up, 5)
            transpose_weights(0)

            def body(g):
                first, last = ends(g)
                for e in range(E):
                    if first:
                        pe.wait_ge(w_lo, DC * (e + 1))
                    for m in range(DC):
                        expert(g, e, m)
                        if m == 0:
                            spread_weights(g, e)
                if not last:
                    for t in range(GB):
                        transpose_x2(g + 1, t)
                if first:
                    pe.wait_ge(w_lo, len(pieces))
                project(g, 0)
                if not last:
                    logits(g + 1)
                project(g, 1)
                project(g, 2)
                if not last:
                    transpose_weights(g + 1)
                project(g, 3)
            over_groups(pe, body)

        @block.scalar
        def _(act):
            def split_hi(n):
                act.wait_ge(w_raw[n % NST], 16 * (n // NST + 1))
                act.activation(pieces[n][1], stage[:, n % NST], ACT.Copy).then_inc(w_hi, 1)

            def x2_hi(g, t):
                act.wait_ge(xt_done, 4 * g + t + 1)
                act.activation(xTh[:, :, t * S:(t + 1) * S], x_bank[t % 2][:, 0:DC * S].rearrange("p (c t) -> p c t", c=DC),
                               ACT.Copy).then_inc(xt_hi, 1)

            def exponent(g):
                act.wait_ge(route, NR * g + 3)
                act.activation(elogit[:], dlogit[:], ACT.Exp).then_inc(exp_rdy, 1)

            def weights_hi(g):
                act.wait_ge(wt_done, g + 1)
                act.activation(wTh[:], l_bank[0:E, 0:GT], ACT.Copy).then_inc(wt_hi, 1)

            def combined_hi(g, t):
                act.wait_ge(acc_done, 32 * (g + 1))
                if t >= 2:
                    act.wait_ge(p_done, 4 * g + t - 1)
                act.activation(combh[:, t % 2], acc[:, :, t * S:(t + 1) * S], ACT.Copy).then_inc(c_hi, 1)

            def square(g, t):
                act.wait_ge(u_rdy, 4 * g + t + 1)
                act.activation(p_bank[t % 2][0:S, :], u_s[:, t % 2], ACT.Square,
                               accum_out=ss[:, t % 2:t % 2 + 1]).then_inc(sq_done, 1)

            act.wait_ge(consts, 16 * 9)
            act.activation(rwh[:], rw_s[:], ACT.Copy).then_inc(rw_hi, 1)
            act.activation(selr[:, 0:E // 2].rearrange("p a b -> p (a b)"),
                           acc[0:E, 0:2].rearrange("p a b -> p (a b)")[:, 0:E * P // 2], ACT.Copy).then_inc(set_up, 1)
            act.activation(selr[:, E // 2:E].rearrange("p a b -> p (a b)"),
                           acc[0:E, 2:4].rearrange("p a b -> p (a b)")[:, 0:E * P // 2], ACT.Copy).then_inc(set_up, 1)
            for t in range(GB):
                x2_hi(0, t)
            split_hi(0)
            split_hi(1)
            exponent(0)
            split_hi(2)
            split_hi(3)
            weights_hi(0)

            def body(g):
                first, last = ends(g)
                for e in range(E):
                    for m in range(DC):
                        k = 32 * g + DC * e + m
                        act.wait_ge(h_done, k + 1)
                        wait(act, acc_done, k - 1)
                        act.activation(act_s[:, m % 2], h_bank[m % 2][:, 0:GT], ACT.Silu,
                                       bias=eb_s[:, e, m:m + 1]).then_inc(act_rdy, 1)
                        if first:
                            split_hi(DC * (e + 1) + m)
                if not last:
                    for t in range(GB):
                        x2_hi(g + 1, t)
                combined_hi(g, 0)
                combined_hi(g, 1)
                if not last:
                    exponent(g + 1)
                combined_hi(g, 2)
                square(g, 0)
                combined_hi(g, 3)
                square(g, 1)
                if not last:
                    weights_hi(g + 1)
                square(g, 2)
                square(g, 3)
            over_groups(act, body)

        @block.vector
        def _(dve):
            def split_lo(n):
                dve.wait_ge(w_hi, n + 1)
                dve.tensor_tensor(pieces[n][2], stage[:, n % NST], pieces[n][1].bitcast(F32),
                                  ALU.subtract).then_inc(w_lo, 1)

            def x2_lo(g, t):
                dve.wait_ge(xt_hi, 4 * g + t + 1)
                cols = slice(t * S, (t + 1) * S)
                dve.tensor_tensor(xTl[:, :, cols], x_bank[t % 2][:, 0:DC * S].rearrange("p (c t) -> p c t", c=DC),
                                  xTh[:, :, cols].bitcast(F32), ALU.subtract).then_inc(xt_lo, 1)

            def router(g):
                step = NR * g

                def spread(a):
                    return a.unsqueeze(2).to_broadcast([S, GB, E])
                dve.wait_ge(lg_done, g + 1)
                dve.tensor_tensor(logit[:], l_bank[0:S, 0:GB * E].rearrange("t (b e) -> t b e", b=GB),
                                  rb_s[:].unsqueeze(1).to_broadcast([S, GB, E]), ALU.add).then_inc(route, 1)
                dve.wait_ge(route, step + 1)
                dve.tensor_reduce(lmax[:], logit[:], AX.X, ALU.max).then_inc(route, 1)
                dve.wait_ge(route, step + 2)
                dve.tensor_tensor(dlogit[:], logit[:], spread(lmax[:]), ALU.subtract).then_inc(route, 1)
                mine = logit[:].unsqueeze(3).to_broadcast([S, GB, E, E])
                other = logit[:].unsqueeze(2).to_broadcast([S, GB, E, E])
                dve.tensor_tensor(above[:], other, mine, ALU.is_gt).then_inc(route, 1)
                dve.tensor_tensor(equal[:], other, mine, ALU.is_equal).then_inc(route, 1)
                dve.wait_ge(route, step + 5)
                dve.tensor_tensor(equal[:], equal[:], tri_s[:].unsqueeze(1).to_broadcast([S, GB, E, E]),
                                  ALU.mult).then_inc(route, 1)
                dve.wait_ge(route, step + 6)
                dve.tensor_tensor(above[:], above[:], equal[:], ALU.add).then_inc(route, 1)
                dve.wait_ge(route, step + 7)
                dve.tensor_reduce(rank[:], above[:], AX.X, ALU.add).then_inc(route, 1)
                dve.wait_ge(route, step + 8)
                dve.tensor_scalar(picked[:], rank[:], 1.5, None, ALU.is_lt).then_inc(route, 1)
                dve.wait_ge(route, step + 9)
                dve.wait_ge(exp_rdy, g + 1)
                dve.tensor_tensor(picked[:], picked[:], elogit[:], ALU.mult).then_inc(route, 1)
                dve.wait_ge(route, step + 10)
                dve.tensor_reduce(wsum[:], picked[:], AX.X, ALU.add).then_inc(route, 1)
                dve.wait_ge(route, step + 11)
                dve.reciprocal(winv[:], wsum[:]).then_inc(route, 1)
                dve.wait_ge(route, step + 12)
                dve.tensor_tensor(weight[:], picked[:], spread(winv[:]), ALU.mult).then_inc(route, 1)

            def weights_lo(g):
                dve.wait_ge(wt_hi, g + 1)
                dve.tensor_tensor(wTl[:], l_bank[0:E, 0:GT], wTh[:].bitcast(F32), ALU.subtract).then_inc(wt_lo, 1)

            def combined_lo(g, t):
                dve.wait_ge(c_hi, 4 * g + t + 1)
                dve.tensor_tensor(combl[:, t % 2], acc[:, :, t * S:(t + 1) * S], combh[:, t % 2].bitcast(F32),
                                  ALU.subtract).then_inc(c_lo, 1)

            def residual(g, t):
                dve.wait_ge(p_done, 4 * g + t + 1)
                dve.wait_ge(x2p_set, 4 * g + t + 1)
                wait(dve, out_in[t % 2], 16 * (2 * g + t // 2))
                dve.tensor_tensor(u_s[:, t % 2], p_bank[t % 2][0:S, :], x2p[:], ALU.add).then_inc(u_rdy, 1)

            def rms_norm(g, t):
                k = 4 * g + t
                dve.wait_ge(rr_set, 2 * (k + 1))
                dve.scalar_tensor_tensor(out=u_s[:, t % 2], in0=u_s[:, t % 2], scalar=rr[:, t % 2:t % 2 + 1],
                                         in1=nw_s[:], op0=ALU.mult, op1=ALU.mult).then_inc(v_rdy, 1)
                dve.wait_ge(v_rdy, k + 1)
                dve.tensor_tensor(u_s[:, t % 2], u_s[:, t % 2], x2r[:, t % 2], ALU.add).then_inc(z_rdy, 1)
                dve.wait_ge(z_rdy, k + 1)
                dve.bn_stats(stat[:, t % 2], u_s[:, t % 2]).then_inc(stat_set, 1)
                dve.wait_ge(stat_set, k + 1)
                dve.memset(carry[:, t:t + 1], 0.0)
                dve.bn_aggr(mv[:, t % 2], stat[:, t % 2]).then_inc(mv_set, 1)

            def layer_norm(g, t):
                dve.wait_ge(rstd_set, 2 * (4 * g + t + 1))
                dve.tensor_scalar(u_s[:, t % 2], u_s[:, t % 2], mv[:, t % 2, 0:1], rstd[:, t % 2:t % 2 + 1],
                                  ALU.subtract, ALU.mult).then_inc(o_rdy, 1)

            dve.memset(half_s[:], -0.5).then_inc(set_up, 1)
            dve.memset(rms_eps_s[:], D * RMS_EPS).then_inc(set_up, 1)
            dve.memset(ln_eps_s[:], LN_EPS).then_inc(set_up, 1)
            dve.wait_ge(rw_hi, 1)
            dve.tensor_tensor(rwl[:], rw_s[:], rwh[:].bitcast(F32), ALU.subtract).then_inc(rw_lo, 1)
            dve.tensor_scalar(nw_s[:], nw_s[:], float(D) ** 0.5, None, ALU.mult).then_inc(rw_lo, 1)
            for t in range(GB):
                x2_lo(0, t)
            dve.wait_ge(set_up, 5)
            split_lo(0)
            split_lo(1)
            router(0)
            split_lo(2)
            split_lo(3)
            weights_lo(0)

            def body(g):
                first, last = ends(g)
                for e in range(E):
                    for m in range(DC):
                        k = 32 * g + DC * e + m
                        if m == 0:
                            dve.wait_ge(wb_done, E * g + e + 1)
                        a = act_s[:, m % 2]
                        dve.wait_ge(act_rdy, k + 1)
                        dve.tensor_tensor(a, a, w_bank[e % 2][:, 0:GT], ALU.mult).then_inc(mul_done, 1)
                        dve.wait_ge(mul_done, k + 1)
                        if e == 0:
                            dve.tensor_copy(acc[:, m], a).then_inc(acc_done, 1)
                        else:
                            dve.tensor_tensor(acc[:, m], acc[:, m], a, ALU.add).then_inc(acc_done, 1)
                        if first:
                            split_lo(DC * (e + 1) + m)
                if not last:
                    for t in range(GB):
                        x2_lo(g + 1, t)
                combined_lo(g, 0)
                combined_lo(g, 1)
                if not last:
                    router(g + 1)
                residual(g, 0)
                combined_lo(g, 2)
                residual(g, 1)
                combined_lo(g, 3)
                rms_norm(g, 0)
                if not last:
                    weights_lo(g + 1)
                layer_norm(g, 0)
                rms_norm(g, 1)
                residual(g, 2)
                layer_norm(g, 1)
                rms_norm(g, 2)
                residual(g, 3)
                layer_norm(g, 2)
                rms_norm(g, 3)
                layer_norm(g, 3)
            over_groups(dve, body)

        @block.gpsimd
        def _(pool):
            def reciprocal_root(dst, src, eps, count, k):
                pool.tensor_tensor(dst, src, eps, ALU.add).then_inc(count, 1)
                pool.wait_ge(count, 2 * k + 1)
                pool.tensor_tensor(dst, dst, half_s[0:S, :], ALU.pow).then_inc(count, 1)

            def biased_residual(g, t):
                pool.wait_ge(x2r_in[t % 2], 16 * (2 * g + t // 2 + 1))
                wait(pool, u_rdy, 4 * g + t)
                pool.tensor_tensor(x2p[:], x2r[:, t % 2], pb_s[:], ALU.add).then_inc(x2p_set, 1)

            def rms(g, t):
                pool.wait_ge(sq_done, 4 * g + t + 1)
                reciprocal_root(rr[:, t % 2:t % 2 + 1], ss[:, t % 2:t % 2 + 1], rms_eps_s[0:S, :], rr_set, 4 * g + t)

            def ln(g, t):
                pool.wait_ge(mv_set, 4 * g + t + 1)
                reciprocal_root(rstd[:, t % 2:t % 2 + 1], mv[:, t % 2, 1:2], ln_eps_s[0:S, :], rstd_set, 4 * g + t)

            pool.wait_ge(set_up, 5)
            pool.wait_ge(consts, 16 * 9)

            def body(g):
                biased_residual(g, 0)
                biased_residual(g, 1)
                rms(g, 0)
                ln(g, 0)
                rms(g, 1)
                biased_residual(g, 2)
                ln(g, 1)
                rms(g, 2)
                biased_residual(g, 3)
                ln(g, 2)
                rms(g, 3)
                ln(g, 3)
            over_groups(pool, body)


def build(nc, args, out):
    x1_d = nc.dram_tensor("x1_d", (B, S, D), F32, kind="Internal").ap()
    x2_d = nc.dram_tensor("x2_d", (B, S, D), F32, kind="Internal").ap()
    q_d = nc.dram_tensor("q_d", (B * XKV, P, 2, XG * S), F32, kind="Internal").ap()
    with ExitStack() as ctx:
        def sem(name):
            return ctx.enter_context(nc.semaphore(name))

        a = args
        self_attention_phase(nc, sem, a["x"], a["xT"], a["w_q"], a["w_k"], a["w_v"], a["w_o"], a["Wq"], a["bq"],
                             a["qn_w"], a["kn_w"], a["causal"], a["ident"], x1_d, q_d)
        cross_attention_phase(nc, sem, a["ctxT"], a["Wk"], a["Wv"], a["Wo"], a["bk"], a["bv"], a["mask"],
                              a["ident"], x1_d, q_d, x2_d)
        feed_forward_phase(nc, sem, x2_d, a["router_w"], a["router_b"], a["expert_w"], a["expert_b"],
                           a["proj_w"], a["proj_b"], a["norm_w"], a["tri"], a["sel"], a["ident"], out)


def layouts(inputs):
    import numpy as np

    def chunks(w):
        return w.reshape(w.shape[0] // P, P, w.shape[1]).transpose(1, 0, 2)

    a = {k: np.asarray(v) for k, v in inputs.items()}
    x, context = a["x"], a["ctx_2048"]
    padded = np.zeros((B, SEP, D), context.dtype)
    padded[:, :SE] = context
    sel = np.zeros((E, E, P), np.float32)
    sel[range(E), range(E)] = 1.0
    arrays = {
        "x": x,
        "xT": x.transpose(0, 2, 1).reshape(B, DC, P, S).transpose(0, 2, 1, 3),
        "w_q": chunks(a["L0_attn_w_q"].T),
        "w_k": chunks(a["L0_attn_w_k"].T),
        "w_v": chunks(a["L0_attn_w_v"].T),
        "w_o": chunks(a["L0_attn_w_o"].T),
        "Wq": a["L0_xattn_Wq"].reshape(DC, P, XKV, XG * XHD).transpose(2, 1, 0, 3),
        "bq": a["L0_xattn_bq"],
        "qn_w": a["L0_xattn_qn_w"].reshape(XHD, 1),
        "kn_w": a["L0_xattn_kn_w"].reshape(XHD, 1),
        "causal": np.triu(np.full((S, S), -BIG, np.float32), 1),
        "ident": np.eye(P, dtype=np.float32),
        "ctxT": padded.reshape(B, KC, KT, DC, P).transpose(0, 1, 4, 3, 2).reshape(B * KC, P, DC, KT),
        "Wk": chunks(a["L0_xattn_Wk"]),
        "Wv": chunks(a["L0_xattn_Wv"]),
        "Wo": chunks(a["L0_xattn_Wo"]),
        "bk": a["L0_xattn_bk"],
        "bv": a["L0_xattn_bv"].reshape(XKV, XHD).T,
        "mask": a["mask_1xSxS2_ff0"].reshape(S, SE),
        "router_w": chunks(a["L0_ffn_router_w"]),
        "router_b": a["L0_ffn_router_b"],
        "expert_w": a["L0_ffn_expert_w"].reshape(E, DC, P, D).transpose(0, 2, 1, 3),
        "expert_b": a["L0_ffn_expert_b"].reshape(E, DC, P).transpose(2, 0, 1),
        "proj_w": chunks(a["L0_ffn_proj_w"]),
        "proj_b": a["L0_ffn_proj_b"],
        "norm_w": a["L0_ffn_norm_w"],
        "tri": np.broadcast_to(np.tril(np.ones((E, E), np.float32), -1), (S, E, E)),
        "sel": sel.reshape(E, E * P),
    }
    return {k: np.ascontiguousarray(v) for k, v in arrays.items()}


def kernel(**inputs):
    import concourse.bacc as bacc
    from concourse.bass_utils import run_bass_kernel_spmd

    nc = bacc.Bacc("TRN2", target_bir_lowering=False, num_devices=1)
    arrays = {f"in_{k}": v for k, v in layouts(inputs).items()}
    args = {k[3:]: nc.dram_tensor(k, v.shape, F32, kind="ExternalInput").ap() for k, v in arrays.items()}
    out = nc.dram_tensor("out", (B, S, D), F32, kind="ExternalOutput").ap()
    build(nc, args, out)
    result = run_bass_kernel_spmd(nc, [arrays], core_ids=[0])
    return result.results[0]["out"]
```

```python
from contextlib import ExitStack

import concourse.bass as bass
from concourse import mybir

F32 = mybir.dt.float32
F32R = mybir.dt.float32r
ALU = mybir.AluOpType
ACT = mybir.ActivationFunctionType
AX = mybir.AxisListType

P = 128
B, S, D = 16, 100, 512
DC = D // P
BIG = 3.0e38
LN_EPS = 1e-5
RMS_EPS = 1e-6

SH, SHD = 16, 32
SR = P // SHD
XH, XKV, XHD = 16, 4, 128
XG = XH // XKV
SE = 361
KC, KT = 3, 121
SEP = KC * KT
SEQ = SE + 1
E = 8
GB = 4
GT = GB * S
G = B // GB


def wait(eng, sem, value):
    if not isinstance(value, int) or value > 0:
        eng.wait_ge(sem, value)


def product3(eng, out, lhi, llo, rhi, rlo, terms, first=True, last=True):
    mm = None
    n = 3 * len(terms)
    k = 0
    for c in terms:
        for l, r in ((lhi, rhi), (lhi, rlo), (llo, rhi)):
            mm = eng.matmul(out, lhsT=l(c), rhs=r(c), start=first and k == 0, stop=last and k == n - 1)
            k += 1
    return mm


def self_attention_phase(nc, sem, x_nat, xT, w_q, w_k, w_v, w_o, Wq, bq, qn_w, kn_w, causal, ident, x1_d, q_d):
    with ExitStack() as ctx:
        def sb(name, shape, dt=F32):
            return ctx.enter_context(nc.sbuf_tensor(name, shape, dt))

        ident_s = sb("a_ident", [P, P])
        causal_s = sb("a_causal", [S, S])
        half_s = sb("a_half", [P, XG])
        rms_eps_s = sb("a_rms_eps", [P, XG])
        ln_eps_s = sb("a_ln_eps", [P, 1])
        carry = sb("a_carry", [S, SR + 1])
        qkw_s = sb("a_qkw", [P, 4])
        bq_s = sb("a_bq", [S, XH * XHD])
        wq_s = sb("a_wq", [P, DC, D])
        wk_s = sb("a_wk", [P, DC, D])
        stage = sb("a_stage", [P, 2, DC, D])
        wvh, wvl = sb("a_wvh", [P, DC, D], F32R), sb("a_wvl", [P, DC, D], F32R)
        woh, wol = sb("a_woh", [P, DC, D], F32R), sb("a_wol", [P, DC, D], F32R)
        Wqh, Wql = sb("a_Wqh", [P, 4, DC, D], F32R), sb("a_Wql", [P, 4, DC, D], F32R)
        xTr = sb("a_xTr", [P, DC, S])
        xTh, xTl = sb("a_xTh", [P, DC, S], F32R), sb("a_xTl", [P, DC, S], F32R)
        xs = sb("a_xs", [S, D])
        qTs, kTs = sb("a_qTs", [P, DC, S]), sb("a_kTs", [P, DC, S])
        v_s = sb("a_v", [S, D])
        probs = sb("a_probs", [S, SR, DC, S])
        nmax = sb("a_nmax", [S, SH])
        psums = sb("a_psums", [S, SR, DC])
        rinv = sb("a_rinv", [S, SR, DC])
        pT = sb("a_pT", [S, SR, DC, S])
        oTh, oTl = sb("a_oTh", [P, DC, S], F32R), sb("a_oTl", [P, DC, S], F32R)
        x1_s = sb("a_x1", [S, D])
        stat = sb("a_stat", [S, 6])
        mv = sb("a_mv", [S, 2])
        rstd = sb("a_rstd", [S, 1])
        x1Th, x1Tl = sb("a_x1Th", [P, DC, S], F32R), sb("a_x1Tl", [P, DC, S], F32R)
        qn = sb("a_qn", [S, XKV, XG * XHD])
        junk = sb("a_junk", [S, XG * XHD])
        qss = sb("a_qss", [S, XH])
        qrs = sb("a_qrs", [S, XH])
        qo = sb("a_qo", [P, 2, 2, XG * S], F32R)

        bank = [ctx.enter_context(nc.psum_tensor(f"a_bank{k}", [P, 512], F32)) for k in range(8)]
        s_bank = bank[0:SR]

        consts, w_raw, w_hi, w_lo = sem("a_consts"), [sem("a_w_raw0"), sem("a_w_raw1")], sem("a_w_hi"), sem("a_w_lo")
        wqk_in, half_set, qkw_set = sem("a_wqk_in"), sem("a_half_set"), sem("a_qkw_set")
        xT_in, x_in, xT_hi, xT_lo = sem("xT_in"), sem("x_in"), sem("xT_hi"), sem("xT_lo")
        qs_done, ks_done, qs_ev, ks_ev = sem("qs_done"), sem("ks_done"), sem("qs_ev"), sem("ks_ev")
        sc_done, t_rdy, p_rdy = sem("sc_done"), sem("t_rdy"), sem("p_rdy")
        pt_done, pt_ev, v_done, v_ev = sem("pt_done"), sem("pt_ev"), sem("v_done"), sem("v_ev")
        rinv_set, pn_rdy = sem("rinv_set"), sem("pn_rdy")
        oT_done, oT_hi, oT_lo, y_done = sem("oT_done"), sem("oT_hi"), sem("oT_lo"), sem("y_done")
        ysum, stat_set, mv_set, rstd_set, x1_rdy = sem("ysum"), sem("stat_set"), sem("mv_set"), sem("rstd_set"), sem("x1_rdy")
        x1T_done, x1T_hi, x1T_lo = sem("x1T_done"), sem("x1T_hi"), sem("x1T_lo")
        qx_done, q_ev, q_ss, q_rs, q_rdy = sem("qx_done"), sem("q_ev"), sem("q_ss"), sem("q_rs"), sem("q_rdy")
        qT_done, qT_hi, qT_lo = sem("qT_done"), sem("qT_hi"), sem("qT_lo")
        x1_out, q_out = sem("x1_out"), [sem("q_out0"), sem("q_out1")]

        pieces = [(w_v, wvh[:], wvl[:]), (w_o, woh[:], wol[:])]
        pieces += [(Wq[n], Wqh[:, n], Wql[:, n]) for n in range(4)]

        def over_batches(eng, body):
            body(0)
            body(1)
            with eng.Fori(2, B - 1) as i:
                body(i)
            body(B - 1)
            body(B)

        block = ctx.enter_context(nc.Block())

        @block.sync
        def _(sp):
            sp.dma_start(xTr[:], xT[0]).then_inc(xT_in, 16)
            sp.dma_start(wq_s[:], w_q).then_inc(wqk_in, 16)
            sp.dma_start(wk_s[:], w_k).then_inc(wqk_in, 16)
            sp.dma_start(ident_s[:], ident).then_inc(consts, 16)
            sp.dma_start(causal_s[:], causal).then_inc(consts, 16)
            sp.dma_start(qkw_s[:, 0:1], qn_w).then_inc(consts, 16)
            sp.dma_start(qkw_s[:, 1:2], kn_w).then_inc(consts, 16)
            sp.dma_start(stage[:, 0], pieces[0][0]).then_inc(w_raw[0], 16)
            sp.dma_start(xs[:], x_nat[0]).then_inc(x_in, 16)
            sp.dma_start(stage[:, 1], pieces[1][0]).then_inc(w_raw[1], 16)
            sp.dma_start(bq_s[:], bq.partition_broadcast(S)).then_inc(consts, 16)
            for n in range(2, len(pieces)):
                sp.wait_ge(w_lo, n - 1)
                sp.dma_start(stage[:, n % 2], pieces[n][0]).then_inc(w_raw[n % 2], 16)
            def body(i):
                is_int = isinstance(i, int)
                back, front = not (is_int and i == 0), not (is_int and i == B)
                if front and not (is_int and i == B - 1):
                    wait(sp, xT_lo, i + 1)
                    wait(sp, ks_done, i + 1)
                    sp.dma_start(xTr[:], xT[bass.ds(i + 1, 1)].rearrange("a p c t -> p (a c) t")).then_inc(xT_in, 16)
                if back:
                    wait(sp, x1_rdy, i)
                    sp.dma_start(x1_d[bass.ds(i - 1, 1)].rearrange("a t d -> t (a d)"), x1_s[:]).then_inc(x1_out, 16)
                    if front:
                        wait(sp, ysum, i)
                        sp.dma_start(xs[:], x_nat[bass.ds(i, 1)].rearrange("a t d -> t (a d)")).then_inc(x_in, 16)
                    for n in range(4):
                        wait(sp, qT_lo, 4 * (i - 1) + n + 1)
                        dst = q_d[bass.ds(4 * (i - 1) + n, 1)].rearrange("a p h t -> p (a h) t")
                        sp.dma_start(dst, qo[:, n % 2].bitcast(F32)).then_inc(q_out[n % 2], 16)
            over_batches(sp, body)
            sp.wait_ge(x1_out, 16 * B)
            for slot in q_out:
                sp.wait_ge(slot, 16 * 2 * B)

        @block.tensor
        def _(pe):
            def project_q(i):
                wait(pe, xT_in, 16 * (i + 1))
                for m in range(DC):
                    for c in range(DC):
                        mm = pe.matmul(bank[6][:, m * S:(m + 1) * S], lhsT=wq_s[:, c, m * P:(m + 1) * P],
                                       rhs=xTr[:, c, :], start=c == 0, stop=c == DC - 1)
                mm.then_inc(qs_done, 1)

            def project_k(i):
                wait(pe, qs_ev, i + 1)
                for m in range(DC):
                    for c in range(DC):
                        mm = pe.matmul(bank[6][:, m * S:(m + 1) * S], lhsT=wk_s[:, c, m * P:(m + 1) * P],
                                       rhs=xTr[:, c, :], start=c == 0, stop=c == DC - 1)
                mm.then_inc(ks_done, 1)

            def transpose_q(i, n):
                pe.wait_ge(q_rdy, 4 * (i - 1) + n + 1)
                if n < 2:
                    pe.wait_ge(q_ev, 4 * (i - 1) + 3 + n)
                else:
                    pe.wait_ge(qT_lo, 4 * (i - 1) + n - 1)
                for h in range(XG):
                    mm = pe.transpose(bank[4 + n % 2][:, h * S:(h + 1) * S],
                                      qn[:, n, h * XHD:(h + 1) * XHD], ident_s[0:S, 0:S])
                mm.then_inc(qT_done, 1)

            pe.wait_ge(wqk_in, 32)
            pe.wait_ge(consts, 80)
            project_q(0)
            project_k(0)

            def body(i):
                is_int = isinstance(i, int)
                back, front = not (is_int and i == 0), not (is_int and i == B)
                if front:
                    pe.wait_ge(qs_ev, i + 1)
                    pe.wait_ge(ks_ev, i + 1)
                    for r in range(SR):
                        for c in range(DC):
                            mm = pe.matmul(s_bank[r][0:S, c * S:(c + 1) * S], lhsT=qTs[r * SHD:(r + 1) * SHD, c, :],
                                           rhs=kTs[r * SHD:(r + 1) * SHD, c, :], start=True, stop=True)
                        mm.then_inc(sc_done, 1)
                if front:
                    wait(pe, xT_lo, i + 1)
                    if is_int and i == 0:
                        pe.wait_ge(w_lo, 1)
                    product3(pe, bank[7][0:S, :], lambda c: xTh[:, c, :], lambda c: xTl[:, c, :],
                             lambda c: wvh[:, c, :], lambda c: wvl[:, c, :], range(1), last=False)
                if back:
                    wait(pe, x1_rdy, i)
                    for c in range(DC):
                        mm = pe.transpose(bank[6][:, c * S:(c + 1) * S], x1_s[:, c * P:(c + 1) * P], ident_s[0:S, 0:S])
                    mm.then_inc(x1T_done, 1)
                if front:
                    product3(pe, bank[7][0:S, :], lambda c: xTh[:, c, :], lambda c: xTl[:, c, :],
                             lambda c: wvh[:, c, :], lambda c: wvl[:, c, :], range(1, DC),
                             first=False).then_inc(v_done, 1)
                if back:
                    wait(pe, x1T_lo, i)
                    for n in range(4):
                        if n >= 2:
                            wait(pe, q_ev, 4 * (i - 1) + n - 1)
                        if is_int and i == 1:
                            pe.wait_ge(w_lo, 3 + n)
                        product3(pe, bank[4 + n % 2][0:S, :], lambda c: x1Th[:, c, :], lambda c: x1Tl[:, c, :],
                                 lambda c: Wqh[:, n, c, :], lambda c: Wql[:, n, c, :], range(DC)).then_inc(qx_done, 1)
                if front:
                    for r in range(SR):
                        pe.wait_ge(pn_rdy, 4 * i + r + 1)
                        for c in range(DC):
                            mm = pe.transpose(s_bank[r][0:S, c * S:(c + 1) * S], probs[:, r, c, :], ident_s[0:S, 0:S])
                        mm.then_inc(pt_done, 1)
                if back:
                    transpose_q(i, 0)
                    transpose_q(i, 1)
                if front:
                    pe.wait_ge(v_ev, i + 1)
                    for r in range(SR):
                        pe.wait_ge(pt_ev, 4 * i + r + 1)
                        for c in range(DC):
                            h = SR * c + r
                            mm = pe.matmul(bank[7][r * SHD:(r + 1) * SHD, c * S:(c + 1) * S],
                                           lhsT=v_s[:, h * SHD:(h + 1) * SHD], rhs=pT[:, r, c, :], start=True, stop=True)
                    mm.then_inc(oT_done, 1)
                    last = is_int and i == B - 1
                    if not last:
                        project_q(i + 1)
                if back:
                    transpose_q(i, 2)
                    transpose_q(i, 3)
                if front:
                    if not last:
                        project_k(i + 1)
                    pe.wait_ge(oT_lo, i + 1)
                    if back:
                        wait(pe, qT_lo, 4 * i)
                    if is_int and i == 0:
                        pe.wait_ge(w_lo, 2)
                    product3(pe, bank[5][0:S, :], lambda c: oTh[:, c, :], lambda c: oTl[:, c, :],
                             lambda c: woh[:, c, :], lambda c: wol[:, c, :], range(DC)).then_inc(y_done, 1)
            over_batches(pe, body)

        @block.scalar
        def _(act):
            def split_hi(n):
                act.wait_ge(w_raw[n % 2], 16 * (n // 2 + 1))
                act.activation(pieces[n][1], stage[:, n % 2], ACT.Copy).then_inc(w_hi, 1)

            def scaled_q(i):
                wait(act, qs_done, i + 1)
                act.activation(qTs[:].rearrange("p c t -> p (c t)"), bank[6][:, 0:DC * S], ACT.Copy,
                               scale=float(SHD) ** -0.5).then_inc(qs_ev, 1)

            def split_xT(i):
                wait(act, xT_in, 16 * (i + 1))
                act.activation(xTh[:], xTr[:], ACT.Copy).then_inc(xT_hi, 1)

            def queries_hi(i, n):
                act.wait_ge(qT_done, 4 * (i - 1) + n + 1)
                wait(act, q_out[n % 2], 16 * (2 * (i - 1) + n // 2))
                act.activation(qo[:, n % 2, 0, :], bank[4 + n % 2][:, 0:XG * S], ACT.Copy,
                               scale=qkw_s[:, 3:4]).then_inc(qT_hi, 1)

            split_xT(0)
            scaled_q(0)
            split_hi(0)
            split_hi(1)

            def body(i):
                is_int = isinstance(i, int)
                back, front = not (is_int and i == 0), not (is_int and i == B)
                if back:
                    wait(act, x1T_done, i)
                    act.activation(x1Th[:].rearrange("p c t -> p (c t)"), bank[6][:, 0:DC * S],
                                   ACT.Copy).then_inc(x1T_hi, 1)
                if front:
                    for r in range(SR):
                        act.wait_ge(t_rdy, 4 * i + r + 1)
                        for c in range(DC):
                            h = r * DC + c
                            e = act.activation(probs[:, r, c, :], probs[:, r, c, :], ACT.Exp, scale=-1.0,
                                               bias=nmax[:, h:h + 1], accum_out=psums[:, r, c:c + 1])
                        e.then_inc(p_rdy, 1)
                    act.wait_ge(v_done, i + 1)
                    act.activation(v_s[:], bank[7][0:S, :], ACT.Copy).then_inc(v_ev, 1)
                    for r in range(SR):
                        act.wait_ge(pt_done, 4 * i + r + 1)
                        act.activation(pT[:, r].rearrange("k c t -> k (c t)"), s_bank[r][0:S, 0:DC * S],
                                       ACT.Copy).then_inc(pt_ev, 1)
                if is_int and i == 0:
                    for n in range(2, 6):
                        split_hi(n)
                if back:
                    queries_hi(i, 0)
                    queries_hi(i, 1)
                if front:
                    act.wait_ge(oT_done, i + 1)
                    act.activation(oTh[:].rearrange("p c t -> p (c t)"), bank[7][:, 0:DC * S],
                                   ACT.Copy).then_inc(oT_hi, 1)
                    last = is_int and i == B - 1
                    if not last:
                        scaled_q(i + 1)
                if back:
                    queries_hi(i, 2)
                    queries_hi(i, 3)
                if front:
                    if not last:
                        split_xT(i + 1)
            over_batches(act, body)

        @block.vector
        def _(dve):
            def split_lo(n):
                dve.wait_ge(w_hi, n + 1)
                dve.tensor_tensor(pieces[n][2], stage[:, n % 2], pieces[n][1].bitcast(F32),
                                  ALU.subtract).then_inc(w_lo, 1)

            def copy_k(i):
                wait(dve, ks_done, i + 1)
                dve.tensor_copy(kTs[:].rearrange("p c t -> p (c t)"), bank[6][:, 0:DC * S]).then_inc(ks_ev, 1)

            def split_xT(i):
                wait(dve, xT_hi, i + 1)
                dve.tensor_tensor(xTl[:], xTr[:], xTh[:].bitcast(F32), ALU.subtract).then_inc(xT_lo, 1)

            dve.memset(half_s[:], -0.5).then_inc(half_set, 1)
            dve.memset(rms_eps_s[:], XHD * RMS_EPS).then_inc(half_set, 1)
            dve.memset(ln_eps_s[:], LN_EPS).then_inc(half_set, 1)
            split_xT(0)
            copy_k(0)
            dve.wait_ge(consts, 80)
            dve.tensor_tensor(qkw_s[:, 2:3], qkw_s[:, 0:1], qkw_s[:, 1:2], ALU.mult).then_inc(qkw_set, 1)
            dve.wait_ge(qkw_set, 1)
            dve.tensor_scalar(qkw_s[:, 3:4], qkw_s[:, 2:3], float(XHD) ** 0.5, None, ALU.mult).then_inc(qkw_set, 1)
            split_lo(0)
            split_lo(1)

            def masked(i, r):
                dve.wait_ge(sc_done, 4 * i + r + 1)
                dve.memset(carry[:, r:r + 1], 0.0)
                for c in range(DC):
                    h = r * DC + c
                    t = dve.tensor_tensor_reduce(out=probs[:, r, c, :], in0=s_bank[r][0:S, c * S:(c + 1) * S],
                                                 in1=causal_s[:], scale=-1.0, scalar=BIG, op0=ALU.add,
                                                 op1=ALU.min, accum_out=nmax[:, h:h + 1])
                t.then_inc(t_rdy, 1)

            def invert_sums(i, r):
                dve.wait_ge(p_rdy, 4 * i + r + 1)
                dve.reciprocal(rinv[:, r], psums[:, r]).then_inc(rinv_set, 1)

            def apply_rms(i, n):
                dve.wait_ge(q_rs, 2 * (4 * (i - 1) + n + 1))
                q4 = qn[:, n].rearrange("t (h d) -> t h d", h=XG)
                dve.tensor_tensor(q4, q4, qrs[:, XG * n:XG * (n + 1)].unsqueeze(2).to_broadcast([S, XG, XHD]),
                                  ALU.mult).then_inc(q_rdy, 1)

            def queries_lo(i, n):
                dve.wait_ge(qT_hi, 4 * (i - 1) + n + 1)
                dve.scalar_tensor_tensor(out=qo[:, n % 2, 1, :], in0=bank[4 + n % 2][:, 0:XG * S],
                                         scalar=qkw_s[:, 3:4], in1=qo[:, n % 2, 0, :].bitcast(F32),
                                         op0=ALU.mult, op1=ALU.subtract).then_inc(qT_lo, 1)

            def body(i):
                is_int = isinstance(i, int)
                back, front = not (is_int and i == 0), not (is_int and i == B)
                if front:
                    masked(i, 0)
                    masked(i, 1)
                if back:
                    wait(dve, x1T_hi, i)
                    dve.tensor_tensor(x1Tl[:].rearrange("p c t -> p (c t)"), bank[6][:, 0:DC * S],
                                      x1Th[:].bitcast(F32).rearrange("p c t -> p (c t)"),
                                      ALU.subtract).then_inc(x1T_lo, 1)
                if front:
                    masked(i, 2)
                    invert_sums(i, 0)
                    masked(i, 3)
                    for r in range(1, SR):
                        invert_sums(i, r)
                if is_int and i == 0:
                    for n in range(2, 6):
                        split_lo(n)
                if back:
                    for n in range(4):
                        dve.wait_ge(qx_done, 4 * (i - 1) + n + 1)
                        dve.tensor_tensor(qn[:, n], bank[4 + n % 2][0:S, :], bq_s[:, n * D:(n + 1) * D],
                                          ALU.add).then_inc(q_ev, 1)
                        if n:
                            dve.wait_ge(q_ss, 4 * (i - 1) + n)
                        dve.wait_ge(q_ev, 4 * (i - 1) + n + 1)
                        for h in range(XG):
                            q = qn[:, n, h * XHD:(h + 1) * XHD]
                            t = dve.tensor_tensor_reduce(out=junk[:, h * XHD:(h + 1) * XHD], in0=q, in1=q, scale=1.0,
                                                         scalar=0.0, op0=ALU.mult, op1=ALU.add,
                                                         accum_out=qss[:, XG * n + h:XG * n + h + 1])
                        t.then_inc(q_ss, 1)
                        if n:
                            apply_rms(i, n - 1)
                    apply_rms(i, 3)
                    queries_lo(i, 0)
                    queries_lo(i, 1)
                if front:
                    last = is_int and i == B - 1
                    dve.wait_ge(oT_hi, i + 1)
                    dve.tensor_tensor(oTl[:].rearrange("p c t -> p (c t)"), bank[7][:, 0:DC * S],
                                      oTh[:].bitcast(F32).rearrange("p c t -> p (c t)"),
                                      ALU.subtract).then_inc(oT_lo, 1)
                if back:
                    queries_lo(i, 2)
                    queries_lo(i, 3)
                if front:
                    if not last:
                        copy_k(i + 1)
                        split_xT(i + 1)
                    wait(dve, x1_out, 16 * i)
                    dve.wait_ge(x_in, 16 * (i + 1))
                    dve.wait_ge(y_done, i + 1)
                    dve.tensor_tensor(x1_s[:], bank[5][0:S, :], xs[:], ALU.add).then_inc(ysum, 1)
                    dve.wait_ge(ysum, i + 1)
                    dve.bn_stats(stat[:], x1_s[:]).then_inc(stat_set, 1)
                    dve.wait_ge(stat_set, i + 1)
                    dve.memset(carry[:, SR:SR + 1], 0.0)
                    dve.bn_aggr(mv[:], stat[:]).then_inc(mv_set, 1)
                    dve.wait_ge(rstd_set, 2 * (i + 1))
                    dve.tensor_scalar(x1_s[:], x1_s[:], mv[:, 0:1], rstd[:, 0:1], ALU.subtract,
                                      ALU.mult).then_inc(x1_rdy, 1)
            over_batches(dve, body)

        @block.gpsimd
        def _(pool):
            pool.wait_ge(half_set, 3)

            def body(i):
                is_int = isinstance(i, int)
                back, front = not (is_int and i == 0), not (is_int and i == B)
                if front:
                    for r in range(SR):
                        pool.wait_ge(rinv_set, 4 * i + r + 1)
                        pool.tensor_tensor(probs[:, r], probs[:, r], rinv[:, r].unsqueeze(2).to_broadcast([S, DC, S]),
                                           ALU.mult).then_inc(pn_rdy, 1)
                if back:
                    for n in range(4):
                        k = 4 * (i - 1) + n
                        rs = qrs[:, XG * n:XG * (n + 1)]
                        pool.wait_ge(q_ss, k + 1)
                        pool.tensor_tensor(rs, qss[:, XG * n:XG * (n + 1)], rms_eps_s[0:S, :], ALU.add).then_inc(q_rs, 1)
                        pool.wait_ge(q_rs, 2 * k + 1)
                        pool.tensor_tensor(rs, rs, half_s[0:S, 0:XG], ALU.pow).then_inc(q_rs, 1)
                if front:
                    pool.wait_ge(mv_set, i + 1)
                    pool.tensor_tensor(rstd[:], mv[:, 1:2], ln_eps_s[0:S, :], ALU.add).then_inc(rstd_set, 1)
                    pool.wait_ge(rstd_set, 2 * i + 1)
                    pool.tensor_tensor(rstd[:], rstd[:], half_s[0:S, 0:1], ALU.pow).then_inc(rstd_set, 1)
            over_batches(pool, body)



def cross_attention_phase(nc, sem, ctxT, Wk, Wv, Wo, bk, bv, mask, ident, x1_d, q_d, x2_d):
    with ExitStack() as ctx:
        def sb(name, shape, dt=F32):
            return ctx.enter_context(nc.sbuf_tensor(name, shape, dt))

        ident_s = sb("b_ident", [P, P])
        mask_s = sb("b_mask", [S, SE])
        bk_s = sb("b_bk", [KT, XKV * XHD])
        bv_s = sb("b_bv", [P, XKV])
        half_s = sb("b_half", [P, XG])
        rms_eps_s = sb("b_rms_eps", [P, XG])
        ln_eps_s = sb("b_ln_eps", [P, 1])
        carry = sb("b_carry", [S, XG + 1])
        pcarry = sb("b_pcarry", [P, 16])
        stage = sb("b_stage", [P, 2, 2, D])
        Wkh, Wkl = sb("b_Wkh", [P, DC, D], F32R), sb("b_Wkl", [P, DC, D], F32R)
        Wvh, Wvl = sb("b_Wvh", [P, DC, D], F32R), sb("b_Wvl", [P, DC, D], F32R)
        Woh, Wol = sb("b_Woh", [P, XH, D], F32R), sb("b_Wol", [P, XH, D], F32R)
        q_s = sb("b_q", [P, 2, 2, XG * S], F32R)
        ctxr = sb("b_ctxr", [P, 2, DC, KT])
        ctxh, ctxl = sb("b_ctxh", [P, KC, DC, KT], F32R), sb("b_ctxl", [P, KC, DC, KT], F32R)
        kn = sb("b_kn", [KT, 2, XKV * XHD])
        junk = sb("b_junk", [KT, XKV * XHD])
        kss, krs = sb("b_kss", [KT, KC, XKV]), sb("b_krs", [KT, KC, XKV])
        kTh, kTl = sb("b_kTh", [P, 2, XKV, SEP + 1], F32R), sb("b_kTl", [P, 2, XKV, SEP + 1], F32R)
        Vh, Vl = sb("b_Vh", [KT, KC, XKV * XHD], F32R), sb("b_Vl", [KT, KC, XKV * XHD], F32R)
        probs = sb("b_probs", [S, 2, XG, SEP])
        nmax, psums, rinv = sb("b_nmax", [S, 2, XG]), sb("b_psums", [S, 2, XG]), sb("b_rinv", [S, 2, XG])
        pTh, pTl = sb("b_pTh", [KT, KC, XG * S], F32R), sb("b_pTl", [KT, KC, XG * S], F32R)
        oTh, oTl = sb("b_oTh", [P, XKV, XG * S], F32R), sb("b_oTl", [P, XKV, XG * S], F32R)
        x1_s, y_s = sb("b_x1", [S, D]), sb("b_y", [S, D])
        stat, mv, rstd = sb("b_stat", [S, 6]), sb("b_mv", [S, 2]), sb("b_rstd", [S, 1])

        bank = [ctx.enter_context(nc.psum_tensor(f"b_bank{k}", [P, 512], F32)) for k in range(8)]
        s_bank, t_bank, o_bank, kv_bank, y_bank = bank[0:2], bank[2:4], bank[4], bank[5:7], bank[7]

        consts, set_up = sem("b_consts"), sem("b_set_up")
        w_raw, w_hi, w_lo = [sem("b_w_raw0"), sem("b_w_raw1")], sem("b_w_hi"), sem("b_w_lo")
        q_in, ctx_in = [sem("b_q_in0"), sem("b_q_in1")], [sem("ctx_in0"), sem("ctx_in1")]
        ctx_hi, ctx_lo = sem("ctx_hi"), sem("ctx_lo")
        s_done, t_rdy, e_rdy, ri_set, p_rdy = sem("b_s_done"), sem("b_t_rdy"), sem("b_e_rdy"), sem("b_ri_set"), sem("b_p_rdy")
        pt_done, pt_hi, pt_lo = sem("b_pt_done"), sem("b_pt_hi"), sem("b_pt_lo")
        o_done, o_hi, o_lo = sem("b_o_done"), sem("b_o_hi"), sem("b_o_lo")
        v_done, v_hi, v_lo = sem("b_v_done"), sem("b_v_hi"), sem("b_v_lo")
        k_done, k_ev, k_ss, k_rs, k_rdy = sem("k_done"), sem("k_ev"), sem("k_ss"), sem("k_rs"), sem("k_rdy")
        kt_done, kt_hi, kt_lo = sem("kt_done"), sem("kt_hi"), sem("kt_lo")
        y_done, ysum, stat_set, mv_set = sem("b_y_done"), sem("b_ysum"), sem("b_stat_set"), sem("b_mv_set")
        rstd_set, x2_rdy, x1_in, x2_out = sem("b_rstd_set"), sem("x2_rdy"), sem("x1_in"), sem("x2_out")

        pieces = []
        for w, h, l, n in ((Wk, Wkh, Wkl, DC), (Wv, Wvh, Wvl, DC), (Wo, Woh, Wol, XH)):
            pieces += [(w[:, c:c + 2], h[:, c:c + 2], l[:, c:c + 2]) for c in range(0, n, 2)]
        KV_PIECES = 4
        KEY_BANK, KEY_T_BANK = (1, 0, 0), (1, 1, 0)

        def over_batches(eng, body):
            body(0, 0)
            with eng.Fori(0, B // 2 - 1) as pair:
                body(2 * pair + 1, 1)
                body(2 * pair + 2, 0)
            body(B - 1, 1)
            body(B, 0)

        def kinds(j):
            return [isinstance(j, int) and j == k for k in (0, B - 1, B)]

        def ctx_loads(jn, c):
            return 16 * (jn + 1) if c == 1 else 16 * (2 * jn + 1 + c // 2)

        block = ctx.enter_context(nc.Block())

        @block.sync
        def _(sp):
            def load_ctx(jn, c):
                if c == 0:
                    wait(sp, ctx_lo, 3 * jn)
                if c == 2:
                    sp.wait_ge(ctx_lo, 3 * jn + 1)
                src = ctxT[bass.ds(KC * jn + c, 1)].rearrange("a p c t -> p (a c) t")
                sp.dma_start(ctxr[:, c % 2], src).then_inc(ctx_in[c % 2], 16)

            def load_q(n, slot, free):
                wait(sp, s_done, free)
                src = q_d[bass.ds(n, 1)].rearrange("a p h t -> p (a h) t")
                sp.dma_start(q_s[:, slot].bitcast(F32), src).then_inc(q_in[slot], 16)

            def load_weights(n):
                if n >= 2:
                    sp.wait_ge(w_lo, n - 1)
                sp.dma_start(stage[:, n % 2], pieces[n][0]).then_inc(w_raw[n % 2], 16)

            load_ctx(0, 0)
            load_weights(0)
            load_weights(1)
            sp.dma_start(bk_s[:], bk.partition_broadcast(KT)).then_inc(consts, 16)
            sp.dma_start(ident_s[:], ident).then_inc(consts, 16)
            load_ctx(0, 1)
            load_q(0, 0, 0)
            sp.dma_start(mask_s[:], mask).then_inc(consts, 16)
            sp.dma_start(bv_s[:], bv).then_inc(consts, 16)
            load_ctx(0, 2)
            load_weights(2)
            load_weights(3)

            def body(j, par):
                first, last, past = kinds(j)
                if not past:
                    load_q(4 * j + 1, 1, 16 * j)
                    if not last:
                        load_ctx(j + 1, 0)
                        load_ctx(j + 1, 1)
                    if first:
                        for n in range(KV_PIECES, len(pieces)):
                            load_weights(n)
                    load_q(4 * j + 2, 0, 16 * j + 4)
                    if not last:
                        load_ctx(j + 1, 2)
                    load_q(4 * j + 3, 1, 16 * j + 8)
                    wait(sp, ysum, j)
                    sp.dma_start(x1_s[:], x1_d[bass.ds(j, 1)].rearrange("a t d -> t (a d)")).then_inc(x1_in, 16)
                if not first:
                    sp.wait_ge(x2_rdy, j)
                    sp.dma_start(x2_d[bass.ds(j - 1, 1)].rearrange("a t d -> t (a d)"), y_s[:]).then_inc(x2_out, 16)
                if not past and not last:
                    load_q(4 * j + 4, 0, 16 * j + 12)
            over_batches(sp, body)
            sp.wait_ge(x2_out, 16 * B)

        @block.tensor
        def _(pe):
            def scores(j, s, h, par):
                if h == 0:
                    pe.wait_ge(q_in[s % 2], 16 * (2 * j + s // 2 + 1))
                    if s == 0:
                        pe.wait_ge(kt_lo, 3 * (j + 1))
                wait(pe, t_rdy, 16 * j + 4 * s + h - 1)
                q = [q_s[:, s % 2, k, h * S:(h + 1) * S] for k in range(2)]
                k_ = [kTh[:, par, s, 0:SEQ], kTl[:, par, s, 0:SEQ]]
                product3(pe, s_bank[h % 2][0:S, 0:SEQ], lambda c: q[0], lambda c: q[1],
                         lambda c: k_[0], lambda c: k_[1], range(1)).then_inc(s_done, 1)

            def transpose_probs(n, s, c):
                if c == 0:
                    pe.wait_ge(p_rdy, 4 * n + 4)
                    wait(pe, pt_lo, 3 * n)
                if c == 2:
                    pe.wait_ge(pt_lo, 3 * n + 1)
                for h in range(XG):
                    mm = pe.transpose(t_bank[c % 2][0:KT, h * S:(h + 1) * S],
                                      probs[:, s % 2, h, c * KT:(c + 1) * KT], ident_s[0:S, 0:S])
                mm.then_inc(pt_done, 1)

            def values_product(n, kv, j):
                if kv == 0:
                    pe.wait_ge(v_lo, 3 * (j + 1))
                pe.wait_ge(pt_lo, 3 * n + 3)
                wait(pe, o_lo, n)
                cols = slice(kv * XHD, (kv + 1) * XHD)
                product3(pe, o_bank[:, 0:XG * S], lambda c: Vh[:, c, cols], lambda c: Vl[:, c, cols],
                         lambda c: pTh[:, c, :], lambda c: pTl[:, c, :], range(KC)).then_inc(o_done, 1)

            def values(j, c):
                if c == 2:
                    pe.wait_ge(v_lo, 3 * j + 1)
                product3(pe, kv_bank[c % 2][0:KT, :], lambda i: ctxh[:, c, i, :], lambda i: ctxl[:, c, i, :],
                         lambda i: Wvh[:, i, :], lambda i: Wvl[:, i, :], range(DC)).then_inc(v_done, 1)

            def keys(jn, c):
                pe.wait_ge(ctx_lo, 3 * jn + c + 1)
                if c < 2:
                    wait(pe, v_lo, 3 * (jn - 1) + c + 2)
                else:
                    pe.wait_ge(k_ev, 3 * jn + 2)
                product3(pe, kv_bank[KEY_BANK[c]][0:KT, :], lambda i: ctxh[:, c, i, :],
                         lambda i: ctxl[:, c, i, :], lambda i: Wkh[:, i, :], lambda i: Wkl[:, i, :],
                         range(DC)).then_inc(k_done, 1)

            def transpose_keys(jn, c):
                pe.wait_ge(k_rdy, 3 * jn + c + 1)
                if c == 1:
                    pe.wait_ge(kt_lo, 3 * jn + 1)
                for kv in range(XKV):
                    mm = pe.transpose(kv_bank[KEY_T_BANK[c]][:, kv * KT:(kv + 1) * KT],
                                      kn[:, c % 2, kv * XHD:(kv + 1) * XHD], ident_s[0:KT, 0:KT])
                mm.then_inc(kt_done, 1)

            def output(j, kv):
                pe.wait_ge(o_lo, 4 * j + kv + 1)
                if kv == 0:
                    wait(pe, ysum, j)
                mm = product3(pe, y_bank[0:S, :], lambda h: oTh[:, kv, h * S:(h + 1) * S],
                              lambda h: oTl[:, kv, h * S:(h + 1) * S], lambda h: Woh[:, XG * kv + h, :],
                              lambda h: Wol[:, XG * kv + h, :], range(XG), first=kv == 0, last=kv == XKV - 1)
                if kv == XKV - 1:
                    mm.then_inc(y_done, 1)

            pe.wait_ge(consts, 64)
            pe.wait_ge(w_lo, 2)
            keys(0, 0)
            keys(0, 1)
            transpose_keys(0, 0)
            keys(0, 2)
            transpose_keys(0, 1)
            transpose_keys(0, 2)

            def body(j, par):
                first, last, past = kinds(j)
                for s in range(1 if past else 4):
                    n, before = 4 * j + s, not (first and s == 0)
                    now = not past
                    for h in range(3):
                        if now:
                            scores(j, s, h, par)
                        if before:
                            transpose_probs(n - 1, (s + 3) % 4, h)
                    if s == 0 and not first:
                        output(j - 1, 2)
                    if s == 1:
                        values(j, 2)
                    if s in (2, 3) and not last:
                        keys(j + 1, s - 1)
                    if now:
                        scores(j, s, 3, par)
                    if before:
                        values_product(n - 1, (s + 3) % 4, j)
                    if s == 0 and now:
                        if first:
                            pe.wait_ge(w_lo, KV_PIECES)
                        values(j, 0)
                        values(j, 1)
                    if s == 1 and not last:
                        keys(j + 1, 0)
                    if s in (2, 3) and not last:
                        transpose_keys(j + 1, s - 2)
                    if s == 1 and not first:
                        output(j - 1, 3)
                    if s in (2, 3):
                        if first:
                            pe.wait_ge(w_lo, KV_PIECES + 2 * (s - 1))
                        output(j, s - 2)
                    if s == 3 and not last:
                        transpose_keys(j + 1, 2)
                if past:
                    output(j - 1, 3)
                elif first:
                    pe.wait_ge(w_lo, len(pieces))
            over_batches(pe, body)

        @block.scalar
        def _(act):
            def split_hi(n):
                act.wait_ge(w_raw[n % 2], 16 * (n // 2 + 1))
                act.activation(pieces[n][1], stage[:, n % 2], ACT.Copy).then_inc(w_hi, 1)

            def keys_hi(jn, c, par):
                act.wait_ge(kt_done, 3 * jn + c + 1)
                act.activation(kTh[:, par, :, c * KT:(c + 1) * KT],
                               kv_bank[KEY_T_BANK[c]][:, 0:XKV * KT].rearrange("d (k t) -> d k t", k=XKV),
                               ACT.Copy).then_inc(kt_hi, 1)

            def values_hi(j, c):
                act.wait_ge(v_done, 3 * j + c + 1)
                act.activation(Vh[:, c, :], kv_bank[c % 2][0:KT, :], ACT.Copy).then_inc(v_hi, 1)

            def probs_hi(n, c):
                act.wait_ge(pt_done, 3 * n + c + 1)
                act.activation(pTh[:, c, :], t_bank[c % 2][0:KT, 0:XG * S], ACT.Copy).then_inc(pt_hi, 1)

            def exponent(j, s, h):
                act.wait_ge(t_rdy, 16 * j + 4 * s + h + 1)
                p = probs[:, s % 2, h, 0:SE]
                act.activation(p, p, ACT.Exp, scale=-1.0, bias=nmax[:, s % 2, h:h + 1],
                               accum_out=psums[:, s % 2, h:h + 1]).then_inc(e_rdy, 1)

            for n in range(KV_PIECES):
                split_hi(n)
            act.wait_ge(consts, 64)
            for c in range(KC):
                keys_hi(0, c, 0)

            def body(j, par):
                first, last, past = kinds(j)
                for s in range(1 if past else 4):
                    n, before, now = 4 * j + s, not (first and s == 0), not past
                    for h in range(3):
                        if before:
                            probs_hi(n - 1, h)
                        if now:
                            exponent(j, s, h)
                    if s == 1:
                        values_hi(j, 2)
                    if now:
                        exponent(j, s, 3)
                    if before:
                        kv = (s + 3) % 4
                        act.wait_ge(o_done, n)
                        act.activation(oTh[:, kv, :], o_bank[:, 0:XG * S], ACT.Identity,
                                       bias=bv_s[:, kv:kv + 1]).then_inc(o_hi, 1)
                    if s == 0 and now:
                        values_hi(j, 0)
                        values_hi(j, 1)
                    if first and s < 2:
                        for k in range(4):
                            split_hi(KV_PIECES + 4 * s + k)
                    if s in (2, 3) and not last:
                        keys_hi(j + 1, s - 2, 1 - par)
                    if s == 3 and not last:
                        keys_hi(j + 1, 2, 1 - par)
            over_batches(act, body)

        @block.vector
        def _(dve):
            def split_lo(n):
                dve.wait_ge(w_hi, n + 1)
                dve.tensor_tensor(pieces[n][2], stage[:, n % 2], pieces[n][1].bitcast(F32),
                                  ALU.subtract).then_inc(w_lo, 1)

            def key_squares(jn, c):
                if c == 2:
                    dve.wait_ge(kt_done, 3 * jn + 1)
                dve.wait_ge(k_done, 3 * jn + c + 1)
                dve.tensor_tensor(kn[:, c % 2, :], kv_bank[KEY_BANK[c]][0:KT, :], bk_s[:], ALU.add).then_inc(k_ev, 1)
                wait(dve, k_ss, 3 * jn + c)
                dve.wait_ge(k_ev, 3 * jn + c + 1)
                for kv in range(XKV):
                    k_ = kn[:, c % 2, kv * XHD:(kv + 1) * XHD]
                    t = dve.tensor_tensor_reduce(out=junk[:, kv * XHD:(kv + 1) * XHD], in0=k_, in1=k_, scale=1.0,
                                                 scalar=0.0, op0=ALU.mult, op1=ALU.add,
                                                 accum_out=kss[:, c, kv:kv + 1])
                t.then_inc(k_ss, 1)

            def key_norm(jn, c):
                dve.wait_ge(k_rs, 2 * (3 * jn + c + 1))
                k4 = kn[:, c % 2, :].rearrange("t (k d) -> t k d", k=XKV)
                dve.tensor_tensor(k4, k4, krs[:, c, :].unsqueeze(2).to_broadcast([KT, XKV, XHD]),
                                  ALU.mult).then_inc(k_rdy, 1)

            def keys_lo(jn, c, par):
                dve.wait_ge(kt_hi, 3 * jn + c + 1)
                cols = slice(c * KT, (c + 1) * KT)
                dve.tensor_tensor(kTl[:, par, :, cols],
                                  kv_bank[KEY_T_BANK[c]][:, 0:XKV * KT].rearrange("d (k t) -> d k t", k=XKV),
                                  kTh[:, par, :, cols].bitcast(F32), ALU.subtract).then_inc(kt_lo, 1)

            def values_lo(j, c):
                dve.wait_ge(v_hi, 3 * j + c + 1)
                dve.tensor_tensor(Vl[:, c, :], kv_bank[c % 2][0:KT, :], Vh[:, c, :].bitcast(F32),
                                  ALU.subtract).then_inc(v_lo, 1)

            def probs_lo(n, c):
                dve.wait_ge(pt_hi, 3 * n + c + 1)
                dve.tensor_tensor(pTl[:, c, :], t_bank[c % 2][0:KT, 0:XG * S], pTh[:, c, :].bitcast(F32),
                                  ALU.subtract).then_inc(pt_lo, 1)

            def masked(j, s, h):
                dve.wait_ge(s_done, 16 * j + 4 * s + h + 1)
                dve.memset(carry[:, h:h + 1], 0.0)
                dve.tensor_tensor_reduce(out=probs[:, s % 2, h, 0:SE], in0=s_bank[h % 2][0:S, 0:SE], in1=mask_s[:],
                                         scale=-1.0, scalar=BIG, op0=ALU.add, op1=ALU.min,
                                         accum_out=nmax[:, s % 2, h:h + 1]).then_inc(t_rdy, 1)

            def invert_sums(j, s, h):
                dve.wait_ge(e_rdy, 16 * j + 4 * s + h + 2)
                dve.reciprocal(rinv[:, s % 2, h:h + 2], psums[:, s % 2, h:h + 2]).then_inc(ri_set, 1)

            dve.memset(half_s[:], -0.5).then_inc(set_up, 1)
            dve.memset(rms_eps_s[:], XHD * RMS_EPS).then_inc(set_up, 1)
            dve.memset(ln_eps_s[:], LN_EPS).then_inc(set_up, 1)
            dve.memset(probs[:, :, :, SE:SEP], 0.0).then_inc(set_up, 1)
            for n in range(KV_PIECES):
                split_lo(n)
            dve.wait_ge(consts, 64)
            key_squares(0, 0)
            key_squares(0, 1)
            key_norm(0, 0)
            keys_lo(0, 0, 0)
            key_squares(0, 2)
            key_norm(0, 1)
            keys_lo(0, 1, 0)
            key_norm(0, 2)
            keys_lo(0, 2, 0)

            def body(j, par):
                first, last, past = kinds(j)
                for s in range(1 if past else 4):
                    n, before, now = 4 * j + s, not (first and s == 0), not past
                    for h in range(3):
                        if now:
                            masked(j, s, h)
                        if before:
                            probs_lo(n - 1, h)
                    if s == 2 and not first:
                        residual_norm(j - 1)
                    if s == 1:
                        values_lo(j, 2)
                    if s in (2, 3) and not last:
                        key_norm(j + 1, s - 2)
                        key_squares(j + 1, s - 1)
                    if now:
                        masked(j, s, 3)
                        invert_sums(j, s, 0)
                    if before:
                        kv = (s + 3) % 4
                        dve.wait_ge(o_hi, n)
                        dve.scalar_tensor_tensor(out=oTl[:, kv, :], in0=o_bank[:, 0:XG * S], scalar=bv_s[:, kv:kv + 1],
                                                 in1=oTh[:, kv, :].bitcast(F32), op0=ALU.add,
                                                 op1=ALU.subtract).then_inc(o_lo, 1)
                    if now:
                        invert_sums(j, s, 2)
                    if s == 2 and not first:
                        apply_norm(j - 1)
                    if s == 0 and now:
                        values_lo(j, 0)
                        values_lo(j, 1)
                    if s == 1 and not last:
                        key_squares(j + 1, 0)
                    if first and s < 2:
                        for k in range(4):
                            split_lo(KV_PIECES + 4 * s + k)
                    if s in (2, 3) and not last:
                        keys_lo(j + 1, s - 2, 1 - par)
                    if s == 3 and not last:
                        key_norm(j + 1, 2)
                        keys_lo(j + 1, 2, 1 - par)
                    if s == 3 and not first:
                        dve.wait_ge(x2_out, 16 * j)
                if past:
                    residual_norm(j - 1)
                    apply_norm(j - 1)

            def residual_norm(j):
                dve.wait_ge(x1_in, 16 * (j + 1))
                dve.wait_ge(y_done, j + 1)
                dve.tensor_tensor(y_s[:], y_bank[0:S, :], x1_s[:], ALU.add).then_inc(ysum, 1)
                dve.wait_ge(ysum, j + 1)
                dve.bn_stats(stat[:], y_s[:]).then_inc(stat_set, 1)
                dve.wait_ge(stat_set, j + 1)
                dve.memset(carry[:, XG:XG + 1], 0.0)
                dve.bn_aggr(mv[:], stat[:]).then_inc(mv_set, 1)

            def apply_norm(j):
                dve.wait_ge(rstd_set, 2 * (j + 1))
                dve.tensor_scalar(y_s[:], y_s[:], mv[:, 0:1], rstd[:, 0:1], ALU.subtract,
                                  ALU.mult).then_inc(x2_rdy, 1)
            over_batches(dve, body)

        @block.gpsimd
        def _(pool):
            def carry_wait(k):
                pool.tensor_tensor(pcarry[:, k:k + 1], half_s[:, 0:1], half_s[:, 0:1], ALU.add)

            def split_ctx(jn, c):
                pool.wait_ge(ctx_in[c % 2], ctx_loads(jn, c))
                wait(pool, v_done, 3 * (jn - 1) + c + 1)
                carry_wait(c)
                pool.tensor_scalar(ctxh[:, c], ctxr[:, c % 2], 1.0, 1.0, ALU.mult, ALU.mult).then_inc(ctx_hi, 1)
                pool.wait_ge(ctx_hi, 3 * jn + c + 1)
                pool.tensor_tensor(ctxl[:, c], ctxr[:, c % 2], ctxh[:, c].bitcast(F32),
                                   ALU.subtract).then_inc(ctx_lo, 1)

            def key_rsqrt(jn, c):
                k = 3 * jn + c
                pool.wait_ge(k_ss, k + 1)
                pool.tensor_tensor(krs[:, c, :], kss[:, c, :], rms_eps_s[0:KT, :], ALU.add).then_inc(k_rs, 1)
                pool.wait_ge(k_rs, 2 * k + 1)
                pool.tensor_tensor(krs[:, c, :], krs[:, c, :], half_s[0:KT, :], ALU.pow).then_inc(k_rs, 1)

            def normalise(j, s):
                n = 4 * j + s
                for h in range(XG):
                    if h % 2 == 0:
                        pool.wait_ge(ri_set, 2 * n + 1 + h // 2)
                        carry_wait(4 + 2 * s + h // 2)
                    p = probs[:, s % 2, h, 0:SE]
                    pool.tensor_scalar(p, p, rinv[:, s % 2, h:h + 1], 1.0, ALU.mult, ALU.mult).then_inc(p_rdy, 1)

            pool.wait_ge(set_up, 4)
            for c in range(KC):
                split_ctx(0, c)
            for c in range(KC):
                key_rsqrt(0, c)

            def body(j, par):
                first, last, past = kinds(j)
                if not past:
                    normalise(j, 0)
                    if not last:
                        split_ctx(j + 1, 0)
                        split_ctx(j + 1, 1)
                    normalise(j, 1)
                    if not last:
                        key_rsqrt(j + 1, 0)
                        split_ctx(j + 1, 2)
                        key_rsqrt(j + 1, 1)
                if not first:
                    pool.wait_ge(mv_set, j)
                    pool.tensor_tensor(rstd[:], mv[:, 1:2], ln_eps_s[0:S, :], ALU.add).then_inc(rstd_set, 1)
                    pool.wait_ge(rstd_set, 2 * j - 1)
                    pool.tensor_tensor(rstd[:], rstd[:], half_s[0:S, 0:1], ALU.pow).then_inc(rstd_set, 1)
                if not past:
                    normalise(j, 2)
                    if not last:
                        key_rsqrt(j + 1, 2)
                    normalise(j, 3)
            over_batches(pool, body)



def feed_forward_phase(nc, sem, x2_d, router_w, router_b, expert_w, expert_b, proj_w, proj_b, norm_w, tri, sel, ident, out):
    with ExitStack() as ctx:
        def sb(name, shape, dt=F32):
            return ctx.enter_context(nc.sbuf_tensor(name, shape, dt))

        ident_s = sb("c_ident", [P, P])
        small = sb("c_small", [P, 32])
        half_s, rms_eps_s, ln_eps_s = small[:, 0:1], small[:, 1:2], small[:, 2:3]
        ss, rr, rstd = [[small[0:S, k + t:k + t + 1] for t in range(GB)] for k in (3, 7, 11)]
        mv = [small[0:S, 15 + 2 * t:17 + 2 * t] for t in range(GB)]
        carry = small[0:S, 23:23 + GB]
        rb_s, tri_s = sb("c_rb", [S, E]), sb("c_tri", [S, E, E])
        eb_s = sb("c_eb", [P, E, DC])
        pb_s, nw_s = sb("c_pb", [S, D]), sb("c_nw", [S, D])
        rw_s = sb("c_rw", [P, DC, E])
        selr = sb("c_selr", [E, E, P], F32R)
        Eh, El = sb("c_Eh", [P, E, DC, D], F32R), sb("c_El", [P, E, DC, D], F32R)
        Ph, Pl = sb("c_Ph", [P, DC, D], F32R), sb("c_Pl", [P, DC, D], F32R)
        x2n = sb("c_x2n", [S, D])
        xTr = sb("c_xTr", [P, DC, GT])
        xTh = sb("c_xTh", [P, DC, GT], F32R)
        with nc.sbuf_tensor("c_sums", [S, GB - 1, D], F32) as sums:
            pass
        xTl = sb("c_xTl", [P, DC, GT], F32R)
        logit, dlogit, elogit = sb("c_logit", [S, GB, E]), sb("c_dlogit", [S, GB, E]), sb("c_elogit", [S, GB, E])
        lmax, rank, picked = sb("c_lmax", [S, GB]), sb("c_rank", [S, GB, E]), sb("c_picked", [S, GB, E])
        wsum, winv = sb("c_wsum", [S, GB]), sb("c_winv", [S, GB])
        above, equal = sb("c_above", [S, GB, E, E]), sb("c_equal", [S, GB, E, E])
        weight = sb("c_weight", [S, GB, E])
        wTh, wTl = sb("c_wTh", [E, GT], F32R), sb("c_wTl", [E, GT], F32R)
        act_s = sb("c_act", [P, 2, GT])
        acc = sb("c_acc", [P, DC, GT])
        with nc.sbuf_tensor("c_raw", [P, 6, D], F32) as raw:
            pass
        combh, combl = sb("c_combh", [P, DC, GT], F32R), sb("c_combl", [P, DC, GT], F32R)
        x2r = sb("c_x2r", [P, 2, D])
        u_s = sb("c_u", [S, D])
        def flat(a):
            return a.rearrange("p c t -> p (c t)")

        stage = [x2r[:, 0], x2r[:, 1]]
        stage += [raw[:, k] for k in range(6)]
        NST = len(stage)
        x2_first = [x2n[:], u_s[:], flat(act_s[:])[0:S, 0:D]]
        x2_last = [flat(xTr[:])[0:S, k * D:(k + 1) * D] for k in range(3)] + [x2n[:]]
        u_last = [u_s[:]] + [sums[:, k] for k in range(GB - 1)]

        def x2_tile(g, t):
            return x2_last[t] if isinstance(g, int) and g == G - 1 else x2r[0:S, t % 2]

        def u_tile(g, t):
            return u_last[t] if isinstance(g, int) and g == G - 1 else u_s[:]
        stat = sb("c_stat", [S, GB, 6])

        bank = [ctx.enter_context(nc.psum_tensor(f"c_bank{k}", [P, 512], F32)) for k in range(8)]
        h_bank, w_bank, x_bank, l_bank = bank[0:2], bank[2:4], bank[4], bank[6]
        p_bank = (bank[5], bank[7])

        consts, set_up = sem("c_consts"), sem("c_set_up")
        w_raw, w_hi, w_lo = [sem(f"c_w_raw{k}") for k in range(NST)], sem("c_w_hi"), sem("c_w_lo")
        rw_in, x2f_in, x2l_in = sem("rw_in"), [sem(f"x2f_in{k}") for k in range(3)], [sem(f"x2l_in{k}") for k in range(GB)]
        xt_used = sem("c_xt_used")
        x2n_in, xt_done, xt_ev, xt_hi, xt_lo = sem("x2n_in"), sem("c_xt_done"), sem("c_xt_ev"), sem("c_xt_hi"), sem("c_xt_lo")
        lg_done, route, exp_rdy = sem("lg_done"), sem("route"), sem("exp_rdy")
        wt_done, wt_hi, wt_lo, wb_done = sem("wt_done"), sem("wt_hi"), sem("wt_lo"), sem("wb_done")
        h_done, act_rdy, mul_done, acc_done = sem("h_done"), sem("act_rdy"), sem("mul_done"), sem("acc_done")
        c_hi, c_lo, p_done = sem("c_hi"), sem("c_lo"), sem("p_done")
        x2r_in, x2p_set, u_rdy, sq_done = [sem("x2r_in0"), sem("x2r_in1")], sem("x2p_set"), sem("u_rdy"), sem("sq_done")
        rr_set, v_rdy, z_rdy = sem("rr_set"), sem("v_rdy"), sem("z_rdy")
        stat_set, mv_set, rstd_set = sem("c_stat_set"), sem("c_mv_set"), sem("c_rstd_set")
        o_rdy, out_in, nw_set, sel_set = sem("c_out_rdy"), sem("out_in"), sem("nw_set"), sem("sel_set")
        NR = 13
        NE = E * DC

        pieces = [(expert_w[e, :, c], Eh[:, e, c], El[:, e, c]) for e in range(E) for c in range(DC)]
        pieces += [(proj_w[:, c], Ph[:, c], Pl[:, c]) for c in range(DC)]

        def splits_after(e, m):
            k = DC * e + m
            first = DC + k + min(e, DC)
            if e >= E - 1:
                return []
            return [first, first + 1] if m == DC - 1 and e < DC else [first]

        RESIDUAL_AT = ((2, 0), (3, 3), (5, 0), (6, 2))
        SQUARE_AT = ((2, 1), (4, 0), (5, 1), (6, 3))
        RMS_AT = ((2, 2), (4, 1), (5, 3), (7, 0))
        NORM_AT = ((3, 0), (4, 2), (6, 0), (7, 1))

        def over_groups(eng, body):
            body(0)
            with eng.Fori(1, G - 1) as g:
                body(g)
            body(G - 1)
            body(G)

        def kinds(g):
            return [not (isinstance(g, int) and g == 0), not (isinstance(g, int) and g == G),
                    not (isinstance(g, int) and g >= G - 1)]

        block = ctx.enter_context(nc.Block())

        @block.sync
        def _(sp):
            def tile(g, t):
                return x2_d[bass.ds(GB * g + t, 1)].rearrange("a t d -> t (a d)")

            def load_x2n(g, t):
                wait(sp, xt_done, 4 * g + t)
                sp.dma_start(x2n[:], tile(g, t)).then_inc(x2n_in, 16)

            def load_x2_first(t):
                if t == 3:
                    sp.wait_ge(xt_done, 1)
                sp.dma_start(x2_first[t % 3], tile(0, t)).then_inc(x2f_in[t % 3], 16)

            def load_x2r(g, t):
                sp.dma_start(x2r[0:S, t % 2], tile(g, t)).then_inc(x2r_in[t % 2], 16)

            def load_weights(n):
                if n >= NST:
                    sp.wait_ge(w_lo, n - NST + 1)
                sp.dma_start(stage[n % NST], pieces[n][0]).then_inc(w_raw[n % NST], 16)

            load_x2_first(0)
            sp.dma_start(ident_s[:], ident).then_inc(consts, 16)
            load_x2_first(1)
            load_x2_first(2)
            sp.dma_start(rw_s[:], router_w).then_inc(rw_in, 16)
            load_weights(0)
            load_weights(1)
            load_x2_first(3)
            load_weights(2)
            load_weights(3)
            half = E * P // 2
            for k in range(2):
                sp.dma_start(acc[0:E, 2 * k:2 * k + 2].rearrange("p a b -> p (a b)")[:, 0:half],
                             sel[:, k * half:(k + 1) * half]).then_inc(consts, 16)
            for a, b in ((rb_s[:], router_b.partition_broadcast(S)), (tri_s[:], tri), (eb_s[:], expert_b)):
                sp.dma_start(a, b).then_inc(consts, 16)
            for n in range(4, NST):
                load_weights(n)
            sp.dma_start(pb_s[:], proj_b.partition_broadcast(S)).then_inc(consts, 16)
            sp.dma_start(nw_s[:], norm_w.partition_broadcast(S)).then_inc(consts, 16)

            def body(g):
                back, now, front = kinds(g)
                if not back:
                    for n in range(NST, len(pieces)):
                        if n % 5 == 0 and n // 5 in range(2, 2 + GB):
                            load_x2n(1, n // 5 - 2)
                        load_weights(n)
                    sp.wait_ge(w_lo, len(pieces))
                if back and not now:
                    for t in range(GB):
                        sp.wait_ge(o_rdy, 4 * (g - 1) + t + 1)
                        sp.dma_start(out[GB * (g - 1) + t], u_last[t]).then_inc(out_in, 16)
                    return
                for t in range(GB):
                    if back and front:
                        load_x2n(g + 1, t)
                    if back and t < 2:
                        load_x2r(g - 1, t)
                for t in range(GB):
                    if back:
                        sp.wait_ge(o_rdy, 4 * (g - 1) + t + 1)
                        dst = out[bass.ds(GB * (g - 1) + t, 1)].rearrange("a t d -> t (a d)")
                        sp.dma_start(dst, u_s[:]).then_inc(out_in, 16)
                        if t < 2:
                            load_x2r(g - 1, t + 2)
                    if now and not front:
                        if t == 0:
                            sp.wait_ge(xt_lo, DC * G)
                        sp.dma_start(x2_last[t], tile(g, t)).then_inc(x2l_in[t], 16)
            over_groups(sp, body)
            sp.wait_ge(out_in, 16 * B)

        @block.tensor
        def _(pe):
            def transpose_x2(g, t):
                first = isinstance(g, int) and g == 0
                if first:
                    pe.wait_ge(x2f_in[t % 3], 16 * (t // 3 + 1))
                else:
                    pe.wait_ge(x2n_in, 16 * (4 * (g - 1) + t + 1))
                wait(pe, xt_ev, 4 * g + t)
                for c in range(DC):
                    src = x2_first[t % 3] if first else x2n[:]
                    mm = pe.transpose(x_bank[:, c * S:(c + 1) * S], src[:, c * P:(c + 1) * P], ident_s[0:S, 0:S])
                mm.then_inc(xt_done, 1)

            def logits(g):
                pe.wait_ge(xt_ev, 4 * g + 4)
                for t in range(GB):
                    for c in range(DC):
                        mm = pe.matmul(l_bank[0:S, t * E:(t + 1) * E], lhsT=xTr[:, c, t * S:(t + 1) * S],
                                       rhs=rw_s[:, c, :], start=c == 0, stop=c == DC - 1)
                mm.then_inc(lg_done, 1)

            def transpose_weights(g):
                pe.wait_ge(route, NR * (g + 1))
                for t in range(GB):
                    mm = pe.transpose(l_bank[0:E, t * S:(t + 1) * S], weight[:, t, :], ident_s[0:S, 0:S])
                mm.then_inc(wt_done, 1)

            def spread_weights(g, e):
                if e == 0:
                    pe.wait_ge(wt_lo, g + 1)
                wait(pe, mul_done, 4 * (E * g + e - 1))
                pe.matmul(w_bank[e % 2][:, 0:GT], lhsT=selr[:, e, :], rhs=wTh[:], start=True, stop=False)
                pe.matmul(w_bank[e % 2][:, 0:GT], lhsT=selr[:, e, :], rhs=wTl[:], start=False,
                          stop=True).then_inc(wb_done, 1)

            def expert(g, e, m):
                k = NE * g + DC * e + m
                wait(pe, act_rdy, k - 1)
                cols = slice(m * P, (m + 1) * P)
                for c in range(DC):
                    if e == 0 and m == 0:
                        pe.wait_ge(xt_lo, DC * g + c + 1)
                    mm = product3(pe, h_bank[m % 2][:, 0:GT], lambda c: Eh[:, e, c, cols], lambda c: El[:, e, c, cols],
                                  lambda c: xTh[:, c, :], lambda c: xTl[:, c, :], [c], first=c == 0, last=c == DC - 1)
                mm.then_inc(h_done, 1)

            def last_outputs(g):
                e = E - 1
                pe.wait_ge(act_rdy, NE * (g + 1) - DC + 1)
                pe.wait_ge(act_rdy, NE * (g + 1) - DC + 2)
                for c in range(DC):
                    for m in (2, 3):
                        cols = slice(m * P, (m + 1) * P)
                        mm = product3(pe, h_bank[m % 2][:, 0:GT], lambda c: Eh[:, e, c, cols], lambda c: El[:, e, c, cols],
                                      lambda c: xTh[:, c, :], lambda c: xTl[:, c, :], [c], first=c == 0, last=c == DC - 1)
                        if c == DC - 1:
                            mm.then_inc(h_done, 1)
                    if c < DC - 1:
                        mm.then_inc(xt_used, 1)

            def project(g, t):
                if t >= 2:
                    pe.wait_ge(sq_done, 4 * g + t - 1)
                cols = slice(t * S, (t + 1) * S)
                for m in range(DC):
                    if t == 0:
                        pe.wait_ge(c_lo, DC * g + m + 1)
                    mm = product3(pe, p_bank[t % 2][0:S, :], lambda m: combh[:, m, cols], lambda m: combl[:, m, cols],
                                  lambda m: Ph[:, m, :], lambda m: Pl[:, m, :], [m], first=m == 0, last=m == DC - 1)
                mm.then_inc(p_done, 1)

            pe.wait_ge(consts, 16)
            for t in range(GB):
                transpose_x2(0, t)
            pe.wait_ge(rw_in, 16)
            logits(0)

            def body(g):
                back, now, front = kinds(g)
                if not now:
                    for t in range(GB):
                        project(g - 1, t)
                    return
                for e in range(E):
                    if not back:
                        pe.wait_ge(w_lo, DC * (e + 1))
                    for m in range(DC):
                        if e < E - 1 or m < 2:
                            expert(g, e, m)
                        elif m == 2:
                            last_outputs(g)
                        if e == 0 and m == 1:
                            if not back:
                                pe.wait_ge(sel_set, 2)
                                transpose_weights(0)
                            spread_weights(g, 0)
                        if e and m == 0:
                            spread_weights(g, e)
                    if front:
                        if e < GB:
                            transpose_x2(g + 1, e)
                        if e == 4:
                            logits(g + 1)
                        if e == 6:
                            transpose_weights(g + 1)
                    if back and e in (1, 2, 4, 5):
                        project(g - 1, (1, 2, 4, 5).index(e))
                if not back:
                    pe.wait_ge(w_lo, len(pieces))
            over_groups(pe, body)

        @block.scalar
        def _(act):
            def split_hi(n):
                act.wait_ge(w_raw[n % NST], 16 * (n // NST + 1))
                act.activation(pieces[n][1], stage[n % NST], ACT.Copy).then_inc(w_hi, 1)

            def copy_x2(g, t):
                act.wait_ge(xt_done, 4 * g + t + 1)
                act.activation(xTr[:, :, t * S:(t + 1) * S], x_bank[:, 0:DC * S].rearrange("p (c t) -> p c t", c=DC),
                               ACT.Copy).then_inc(xt_ev, 1)

            def x2_hi(g, c):
                act.wait_ge(xt_ev, 4 * g + 4)
                if c < DC - 1:
                    wait(act, xt_used, (DC - 1) * (g - 1) + c + 1)
                else:
                    wait(act, h_done, NE * g)
                act.activation(xTh[:, c], xTr[:, c], ACT.Copy).then_inc(xt_hi, 1)

            def exponent(g):
                act.wait_ge(route, NR * g + 3)
                act.activation(elogit[:], dlogit[:], ACT.Exp).then_inc(exp_rdy, 1)

            def weights_hi(g):
                act.wait_ge(wt_done, g + 1)
                wait(act, wb_done, E * g)
                act.activation(wTh[:], l_bank[0:E, 0:GT], ACT.Copy).then_inc(wt_hi, 1)

            def silu(g, e, m):
                k = NE * g + DC * e + m
                act.wait_ge(h_done, k + 1)
                wait(act, acc_done, k - 1)
                act.activation(act_s[:, m % 2], h_bank[m % 2][:, 0:GT], ACT.Silu,
                               bias=eb_s[:, e, m:m + 1]).then_inc(act_rdy, 1)

            def combined_hi(g, m):
                act.wait_ge(acc_done, NE * (g + 1) - DC + m + 1)
                wait(act, p_done, 4 * g)
                act.activation(combh[:, m], acc[:, m], ACT.Copy).then_inc(c_hi, 1)

            def square(g, t):
                act.wait_ge(u_rdy, 4 * g + t + 1)
                act.activation(p_bank[t % 2][0:S, :], u_tile(g, t), ACT.Square, accum_out=ss[t]).then_inc(sq_done, 1)

            for t in range(GB):
                copy_x2(0, t)
            for c in range(DC):
                x2_hi(0, c)
            for n in range(DC):
                split_hi(n)
            act.wait_ge(consts, 16 * 8)
            for k in range(2):
                half = E * P // 2
                act.activation(selr[:, k * E // 2:(k + 1) * E // 2].rearrange("p a b -> p (a b)"),
                               acc[0:E, 2 * k:2 * k + 2].rearrange("p a b -> p (a b)")[:, 0:half],
                               ACT.Copy).then_inc(sel_set, 1)
            exponent(0)

            def body(g):
                back, now, front = kinds(g)
                if not now:
                    for t in range(GB):
                        square(g - 1, t)
                    return
                for e in range(E):
                    for m in range(DC):
                        if front and e == E - 1 and m == 2:
                            for c in range(DC - 1):
                                x2_hi(g + 1, c)
                        silu(g, e, m)
                        if front and e == E - 1 and m == 2:
                            x2_hi(g + 1, DC - 1)
                        if not back:
                            if (e, m) == (0, 1):
                                weights_hi(0)
                            for n in splits_after(e, m):
                                split_hi(n)
                        if front and 1 <= e <= GB and m == 0:
                            copy_x2(g + 1, e - 1)
                        if back and (e, m) in SQUARE_AT:
                            square(g - 1, SQUARE_AT.index((e, m)))
                        if front and (e, m) == (5, 3):
                            exponent(g + 1)
                if front:
                    weights_hi(g + 1)
                for m in range(DC):
                    combined_hi(g, m)
            over_groups(act, body)

        @block.vector
        def _(dve):
            def split_lo(n):
                dve.wait_ge(w_hi, n + 1)
                dve.tensor_tensor(pieces[n][2], stage[n % NST], pieces[n][1].bitcast(F32),
                                  ALU.subtract).then_inc(w_lo, 1)

            def x2_lo(g, c):
                dve.wait_ge(xt_hi, DC * g + c + 1)
                dve.tensor_tensor(xTl[:, c], xTr[:, c], xTh[:, c].bitcast(F32), ALU.subtract).then_inc(xt_lo, 1)

            def spread(a):
                return a.unsqueeze(2).to_broadcast([S, GB, E])

            def rank_logits(g):
                step = NR * g
                dve.wait_ge(lg_done, g + 1)
                dve.tensor_tensor(logit[:], l_bank[0:S, 0:GB * E].rearrange("t (b e) -> t b e", b=GB),
                                  rb_s[:].unsqueeze(1).to_broadcast([S, GB, E]), ALU.add).then_inc(route, 1)
                dve.wait_ge(route, step + 1)
                dve.tensor_reduce(lmax[:], logit[:], AX.X, ALU.max).then_inc(route, 1)
                dve.wait_ge(route, step + 2)
                dve.tensor_tensor(dlogit[:], logit[:], spread(lmax[:]), ALU.subtract).then_inc(route, 1)
                mine = logit[:].unsqueeze(3).to_broadcast([S, GB, E, E])
                other = logit[:].unsqueeze(2).to_broadcast([S, GB, E, E])
                dve.tensor_tensor(above[:], other, mine, ALU.is_gt).then_inc(route, 1)
                dve.tensor_tensor(equal[:], other, mine, ALU.is_equal).then_inc(route, 1)
                dve.wait_ge(route, step + 5)
                dve.tensor_tensor(equal[:], equal[:], tri_s[:].unsqueeze(1).to_broadcast([S, GB, E, E]),
                                  ALU.mult).then_inc(route, 1)
                dve.wait_ge(route, step + 6)
                dve.tensor_tensor(above[:], above[:], equal[:], ALU.add).then_inc(route, 1)
                dve.wait_ge(route, step + 7)
                dve.tensor_reduce(rank[:], above[:], AX.X, ALU.add).then_inc(route, 1)
                dve.wait_ge(route, step + 8)
                dve.tensor_scalar(picked[:], rank[:], 1.5, None, ALU.is_lt).then_inc(route, 1)

            def weigh(g):
                step = NR * g
                dve.wait_ge(route, step + 9)
                dve.wait_ge(exp_rdy, g + 1)
                dve.tensor_tensor(picked[:], picked[:], elogit[:], ALU.mult).then_inc(route, 1)
                dve.wait_ge(route, step + 10)
                dve.tensor_reduce(wsum[:], picked[:], AX.X, ALU.add).then_inc(route, 1)
                dve.wait_ge(route, step + 11)
                dve.reciprocal(winv[:], wsum[:]).then_inc(route, 1)
                dve.wait_ge(route, step + 12)
                dve.tensor_tensor(weight[:], picked[:], spread(winv[:]), ALU.mult).then_inc(route, 1)

            def weights_lo(g):
                dve.wait_ge(wt_hi, g + 1)
                dve.tensor_tensor(wTl[:], l_bank[0:E, 0:GT], wTh[:].bitcast(F32), ALU.subtract).then_inc(wt_lo, 1)

            def weighted_sum(g, e, m):
                k = NE * g + DC * e + m
                if m == 0:
                    dve.wait_ge(wb_done, E * g + e + 1)
                a = act_s[:, m % 2]
                dve.wait_ge(act_rdy, k + 1)
                dve.tensor_tensor(a, a, w_bank[e % 2][:, 0:GT], ALU.mult).then_inc(mul_done, 1)
                dve.wait_ge(mul_done, k + 1)
                if e == 0:
                    dve.tensor_copy(acc[:, m], a).then_inc(acc_done, 1)
                else:
                    dve.tensor_tensor(acc[:, m], acc[:, m], a, ALU.add).then_inc(acc_done, 1)

            def combined_lo(g, m):
                dve.wait_ge(c_hi, DC * g + m + 1)
                dve.tensor_tensor(combl[:, m], acc[:, m], combh[:, m].bitcast(F32), ALU.subtract).then_inc(c_lo, 1)

            def residual(g, t):
                dve.wait_ge(p_done, 4 * g + t + 1)
                dve.wait_ge(x2p_set, 4 * g + t + 1)
                u = u_tile(g, t)
                dve.tensor_tensor(u, p_bank[t % 2][0:S, :], u, ALU.add).then_inc(u_rdy, 1)

            def rms_norm(g, t):
                k, u = 4 * g + t, u_tile(g, t)
                dve.wait_ge(rr_set, 2 * (k + 1))
                dve.scalar_tensor_tensor(out=u, in0=u, scalar=rr[t], in1=nw_s[:], op0=ALU.mult,
                                         op1=ALU.mult).then_inc(v_rdy, 1)
                dve.wait_ge(v_rdy, k + 1)
                dve.tensor_tensor(u, u, x2_tile(g, t), ALU.add).then_inc(z_rdy, 1)
                dve.wait_ge(z_rdy, k + 1)
                dve.bn_stats(stat[:, t], u).then_inc(stat_set, 1)
                dve.wait_ge(stat_set, k + 1)
                dve.memset(carry[:, t:t + 1], 0.0)
                dve.bn_aggr(mv[t], stat[:, t]).then_inc(mv_set, 1)

            def layer_norm(g, t):
                u = u_tile(g, t)
                dve.wait_ge(rstd_set, 2 * (4 * g + t + 1))
                dve.tensor_scalar(u, u, mv[t][:, 0:1], rstd[t], ALU.subtract, ALU.mult).then_inc(o_rdy, 1)

            dve.memset(half_s, -0.5).then_inc(set_up, 1)
            dve.memset(rms_eps_s, D * RMS_EPS).then_inc(set_up, 1)
            dve.memset(ln_eps_s, LN_EPS).then_inc(set_up, 1)
            for c in range(DC):
                x2_lo(0, c)
            for n in range(DC):
                split_lo(n)
            dve.wait_ge(consts, 16 * 8)
            rank_logits(0)
            weigh(0)
            dve.tensor_scalar(nw_s[:], nw_s[:], float(D) ** 0.5, None, ALU.mult).then_inc(nw_set, 1)
            dve.wait_ge(sel_set, 2)
            dve.wait_ge(nw_set, 1)

            def body(g):
                back, now, front = kinds(g)
                if not now:
                    for t in range(GB + 2):
                        if t < GB:
                            residual(g - 1, t)
                        if 1 <= t <= GB:
                            rms_norm(g - 1, t - 1)
                        if t >= 2:
                            layer_norm(g - 1, t - 2)
                    return
                for e in range(E):
                    for m in range(DC):
                        if front and (e, m) == (E - 1, 2):
                            for c in range(DC):
                                x2_lo(g + 1, c)
                        if not back and (e, m) == (0, 0):
                            weights_lo(0)
                        weighted_sum(g, e, m)
                        if front and (e, m) == (E - 1, 2):
                            weights_lo(g + 1)
                        if not back:
                            for n in splits_after(e, m):
                                split_lo(n)
                        if back:
                            for at, step in ((RESIDUAL_AT, residual), (RMS_AT, rms_norm), (NORM_AT, layer_norm)):
                                if (e, m) in at:
                                    step(g - 1, at.index((e, m)))
                        if front and (e, m) == (5, 2):
                            rank_logits(g + 1)
                        if front and (e, m) == (6, 1):
                            weigh(g + 1)
                for m in range(DC):
                    combined_lo(g, m)
            over_groups(dve, body)

        @block.gpsimd
        def _(pool):
            def reciprocal_root(dst, src, eps, count, k):
                pool.tensor_tensor(dst, src, eps, ALU.add).then_inc(count, 1)
                pool.wait_ge(count, 2 * k + 1)
                pool.tensor_tensor(dst, dst, half_s[0:S, :], ALU.pow).then_inc(count, 1)

            def biased_residual(g, t):
                if isinstance(g, int) and g == G - 1:
                    pool.wait_ge(x2l_in[t], 16)
                    if t == 1:
                        pool.wait_ge(h_done, NE * G)
                else:
                    pool.wait_ge(x2r_in[t % 2], 16 * (2 * g + t // 2 + 1))
                pool.tensor_tensor(u_tile(g, t), x2_tile(g, t), pb_s[:], ALU.add).then_inc(x2p_set, 1)

            def rms(g, t):
                pool.wait_ge(sq_done, 4 * g + t + 1)
                reciprocal_root(rr[t], ss[t], rms_eps_s[0:S, :], rr_set, 4 * g + t)

            def ln(g, t):
                pool.wait_ge(mv_set, 4 * g + t + 1)
                reciprocal_root(rstd[t], mv[t][:, 1:2], ln_eps_s[0:S, :], rstd_set, 4 * g + t)

            pool.wait_ge(set_up, 3)
            pool.wait_ge(consts, 16 * 8)

            def body(g):
                back, now, front = kinds(g)
                if back and now:
                    for t in range(GB):
                        biased_residual(g - 1, t)
                        rms(g - 1, t)
                        ln(g - 1, t)
                        pool.wait_ge(out_in, 16 * (4 * (g - 1) + t + 1))
                if not now:
                    for t in range(GB):
                        biased_residual(g - 1, t)
                    for t in range(GB + 1):
                        if t < GB:
                            rms(g - 1, t)
                        if t:
                            ln(g - 1, t - 1)
            over_groups(pool, body)


def build(nc, args, out):
    x1_d = nc.dram_tensor("x1_d", (B, S, D), F32, kind="Internal").ap()
    x2_d = nc.dram_tensor("x2_d", (B, S, D), F32, kind="Internal").ap()
    q_d = nc.dram_tensor("q_d", (B * XKV, P, 2, XG * S), F32, kind="Internal").ap()
    with ExitStack() as ctx:
        def sem(name):
            return ctx.enter_context(nc.semaphore(name))

        a = args
        self_attention_phase(nc, sem, a["x"], a["xT"], a["w_q"], a["w_k"], a["w_v"], a["w_o"], a["Wq"], a["bq"],
                             a["qn_w"], a["kn_w"], a["causal"], a["ident"], x1_d, q_d)
        cross_attention_phase(nc, sem, a["ctxT"], a["Wk"], a["Wv"], a["Wo"], a["bk"], a["bv"], a["mask"],
                              a["ident"], x1_d, q_d, x2_d)
        feed_forward_phase(nc, sem, x2_d, a["router_w"], a["router_b"], a["expert_w"], a["expert_b"],
                           a["proj_w"], a["proj_b"], a["norm_w"], a["tri"], a["sel"], a["ident"], out)


def layouts(inputs):
    import numpy as np

    def chunks(w):
        return w.reshape(w.shape[0] // P, P, w.shape[1]).transpose(1, 0, 2)

    a = {k: np.asarray(v) for k, v in inputs.items()}
    x, context = a["x"], a["ctx_2048"]
    padded = np.zeros((B, SEP, D), context.dtype)
    padded[:, :SE] = context
    sel = np.zeros((E, E, P), np.float32)
    sel[range(E), range(E)] = 1.0
    arrays = {
        "x": x,
        "xT": x.transpose(0, 2, 1).reshape(B, DC, P, S).transpose(0, 2, 1, 3),
        "w_q": chunks(a["L0_attn_w_q"].T),
        "w_k": chunks(a["L0_attn_w_k"].T),
        "w_v": chunks(a["L0_attn_w_v"].T),
        "w_o": chunks(a["L0_attn_w_o"].T),
        "Wq": a["L0_xattn_Wq"].reshape(DC, P, XKV, XG * XHD).transpose(2, 1, 0, 3),
        "bq": a["L0_xattn_bq"],
        "qn_w": a["L0_xattn_qn_w"].reshape(XHD, 1),
        "kn_w": a["L0_xattn_kn_w"].reshape(XHD, 1),
        "causal": np.triu(np.full((S, S), -BIG, np.float32), 1),
        "ident": np.eye(P, dtype=np.float32),
        "ctxT": padded.reshape(B, KC, KT, DC, P).transpose(0, 1, 4, 3, 2).reshape(B * KC, P, DC, KT),
        "Wk": chunks(a["L0_xattn_Wk"]),
        "Wv": chunks(a["L0_xattn_Wv"]),
        "Wo": chunks(a["L0_xattn_Wo"]),
        "bk": a["L0_xattn_bk"],
        "bv": a["L0_xattn_bv"].reshape(XKV, XHD).T,
        "mask": a["mask_1xSxS2_ff0"].reshape(S, SE),
        "router_w": chunks(a["L0_ffn_router_w"]),
        "router_b": a["L0_ffn_router_b"],
        "expert_w": a["L0_ffn_expert_w"].reshape(E, DC, P, D).transpose(0, 2, 1, 3),
        "expert_b": a["L0_ffn_expert_b"].reshape(E, DC, P).transpose(2, 0, 1),
        "proj_w": chunks(a["L0_ffn_proj_w"]),
        "proj_b": a["L0_ffn_proj_b"],
        "norm_w": a["L0_ffn_norm_w"],
        "tri": np.broadcast_to(np.tril(np.ones((E, E), np.float32), -1), (S, E, E)),
        "sel": sel.reshape(E, E * P),
    }
    return {k: np.ascontiguousarray(v) for k, v in arrays.items()}


def kernel(**inputs):
    import concourse.bacc as bacc
    from concourse.bass_utils import run_bass_kernel_spmd

    nc = bacc.Bacc("TRN2", target_bir_lowering=False, num_devices=1)
    arrays = {f"in_{k}": v for k, v in layouts(inputs).items()}
    args = {k[3:]: nc.dram_tensor(k, v.shape, F32, kind="ExternalInput").ap() for k, v in arrays.items()}
    out = nc.dram_tensor("out", (B, S, D), F32, kind="ExternalOutput").ap()
    build(nc, args, out)
    result = run_bass_kernel_spmd(nc, [arrays], core_ids=[0])
    return result.results[0]["out"]
```

```python
from contextlib import ExitStack

import concourse.bass as bass
from concourse import mybir

F32 = mybir.dt.float32
F32R = mybir.dt.float32r
ALU = mybir.AluOpType
ACT = mybir.ActivationFunctionType
AX = mybir.AxisListType

P = 128
B, S, D = 16, 100, 512
DC = D // P
BIG = 3.0e38
LN_EPS = 1e-5
RMS_EPS = 1e-6

SH, SHD = 16, 32
SR = P // SHD
XH, XKV, XHD = 16, 4, 128
XG = XH // XKV
SE = 361
KC, KT = 3, 121
SEP = KC * KT
SEQ = SE + 1
E = 8
GB = 4
GT = GB * S
G = B // GB


def wait(eng, sem, value):
    if not isinstance(value, int) or value > 0:
        eng.wait_ge(sem, value)


def product3(eng, out, lhi, llo, rhi, rlo, terms, first=True, last=True):
    mm = None
    n = 3 * len(terms)
    k = 0
    for c in terms:
        for l, r in ((lhi, rhi), (lhi, rlo), (llo, rhi)):
            mm = eng.matmul(out, lhsT=l(c), rhs=r(c), start=first and k == 0, stop=last and k == n - 1)
            k += 1
    return mm


def self_attention_phase(nc, sem, x_nat, xT, w_q, w_k, w_v, w_o, Wq, bq, qn_w, kn_w, causal, ident, x1_d, q_d):
    with ExitStack() as ctx:
        def sb(name, shape, dt=F32):
            return ctx.enter_context(nc.sbuf_tensor(name, shape, dt))

        ident_s = sb("a_ident", [P, P])
        causal_s = sb("a_causal", [S, S])
        half_s = sb("a_half", [P, XG])
        rms_eps_s = sb("a_rms_eps", [P, XG])
        ln_eps_s = sb("a_ln_eps", [P, 1])
        carry = sb("a_carry", [S, SR + 1])
        qkw_s = sb("a_qkw", [P, 4])
        bq_s = sb("a_bq", [S, XH * XHD])
        wq_s = sb("a_wq", [P, DC, D])
        wk_s = sb("a_wk", [P, DC, D])
        stage = sb("a_stage", [P, 2, DC, D])
        wvh, wvl = sb("a_wvh", [P, DC, D], F32R), sb("a_wvl", [P, DC, D], F32R)
        woh, wol = sb("a_woh", [P, DC, D], F32R), sb("a_wol", [P, DC, D], F32R)
        Wqh, Wql = sb("a_Wqh", [P, 4, DC, D], F32R), sb("a_Wql", [P, 4, DC, D], F32R)
        pcarry = sb("a_pcarry", [P, 1])
        xTr = sb("a_xTr", [P, DC, 2 * S])
        xTh, xTl = sb("a_xTh", [P, DC, 2 * S], F32R), sb("a_xTl", [P, DC, 2 * S], F32R)
        xs = sb("a_xs", [S, D])
        qTs, kTs, kTn = [sb(f"a_{k}", [P, DC, 2 * S]) for k in ("qTs", "kTs", "kTn")]
        v_s = sb("a_v", [S, D])
        probs = sb("a_probs", [S, SR, DC, S])
        nmax = sb("a_nmax", [S, SH])
        psums = sb("a_psums", [S, SR, DC])
        rinv = sb("a_rinv", [S, SR, DC])
        pT = sb("a_pT", [S, SR, DC, S])
        oTh, oTl = sb("a_oTh", [P, DC, S], F32R), sb("a_oTl", [P, DC, S], F32R)
        x1_s = sb("a_x1", [S, D])
        stat = sb("a_stat", [S, 6])
        mv = sb("a_mv", [S, 2])
        rstd = sb("a_rstd", [S, 1])
        x1Th, x1Tl = sb("a_x1Th", [P, DC, S], F32R), sb("a_x1Tl", [P, DC, S], F32R)
        qn = sb("a_qn", [S, XKV, XG * XHD])
        junk = sb("a_junk", [S, XG * XHD])
        qss = sb("a_qss", [S, XH])
        qrs = sb("a_qrs", [S, XH])
        qo = sb("a_qo", [P, 2, 2, XG * S], F32R)

        bank = [ctx.enter_context(nc.psum_tensor(f"a_bank{k}", [P, 512], F32)) for k in range(8)]
        s_bank = bank[0:SR]

        consts, w_raw, w_hi, w_lo = sem("a_consts"), [sem("a_w_raw0"), sem("a_w_raw1")], sem("a_w_hi"), sem("a_w_lo")
        wq_in, wk_in = [[sem(f"a_{w}_in{m}") for m in range(DC)] for w in ("wq", "wk")]
        causal_in, bq_in = sem("causal_in"), sem("bq_in")
        half_set, qkw_set = sem("a_half_set"), sem("a_qkw_set")
        xT_in, x_in, xT_hi, xT_lo = sem("xT_in"), sem("x_in"), sem("xT_hi"), sem("xT_lo")
        qs_done, ks_done, qs_ev = sem("qs_done"), sem("ks_done"), sem("qs_ev")
        kn_ev, ks_ev = sem("kn_ev"), sem("ks_ev")
        sc_done, t_rdy, p_rdy = sem("sc_done"), sem("t_rdy"), sem("p_rdy")
        pt_done, pt_ev, v_done, v_ev = sem("pt_done"), sem("pt_ev"), sem("v_done"), sem("v_ev")
        rinv_set, pn_rdy = sem("rinv_set"), sem("pn_rdy")
        oT_done, oT_hi, oT_lo, y_done = sem("oT_done"), sem("oT_hi"), sem("oT_lo"), sem("y_done")
        ysum, stat_set, mv_set, rstd_set, x1_rdy = sem("ysum"), sem("stat_set"), sem("mv_set"), sem("rstd_set"), sem("x1_rdy")
        x1T_done, x1T_hi, x1T_lo = sem("x1T_done"), sem("x1T_hi"), sem("x1T_lo")
        qx_done, q_ev, q_ss, q_rs, q_rdy = sem("qx_done"), sem("q_ev"), sem("q_ss"), sem("q_rs"), sem("q_rdy")
        qT_done, qT_hi, qT_lo = sem("qT_done"), sem("qT_hi"), sem("qT_lo")
        x1_out, q_out = sem("x1_out"), [sem("q_out0"), sem("q_out1")]

        pieces = [(w_v, wvh[:], wvl[:]), (w_o, woh[:], wol[:])]
        pieces += [(Wq[n], Wqh[:, n], Wql[:, n]) for n in range(4)]

        def over_batches(eng, body):
            body(0, 0, 0)
            body(1, 1, 0)
            with eng.Fori(1, B // 2 - 1) as pair:
                body(2 * pair, 0, pair)
                body(2 * pair + 1, 1, pair)
            body(B - 2, 0, B // 2 - 1)
            body(B - 1, 1, B // 2 - 1)
            body(B, 0, B // 2)

        def has_next(pair):
            return not (isinstance(pair, int) and pair >= B // 2 - 1)

        block = ctx.enter_context(nc.Block())

        @block.sync
        def _(sp):
            sp.dma_start(xTr[:], xT[0]).then_inc(xT_in, 16)
            sp.dma_start(causal_s[:], causal).then_inc(causal_in, 16)
            for dst, src, loaded in ((wk_s, w_k, wk_in), (wq_s, w_q, wq_in)):
                for m in range(DC):
                    sp.dma_start(dst[:, :, m * P:(m + 1) * P], src[:, :, m * P:(m + 1) * P]).then_inc(loaded[m], 16)
            sp.dma_start(qkw_s[:, 0:1], qn_w).then_inc(consts, 16)
            sp.dma_start(qkw_s[:, 1:2], kn_w).then_inc(consts, 16)
            sp.dma_start(ident_s[:], ident).then_inc(consts, 16)
            sp.dma_start(stage[:, 0], pieces[0][0]).then_inc(w_raw[0], 16)
            sp.dma_start(xs[:], x_nat[0]).then_inc(x_in, 16)
            sp.dma_start(stage[:, 1], pieces[1][0]).then_inc(w_raw[1], 16)
            sp.dma_start(bq_s[:], bq.partition_broadcast(S)).then_inc(bq_in, 16)
            def body(i, par, pair):
                is_int = isinstance(i, int)
                back, front = not (is_int and i == 0), not (is_int and i == B)
                if par == 0 and has_next(pair):
                    sp.wait_ge(xT_lo, pair + 1)
                    if not back:
                        sp.wait_ge(qs_done, 2)
                    sp.dma_start(xTr[:], xT[bass.ds(pair + 1, 1)].rearrange("a p c t -> p (a c) t")).then_inc(xT_in, 16)
                if not back:
                    for n in range(2, len(pieces)):
                        sp.wait_ge(w_lo, n - 1)
                        sp.dma_start(stage[:, n % 2], pieces[n][0]).then_inc(w_raw[n % 2], 16)
                if back:
                    wait(sp, x1_rdy, i)
                    sp.dma_start(x1_d[bass.ds(i - 1, 1)].rearrange("a t d -> t (a d)"), x1_s[:]).then_inc(x1_out, 16)
                    if front:
                        wait(sp, ysum, i)
                        sp.dma_start(xs[:], x_nat[bass.ds(i, 1)].rearrange("a t d -> t (a d)")).then_inc(x_in, 16)
                    for n in range(4):
                        wait(sp, qT_lo, 4 * (i - 1) + n + 1)
                        dst = q_d[bass.ds(4 * (i - 1) + n, 1)].rearrange("a p h t -> p (a h) t")
                        sp.dma_start(dst, qo[:, n % 2].bitcast(F32)).then_inc(q_out[n % 2], 16)
            over_batches(sp, body)
            sp.wait_ge(x1_out, 16 * B)
            for slot in q_out:
                sp.wait_ge(slot, 16 * 2 * B)

        @block.tensor
        def _(pe):
            def project(pair, w, ms, loaded):
                is_q = w is wq_s
                pe.wait_ge(xT_in, 16 * (pair + 1))
                for m in ms:
                    if isinstance(pair, int) and pair == 0:
                        pe.wait_ge(loaded[m], 16)
                    for c in range(DC):
                        mm = pe.matmul(bank[m // 2 if is_q else 2 + m // 2][:, m % 2 * 2 * S:(m % 2 + 1) * 2 * S],
                                       lhsT=w[:, c, m * P:(m + 1) * P], rhs=xTr[:, c, :], start=c == 0, stop=c == DC - 1)
                    if m % 2:
                        mm.then_inc(qs_done if is_q else ks_done, 1)

            def project_next(pair, par, ms):
                if par == 0:
                    project(pair + 1, wk_s, ms, wk_in)
                else:
                    project(pair + 1, wq_s, ms, wq_in)

            def transpose_q(i, n):
                pe.wait_ge(q_rdy, 4 * (i - 1) + n + 1)
                if n < 2:
                    pe.wait_ge(q_ev, 4 * (i - 1) + 3 + n)
                else:
                    pe.wait_ge(qT_lo, 4 * (i - 1) + n - 1)
                for h in range(XG):
                    mm = pe.transpose(bank[4 + n % 2][:, h * S:(h + 1) * S],
                                      qn[:, n, h * XHD:(h + 1) * XHD], ident_s[0:S, 0:S])
                mm.then_inc(qT_done, 1)

            project(0, wk_s, range(DC), wk_in)
            project(0, wq_s, range(DC), wq_in)
            pe.wait_ge(consts, 48)

            def body(i, par, pair):
                is_int = isinstance(i, int)
                back, front = not (is_int and i == 0), not (is_int and i == B)
                if front:
                    pe.wait_ge(qs_ev, 2 * (pair + 1))
                    pe.wait_ge(ks_ev, pair + 1)
                    if par == 1 and has_next(pair):
                        pe.wait_ge(kn_ev, 2 * (pair + 2))
                    cols = slice(par * S, (par + 1) * S)
                    for r in range(SR):
                        for c in range(DC):
                            mm = pe.matmul(s_bank[r][0:S, c * S:(c + 1) * S], lhsT=qTs[r * SHD:(r + 1) * SHD, c, cols],
                                           rhs=kTs[r * SHD:(r + 1) * SHD, c, cols], start=True, stop=True)
                        mm.then_inc(sc_done, 1)
                if front:
                    pe.wait_ge(xT_lo, pair + 1)
                    if is_int and i == 0:
                        pe.wait_ge(w_lo, 1)
                    product3(pe, bank[7][0:S, :], lambda c: xTh[:, c, cols], lambda c: xTl[:, c, cols],
                             lambda c: wvh[:, c, :], lambda c: wvl[:, c, :], range(1), last=False)
                if back:
                    wait(pe, x1_rdy, i)
                    for c in range(DC):
                        mm = pe.transpose(bank[6][:, c * S:(c + 1) * S], x1_s[:, c * P:(c + 1) * P], ident_s[0:S, 0:S])
                    mm.then_inc(x1T_done, 1)
                if front:
                    product3(pe, bank[7][0:S, :], lambda c: xTh[:, c, cols], lambda c: xTl[:, c, cols],
                             lambda c: wvh[:, c, :], lambda c: wvl[:, c, :], range(1, DC),
                             first=False).then_inc(v_done, 1)
                if back:
                    wait(pe, x1T_lo, i)
                    for n in range(4):
                        if n >= 2:
                            wait(pe, q_ev, 4 * (i - 1) + n - 1)
                        if is_int and i == 1:
                            pe.wait_ge(w_lo, 3 + n)
                        product3(pe, bank[4 + n % 2][0:S, :], lambda c: x1Th[:, c, :], lambda c: x1Tl[:, c, :],
                                 lambda c: Wqh[:, n, c, :], lambda c: Wql[:, n, c, :], range(DC)).then_inc(qx_done, 1)
                if front:
                    for r in range(SR):
                        pe.wait_ge(pn_rdy, 4 * i + r + 1)
                        for c in range(DC):
                            mm = pe.transpose(s_bank[r][0:S, c * S:(c + 1) * S], probs[:, r, c, :], ident_s[0:S, 0:S])
                        mm.then_inc(pt_done, 1)
                if back:
                    transpose_q(i, 0)
                    transpose_q(i, 1)
                if front:
                    pe.wait_ge(v_ev, i + 1)
                    for r in range(SR):
                        pe.wait_ge(pt_ev, 4 * i + r + 1)
                        for c in range(DC):
                            h = SR * c + r
                            mm = pe.matmul(bank[7][r * SHD:(r + 1) * SHD, c * S:(c + 1) * S],
                                           lhsT=v_s[:, h * SHD:(h + 1) * SHD], rhs=pT[:, r, c, :], start=True, stop=True)
                    mm.then_inc(oT_done, 1)
                    if has_next(pair):
                        project_next(pair, par, range(1))
                if back:
                    transpose_q(i, 2)
                    transpose_q(i, 3)
                if front:
                    if has_next(pair):
                        project_next(pair, par, range(1, DC))
                    pe.wait_ge(oT_lo, i + 1)
                    if is_int and i == 0:
                        pe.wait_ge(w_lo, 2)
                    product3(pe, bank[6][0:S, :], lambda c: oTh[:, c, :], lambda c: oTl[:, c, :],
                             lambda c: woh[:, c, :], lambda c: wol[:, c, :], range(DC)).then_inc(y_done, 1)
            over_batches(pe, body)

        @block.scalar
        def _(act):
            def split_hi(n):
                act.wait_ge(w_raw[n % 2], 16 * (n // 2 + 1))
                act.activation(pieces[n][1], stage[:, n % 2], ACT.Copy).then_inc(w_hi, 1)

            def scaled_q(pair, half):
                act.wait_ge(qs_done, 2 * pair + half + 1)
                act.activation(qTs[:, 2 * half:2 * half + 2].rearrange("p c t -> p (c t)"), bank[half][:, 0:4 * S], ACT.Copy,
                               scale=float(SHD) ** -0.5).then_inc(qs_ev, 1)

            def split_xT(pair):
                act.wait_ge(xT_in, 16 * (pair + 1))
                act.activation(xTh[:], xTr[:], ACT.Copy).then_inc(xT_hi, 1)

            def queries_hi(i, n):
                act.wait_ge(qT_done, 4 * (i - 1) + n + 1)
                wait(act, q_out[n % 2], 16 * (2 * (i - 1) + n // 2))
                act.activation(qo[:, n % 2, 0, :], bank[4 + n % 2][:, 0:XG * S], ACT.Copy,
                               scale=qkw_s[:, 3:4]).then_inc(qT_hi, 1)

            split_xT(0)
            scaled_q(0, 0)
            scaled_q(0, 1)
            split_hi(0)
            split_hi(1)

            def body(i, par, pair):
                is_int = isinstance(i, int)
                back, front = not (is_int and i == 0), not (is_int and i == B)
                if back:
                    wait(act, x1T_done, i)
                    act.activation(x1Th[:].rearrange("p c t -> p (c t)"), bank[6][:, 0:DC * S],
                                   ACT.Copy).then_inc(x1T_hi, 1)
                if front:
                    for r in range(SR):
                        act.wait_ge(t_rdy, 4 * i + r + 1)
                        for c in range(DC):
                            h = r * DC + c
                            e = act.activation(probs[:, r, c, :], probs[:, r, c, :], ACT.Exp, scale=-1.0,
                                               bias=nmax[:, h:h + 1], accum_out=psums[:, r, c:c + 1])
                        e.then_inc(p_rdy, 1)
                    if is_int and i == 1:
                        split_hi(5)
                    act.wait_ge(v_done, i + 1)
                    act.activation(v_s[:], bank[7][0:S, :], ACT.Copy).then_inc(v_ev, 1)
                    for r in range(SR):
                        act.wait_ge(pt_done, 4 * i + r + 1)
                        act.activation(pT[:, r].rearrange("k c t -> k (c t)"), s_bank[r][0:S, 0:DC * S],
                                       ACT.Copy).then_inc(pt_ev, 1)
                if is_int and i == 0:
                    split_hi(2)
                if back:
                    queries_hi(i, 0)
                    queries_hi(i, 1)
                if front:
                    act.wait_ge(oT_done, i + 1)
                    act.activation(oTh[:].rearrange("p c t -> p (c t)"), bank[7][:, 0:DC * S],
                                   ACT.Copy).then_inc(oT_hi, 1)
                if back:
                    queries_hi(i, 2)
                    queries_hi(i, 3)
                if par == 1 and has_next(pair):
                    scaled_q(pair + 1, 0)
                    scaled_q(pair + 1, 1)
                    split_xT(pair + 1)
                if is_int and i == 0:
                    split_hi(3)
                    split_hi(4)
            over_batches(act, body)

        @block.vector
        def _(dve):
            def split_lo(n):
                dve.wait_ge(w_hi, n + 1)
                dve.tensor_tensor(pieces[n][2], stage[:, n % 2], pieces[n][1].bitcast(F32),
                                  ALU.subtract).then_inc(w_lo, 1)

            def copy_k(pair, half):
                dve.wait_ge(ks_done, 2 * pair + half + 1)
                dve.tensor_copy(kTn[:, 2 * half:2 * half + 2].rearrange("p c t -> p (c t)"),
                                bank[2 + half][:, 0:4 * S]).then_inc(kn_ev, 1)

            def split_xT(pair):
                dve.wait_ge(xT_hi, pair + 1)
                dve.tensor_tensor(xTl[:], xTr[:], xTh[:].bitcast(F32), ALU.subtract).then_inc(xT_lo, 1)

            dve.memset(half_s[:], -0.5).then_inc(half_set, 1)
            dve.memset(rms_eps_s[:], XHD * RMS_EPS).then_inc(half_set, 1)
            dve.memset(ln_eps_s[:], LN_EPS).then_inc(half_set, 1)
            split_xT(0)
            copy_k(0, 0)
            copy_k(0, 1)
            dve.wait_ge(causal_in, 16)
            dve.wait_ge(consts, 48)
            dve.tensor_tensor(qkw_s[:, 2:3], qkw_s[:, 0:1], qkw_s[:, 1:2], ALU.mult).then_inc(qkw_set, 1)
            dve.wait_ge(qkw_set, 1)
            dve.tensor_scalar(qkw_s[:, 3:4], qkw_s[:, 2:3], float(XHD) ** 0.5, None, ALU.mult).then_inc(qkw_set, 1)
            split_lo(0)
            split_lo(1)

            def masked(i, r):
                dve.wait_ge(sc_done, 4 * i + r + 1)
                dve.memset(carry[:, r:r + 1], 0.0)
                for c in range(DC):
                    h = r * DC + c
                    t = dve.tensor_tensor_reduce(out=probs[:, r, c, :], in0=s_bank[r][0:S, c * S:(c + 1) * S],
                                                 in1=causal_s[:], scale=-1.0, scalar=BIG, op0=ALU.add,
                                                 op1=ALU.min, accum_out=nmax[:, h:h + 1])
                t.then_inc(t_rdy, 1)

            def invert_sums(i, r):
                dve.wait_ge(p_rdy, 4 * i + r + 1)
                dve.reciprocal(rinv[:, r], psums[:, r]).then_inc(rinv_set, 1)

            def apply_rms(i, n):
                dve.wait_ge(q_rs, 2 * (4 * (i - 1) + n + 1))
                q4 = qn[:, n].rearrange("t (h d) -> t h d", h=XG)
                dve.tensor_tensor(q4, q4, qrs[:, XG * n:XG * (n + 1)].unsqueeze(2).to_broadcast([S, XG, XHD]),
                                  ALU.mult).then_inc(q_rdy, 1)

            def queries_lo(i, n):
                dve.wait_ge(qT_hi, 4 * (i - 1) + n + 1)
                dve.scalar_tensor_tensor(out=qo[:, n % 2, 1, :], in0=bank[4 + n % 2][:, 0:XG * S],
                                         scalar=qkw_s[:, 3:4], in1=qo[:, n % 2, 0, :].bitcast(F32),
                                         op0=ALU.mult, op1=ALU.subtract).then_inc(qT_lo, 1)

            def body(i, par, pair):
                is_int = isinstance(i, int)
                back, front = not (is_int and i == 0), not (is_int and i == B)
                if front:
                    masked(i, 0)
                    masked(i, 1)
                if back:
                    wait(dve, x1T_hi, i)
                    dve.tensor_tensor(x1Tl[:].rearrange("p c t -> p (c t)"), bank[6][:, 0:DC * S],
                                      x1Th[:].bitcast(F32).rearrange("p c t -> p (c t)"),
                                      ALU.subtract).then_inc(x1T_lo, 1)
                    if is_int and i == 1:
                        split_lo(4)
                if front:
                    masked(i, 2)
                    invert_sums(i, 0)
                    masked(i, 3)
                    for r in range(1, SR):
                        invert_sums(i, r)
                if is_int and i == 0:
                    split_lo(2)
                if is_int and i == 1:
                    dve.wait_ge(bq_in, 16)
                if back:
                    for n in range(4):
                        dve.wait_ge(qx_done, 4 * (i - 1) + n + 1)
                        dve.tensor_tensor(qn[:, n], bank[4 + n % 2][0:S, :], bq_s[:, n * D:(n + 1) * D],
                                          ALU.add).then_inc(q_ev, 1)
                        if n:
                            dve.wait_ge(q_ss, 4 * (i - 1) + n)
                        dve.wait_ge(q_ev, 4 * (i - 1) + n + 1)
                        for h in range(XG):
                            q = qn[:, n, h * XHD:(h + 1) * XHD]
                            t = dve.tensor_tensor_reduce(out=junk[:, h * XHD:(h + 1) * XHD], in0=q, in1=q, scale=1.0,
                                                         scalar=0.0, op0=ALU.mult, op1=ALU.add,
                                                         accum_out=qss[:, XG * n + h:XG * n + h + 1])
                        t.then_inc(q_ss, 1)
                        if is_int and i == 1 and n == 0:
                            split_lo(5)
                        if n:
                            apply_rms(i, n - 1)
                    apply_rms(i, 3)
                    queries_lo(i, 0)
                    queries_lo(i, 1)
                if front:
                    dve.wait_ge(oT_hi, i + 1)
                    dve.tensor_tensor(oTl[:].rearrange("p c t -> p (c t)"), bank[7][:, 0:DC * S],
                                      oTh[:].bitcast(F32).rearrange("p c t -> p (c t)"),
                                      ALU.subtract).then_inc(oT_lo, 1)
                if back:
                    queries_lo(i, 2)
                    queries_lo(i, 3)
                if front:
                    if par == 0 and has_next(pair):
                        dve.wait_ge(ks_ev, pair + 1)
                        copy_k(pair + 1, 0)
                        copy_k(pair + 1, 1)
                    if par == 1 and has_next(pair):
                        split_xT(pair + 1)
                    if is_int and i == 0:
                        split_lo(3)
                    wait(dve, x1_out, 16 * i)
                    dve.wait_ge(x_in, 16 * (i + 1))
                    dve.wait_ge(y_done, i + 1)
                    dve.tensor_tensor(x1_s[:], bank[6][0:S, :], xs[:], ALU.add).then_inc(ysum, 1)
                    dve.wait_ge(ysum, i + 1)
                    dve.bn_stats(stat[:], x1_s[:]).then_inc(stat_set, 1)
                    dve.wait_ge(stat_set, i + 1)
                    dve.memset(carry[:, SR:SR + 1], 0.0)
                    dve.bn_aggr(mv[:], stat[:]).then_inc(mv_set, 1)
                    dve.wait_ge(rstd_set, 2 * (i + 1))
                    dve.tensor_scalar(x1_s[:], x1_s[:], mv[:, 0:1], rstd[:, 0:1], ALU.subtract,
                                      ALU.mult).then_inc(x1_rdy, 1)
            over_batches(dve, body)

        @block.gpsimd
        def _(pool):
            def keys_in_place(pair):
                pool.wait_ge(kn_ev, 2 * (pair + 1))
                pool.tensor_tensor(pcarry[:], half_s[:, 0:1], half_s[:, 0:1], ALU.add)
                pool.tensor_scalar(kTs[:].rearrange("p c t -> p (c t)"), kTn[:].rearrange("p c t -> p (c t)"), 1.0, 1.0,
                                   ALU.mult, ALU.mult).then_inc(ks_ev, 1)

            pool.wait_ge(half_set, 3)
            keys_in_place(0)

            def body(i, par, pair):
                is_int = isinstance(i, int)
                back, front = not (is_int and i == 0), not (is_int and i == B)
                if front:
                    for r in range(SR):
                        pool.wait_ge(rinv_set, 4 * i + r + 1)
                        pool.tensor_tensor(probs[:, r], probs[:, r], rinv[:, r].unsqueeze(2).to_broadcast([S, DC, S]),
                                           ALU.mult).then_inc(pn_rdy, 1)
                if back:
                    for n in range(4):
                        k = 4 * (i - 1) + n
                        rs = qrs[:, XG * n:XG * (n + 1)]
                        pool.wait_ge(q_ss, k + 1)
                        pool.tensor_tensor(rs, qss[:, XG * n:XG * (n + 1)], rms_eps_s[0:S, :], ALU.add).then_inc(q_rs, 1)
                        pool.wait_ge(q_rs, 2 * k + 1)
                        pool.tensor_tensor(rs, rs, half_s[0:S, 0:XG], ALU.pow).then_inc(q_rs, 1)
                if par == 1 and has_next(pair):
                    pool.wait_ge(sc_done, 4 * i + 4)
                    keys_in_place(pair + 1)
                if front:
                    pool.wait_ge(mv_set, i + 1)
                    pool.tensor_tensor(rstd[:], mv[:, 1:2], ln_eps_s[0:S, :], ALU.add).then_inc(rstd_set, 1)
                    pool.wait_ge(rstd_set, 2 * i + 1)
                    pool.tensor_tensor(rstd[:], rstd[:], half_s[0:S, 0:1], ALU.pow).then_inc(rstd_set, 1)
            over_batches(pool, body)



def cross_attention_phase(nc, sem, ctxT, Wk, Wv, Wo, bk, bv, mask, ident, x1_d, q_d, x2_d):
    with ExitStack() as ctx:
        def sb(name, shape, dt=F32):
            return ctx.enter_context(nc.sbuf_tensor(name, shape, dt))

        ident_s = sb("b_ident", [P, P])
        mask_s = sb("b_mask", [S, SE])
        bk_s = sb("b_bk", [KT, XKV * XHD])
        bv_s = sb("b_bv", [P, XKV])
        half_s = sb("b_half", [P, XG])
        rms_eps_s = sb("b_rms_eps", [P, XG])
        ln_eps_s = sb("b_ln_eps", [P, 1])
        carry = sb("b_carry", [S, XG + 1])
        pcarry = sb("b_pcarry", [P, 16])
        stage = sb("b_stage", [P, 2, 2, D])
        Wkh, Wkl = sb("b_Wkh", [P, DC, D], F32R), sb("b_Wkl", [P, DC, D], F32R)
        Wvh, Wvl = sb("b_Wvh", [P, DC, D], F32R), sb("b_Wvl", [P, DC, D], F32R)
        Woh, Wol = sb("b_Woh", [P, XH, D], F32R), sb("b_Wol", [P, XH, D], F32R)
        q_s = sb("b_q", [P, 2, 2, XG * S], F32R)
        ctxr = sb("b_ctxr", [P, 2, DC, KT])
        ctxh, ctxl = sb("b_ctxh", [P, KC, DC, KT], F32R), sb("b_ctxl", [P, KC, DC, KT], F32R)
        kn = sb("b_kn", [KT, 2, XKV * XHD])
        junk = sb("b_junk", [KT, XKV * XHD])
        kss, krs = sb("b_kss", [KT, KC, XKV]), sb("b_krs", [KT, KC, XKV])
        kTh, kTl = sb("b_kTh", [P, 2, XKV, SEP + 1], F32R), sb("b_kTl", [P, 2, XKV, SEP + 1], F32R)
        Vh, Vl = sb("b_Vh", [KT, KC, XKV * XHD], F32R), sb("b_Vl", [KT, KC, XKV * XHD], F32R)
        probs = sb("b_probs", [S, 2, XG, SEP])
        nmax, psums, rinv = sb("b_nmax", [S, 2, XG]), sb("b_psums", [S, 2, XG]), sb("b_rinv", [S, 2, XG])
        pTh, pTl = sb("b_pTh", [KT, KC, XG * S], F32R), sb("b_pTl", [KT, KC, XG * S], F32R)
        oTh, oTl = sb("b_oTh", [P, XKV, XG * S], F32R), sb("b_oTl", [P, XKV, XG * S], F32R)
        x1_s, y_s = sb("b_x1", [S, D]), sb("b_y", [S, D])
        stat, mv, rstd = sb("b_stat", [S, 6]), sb("b_mv", [S, 2]), sb("b_rstd", [S, 1])

        bank = [ctx.enter_context(nc.psum_tensor(f"b_bank{k}", [P, 512], F32)) for k in range(8)]
        s_bank, t_bank, o_bank, kv_bank, y_bank = bank[0:2], bank[2:4], bank[4], bank[5:7], bank[7]

        consts, set_up = sem("b_consts"), sem("b_set_up")
        w_raw, w_hi, w_lo = [sem("b_w_raw0"), sem("b_w_raw1")], sem("b_w_hi"), sem("b_w_lo")
        q_in, ctx_in = [sem("b_q_in0"), sem("b_q_in1")], [sem("ctx_in0"), sem("ctx_in1")]
        ctx_hi, ctx_lo = sem("ctx_hi"), sem("ctx_lo")
        s_done, t_rdy, e_rdy, ri_set, p_rdy = sem("b_s_done"), sem("b_t_rdy"), sem("b_e_rdy"), sem("b_ri_set"), sem("b_p_rdy")
        pt_done, pt_hi, pt_lo = sem("b_pt_done"), sem("b_pt_hi"), sem("b_pt_lo")
        o_done, o_hi, o_lo = sem("b_o_done"), sem("b_o_hi"), sem("b_o_lo")
        v_done, v_hi, v_lo = sem("b_v_done"), sem("b_v_hi"), sem("b_v_lo")
        k_done, k_ev, k_ss, k_rs, k_rdy = sem("k_done"), sem("k_ev"), sem("k_ss"), sem("k_rs"), sem("k_rdy")
        kt_done, kt_hi, kt_lo = sem("kt_done"), sem("kt_hi"), sem("kt_lo")
        y_done, ysum, stat_set, mv_set = sem("b_y_done"), sem("b_ysum"), sem("b_stat_set"), sem("b_mv_set")
        rstd_set, x2_rdy, x1_in, x2_out = sem("b_rstd_set"), sem("x2_rdy"), sem("x1_in"), sem("x2_out")

        pieces = []
        for w, h, l, n in ((Wk, Wkh, Wkl, DC), (Wv, Wvh, Wvl, DC), (Wo, Woh, Wol, XH)):
            pieces += [(w[:, c:c + 2], h[:, c:c + 2], l[:, c:c + 2]) for c in range(0, n, 2)]
        KV_PIECES = 4
        KEY_BANK, KEY_T_BANK = (1, 0, 0), (1, 1, 0)

        def over_batches(eng, body):
            body(0, 0)
            with eng.Fori(0, B // 2 - 1) as pair:
                body(2 * pair + 1, 1)
                body(2 * pair + 2, 0)
            body(B - 1, 1)
            body(B, 0)

        def kinds(j):
            return [isinstance(j, int) and j == k for k in (0, B - 1, B)]

        def key_bank(jn, c):
            return y_bank if isinstance(jn, int) and jn == 0 and c == 2 else kv_bank[KEY_BANK[c]]

        def value_bank(j, c):
            return (t_bank[0], t_bank[1], o_bank)[c] if isinstance(j, int) and j == 0 else kv_bank[c % 2]

        def ctx_loads(jn, c):
            return 16 * (jn + 1) if c == 1 else 16 * (2 * jn + 1 + c // 2)

        block = ctx.enter_context(nc.Block())

        @block.sync
        def _(sp):
            def load_ctx(jn, c):
                if c == 0:
                    wait(sp, ctx_lo, 3 * jn)
                if c == 2:
                    sp.wait_ge(ctx_lo, 3 * jn + 1)
                src = ctxT[bass.ds(KC * jn + c, 1)].rearrange("a p c t -> p (a c) t")
                sp.dma_start(ctxr[:, c % 2], src).then_inc(ctx_in[c % 2], 16)

            def load_q(n, slot, free):
                wait(sp, s_done, free)
                src = q_d[bass.ds(n, 1)].rearrange("a p h t -> p (a h) t")
                sp.dma_start(q_s[:, slot].bitcast(F32), src).then_inc(q_in[slot], 16)

            def load_weights(n):
                if n >= 2:
                    sp.wait_ge(w_lo, n - 1)
                sp.dma_start(stage[:, n % 2], pieces[n][0]).then_inc(w_raw[n % 2], 16)

            load_ctx(0, 0)
            load_weights(0)
            load_weights(1)
            sp.dma_start(bk_s[:], bk.partition_broadcast(KT)).then_inc(consts, 16)
            sp.dma_start(ident_s[:], ident).then_inc(consts, 16)
            load_ctx(0, 1)
            load_q(0, 0, 0)
            sp.dma_start(mask_s[:], mask).then_inc(consts, 16)
            sp.dma_start(bv_s[:], bv).then_inc(consts, 16)
            load_ctx(0, 2)
            load_weights(2)
            load_weights(3)

            def body(j, par):
                first, last, past = kinds(j)
                if not past:
                    load_q(4 * j + 1, 1, 16 * j)
                    if first:
                        load_weights(KV_PIECES)
                        load_weights(KV_PIECES + 1)
                    if not last:
                        load_ctx(j + 1, 0)
                        load_ctx(j + 1, 1)
                    load_q(4 * j + 2, 0, 16 * j + 4)
                    if first:
                        load_weights(KV_PIECES + 2)
                        load_weights(KV_PIECES + 3)
                    if not last:
                        load_ctx(j + 1, 2)
                    load_q(4 * j + 3, 1, 16 * j + 8)
                    if first:
                        load_weights(KV_PIECES + 4)
                        load_weights(KV_PIECES + 5)
                    wait(sp, ysum, j)
                    sp.dma_start(x1_s[:], x1_d[bass.ds(j, 1)].rearrange("a t d -> t (a d)")).then_inc(x1_in, 16)
                if not past and not last:
                    load_q(4 * j + 4, 0, 16 * j + 12)
                if not first:
                    sp.wait_ge(x2_rdy, j)
                    sp.dma_start(x2_d[bass.ds(j - 1, 1)].rearrange("a t d -> t (a d)"), y_s[:]).then_inc(x2_out, 16)
                if first:
                    load_weights(KV_PIECES + 6)
                    load_weights(KV_PIECES + 7)
            over_batches(sp, body)
            sp.wait_ge(x2_out, 16 * B)

        @block.tensor
        def _(pe):
            def scores(j, s, h, par):
                if h == 0:
                    pe.wait_ge(q_in[s % 2], 16 * (2 * j + s // 2 + 1))
                    if s == 0:
                        pe.wait_ge(kt_lo, 3 * (j + 1))
                wait(pe, t_rdy, 16 * j + 4 * s + h - 1)
                q = [q_s[:, s % 2, k, h * S:(h + 1) * S] for k in range(2)]
                k_ = [kTh[:, par, s, 0:SEQ], kTl[:, par, s, 0:SEQ]]
                product3(pe, s_bank[h % 2][0:S, 0:SEQ], lambda c: q[0], lambda c: q[1],
                         lambda c: k_[0], lambda c: k_[1], range(1)).then_inc(s_done, 1)

            def transpose_probs(n, s, c):
                if c == 0:
                    pe.wait_ge(p_rdy, 4 * n + 4)
                    wait(pe, pt_lo, 3 * n)
                if c == 2:
                    pe.wait_ge(pt_lo, 3 * n + 1)
                for h in range(XG):
                    mm = pe.transpose(t_bank[c % 2][0:KT, h * S:(h + 1) * S],
                                      probs[:, s % 2, h, c * KT:(c + 1) * KT], ident_s[0:S, 0:S])
                mm.then_inc(pt_done, 1)

            def values_product(n, kv, j):
                if kv == 0:
                    pe.wait_ge(v_lo, 3 * (j + 1))
                pe.wait_ge(pt_lo, 3 * n + 3)
                wait(pe, o_lo, n)
                cols = slice(kv * XHD, (kv + 1) * XHD)
                product3(pe, o_bank[:, 0:XG * S], lambda c: Vh[:, c, cols], lambda c: Vl[:, c, cols],
                         lambda c: pTh[:, c, :], lambda c: pTl[:, c, :], range(KC)).then_inc(o_done, 1)

            def values(j, c):
                if c == 2 and not (isinstance(j, int) and j == 0):
                    pe.wait_ge(v_lo, 3 * j + 1)
                product3(pe, value_bank(j, c)[0:KT, :], lambda i: ctxh[:, c, i, :], lambda i: ctxl[:, c, i, :],
                         lambda i: Wvh[:, i, :], lambda i: Wvl[:, i, :], range(DC)).then_inc(v_done, 1)

            def keys(jn, c, chunks=range(DC)):
                if chunks[0] == 0:
                    pe.wait_ge(ctx_lo, 3 * jn + c + 1)
                    if c < 2:
                        wait(pe, v_lo, 3 * (jn - 1) + c + 2)
                    elif not (isinstance(jn, int) and jn == 0):
                        pe.wait_ge(k_ev, 3 * jn + 2)
                mm = product3(pe, key_bank(jn, c)[0:KT, :], lambda i: ctxh[:, c, i, :],
                              lambda i: ctxl[:, c, i, :], lambda i: Wkh[:, i, :], lambda i: Wkl[:, i, :],
                              chunks, first=chunks[0] == 0, last=chunks[-1] == DC - 1)
                if chunks[-1] == DC - 1:
                    mm.then_inc(k_done, 1)

            def transpose_keys(jn, c):
                pe.wait_ge(k_rdy, 3 * jn + c + 1)
                if c == 1:
                    pe.wait_ge(kt_lo, 3 * jn + 1)
                for kv in range(XKV):
                    mm = pe.transpose(kv_bank[KEY_T_BANK[c]][:, kv * KT:(kv + 1) * KT],
                                      kn[:, c % 2, kv * XHD:(kv + 1) * XHD], ident_s[0:KT, 0:KT])
                mm.then_inc(kt_done, 1)

            def output(j, kv, heads=range(XG)):
                if heads[0] == 0:
                    pe.wait_ge(o_lo, 4 * j + kv + 1)
                if kv == 0 and heads[0] == 0:
                    wait(pe, ysum, j)
                mm = product3(pe, y_bank[0:S, :], lambda h: oTh[:, kv, h * S:(h + 1) * S],
                              lambda h: oTl[:, kv, h * S:(h + 1) * S], lambda h: Woh[:, XG * kv + h, :],
                              lambda h: Wol[:, XG * kv + h, :], heads, first=kv == 0 and heads[0] == 0,
                              last=kv == XKV - 1 and heads[-1] == XG - 1)
                if kv == XKV - 1 and heads[-1] == XG - 1:
                    mm.then_inc(y_done, 1)

            pe.wait_ge(w_lo, 2)
            keys(0, 0)
            keys(0, 1)
            keys(0, 2)
            pe.wait_ge(w_lo, KV_PIECES)
            pe.wait_ge(consts, 64)
            for c in range(KC):
                values(0, c)
                transpose_keys(0, c)

            def body(j, par):
                first, last, past = kinds(j)
                for s in range(1 if past else 4):
                    n, before = 4 * j + s, not (first and s == 0)
                    now = not past
                    def quarter(q):
                        if s < 2 and not first:
                            output(j - 1, s + 2, (q,))
                        if s >= 2 and not last:
                            keys(j + 1, s - 1, (q,))

                    for h in range(3):
                        if now:
                            scores(j, s, h, par)
                        if before:
                            transpose_probs(n - 1, (s + 3) % 4, h)
                        quarter(h)
                    if now:
                        scores(j, s, 3, par)
                    quarter(3)
                    if s == 0 and now and not first:
                        values(j, 0)
                    if s == 1 and not last:
                        keys(j + 1, 0)
                    if s >= 2 and first:
                        pe.wait_ge(w_lo, KV_PIECES + 2 * (s - 1))
                    if s == 2:
                        output(j, 0)
                    if s == 3:
                        output(j, 1, range(XG // 2))
                    if before:
                        values_product(n - 1, (s + 3) % 4, j)
                    if s == 0 and now and not first:
                        values(j, 1)
                        values(j, 2)
                    if s in (2, 3) and not last:
                        transpose_keys(j + 1, s - 2)
                    if s == 3:
                        if not last:
                            transpose_keys(j + 1, 2)
                        output(j, 1, range(XG // 2, XG))
                if past:
                    output(j - 1, 3)
                elif first:
                    pe.wait_ge(w_lo, len(pieces))
            over_batches(pe, body)

        @block.scalar
        def _(act):
            def split_hi(n):
                act.wait_ge(w_raw[n % 2], 16 * (n // 2 + 1))
                act.activation(pieces[n][1], stage[:, n % 2], ACT.Copy).then_inc(w_hi, 1)

            def keys_hi(jn, c, par):
                act.wait_ge(kt_done, 3 * jn + c + 1)
                act.activation(kTh[:, par, :, c * KT:(c + 1) * KT],
                               kv_bank[KEY_T_BANK[c]][:, 0:XKV * KT].rearrange("d (k t) -> d k t", k=XKV),
                               ACT.Copy).then_inc(kt_hi, 1)

            def values_hi(j, c):
                act.wait_ge(v_done, 3 * j + c + 1)
                act.activation(Vh[:, c, :], value_bank(j, c)[0:KT, :], ACT.Copy).then_inc(v_hi, 1)

            def probs_hi(n, c):
                act.wait_ge(pt_done, 3 * n + c + 1)
                act.activation(pTh[:, c, :], t_bank[c % 2][0:KT, 0:XG * S], ACT.Copy).then_inc(pt_hi, 1)

            def exponent(j, s, h):
                act.wait_ge(t_rdy, 16 * j + 4 * s + h + 1)
                p = probs[:, s % 2, h, 0:SE]
                act.activation(p, p, ACT.Exp, scale=-1.0, bias=nmax[:, s % 2, h:h + 1],
                               accum_out=psums[:, s % 2, h:h + 1]).then_inc(e_rdy, 1)

            for n in range(KV_PIECES):
                split_hi(n)
            act.wait_ge(consts, 64)
            for c in range(KC):
                values_hi(0, c)
                keys_hi(0, c, 0)

            def body(j, par):
                first, last, past = kinds(j)
                for s in range(1 if past else 4):
                    n, before, now = 4 * j + s, not (first and s == 0), not past
                    for h in range(3):
                        if before:
                            probs_hi(n - 1, h)
                        if now:
                            exponent(j, s, h)
                    if now:
                        exponent(j, s, 3)
                    if first:
                        for k in range(2):
                            split_hi(KV_PIECES + 2 * s + k)
                    if before:
                        kv = (s + 3) % 4
                        act.wait_ge(o_done, n)
                        act.activation(oTh[:, kv, :], o_bank[:, 0:XG * S], ACT.Identity,
                                       bias=bv_s[:, kv:kv + 1]).then_inc(o_hi, 1)
                    if s == 0 and now and not first:
                        for c in range(KC):
                            values_hi(j, c)
                    if s in (2, 3) and not last:
                        keys_hi(j + 1, s - 2, 1 - par)
                    if s == 3 and not last:
                        keys_hi(j + 1, 2, 1 - par)
            over_batches(act, body)

        @block.vector
        def _(dve):
            def split_lo(n):
                dve.wait_ge(w_hi, n + 1)
                dve.tensor_tensor(pieces[n][2], stage[:, n % 2], pieces[n][1].bitcast(F32),
                                  ALU.subtract).then_inc(w_lo, 1)

            def key_squares(jn, c):
                if c == 2:
                    dve.wait_ge(kt_done, 3 * jn + 1)
                dve.wait_ge(k_done, 3 * jn + c + 1)
                dve.tensor_tensor(kn[:, c % 2, :], key_bank(jn, c)[0:KT, :], bk_s[:], ALU.add).then_inc(k_ev, 1)
                wait(dve, k_ss, 3 * jn + c)
                dve.wait_ge(k_ev, 3 * jn + c + 1)
                for kv in range(XKV):
                    k_ = kn[:, c % 2, kv * XHD:(kv + 1) * XHD]
                    t = dve.tensor_tensor_reduce(out=junk[:, kv * XHD:(kv + 1) * XHD], in0=k_, in1=k_, scale=1.0,
                                                 scalar=0.0, op0=ALU.mult, op1=ALU.add,
                                                 accum_out=kss[:, c, kv:kv + 1])
                t.then_inc(k_ss, 1)

            def key_norm(jn, c):
                dve.wait_ge(k_rs, 2 * (3 * jn + c + 1))
                k4 = kn[:, c % 2, :].rearrange("t (k d) -> t k d", k=XKV)
                dve.tensor_tensor(k4, k4, krs[:, c, :].unsqueeze(2).to_broadcast([KT, XKV, XHD]),
                                  ALU.mult).then_inc(k_rdy, 1)

            def keys_lo(jn, c, par):
                dve.wait_ge(kt_hi, 3 * jn + c + 1)
                cols = slice(c * KT, (c + 1) * KT)
                dve.tensor_tensor(kTl[:, par, :, cols],
                                  kv_bank[KEY_T_BANK[c]][:, 0:XKV * KT].rearrange("d (k t) -> d k t", k=XKV),
                                  kTh[:, par, :, cols].bitcast(F32), ALU.subtract).then_inc(kt_lo, 1)

            def values_lo(j, c):
                dve.wait_ge(v_hi, 3 * j + c + 1)
                dve.tensor_tensor(Vl[:, c, :], value_bank(j, c)[0:KT, :], Vh[:, c, :].bitcast(F32),
                                  ALU.subtract).then_inc(v_lo, 1)

            def probs_lo(n, c):
                dve.wait_ge(pt_hi, 3 * n + c + 1)
                dve.tensor_tensor(pTl[:, c, :], t_bank[c % 2][0:KT, 0:XG * S], pTh[:, c, :].bitcast(F32),
                                  ALU.subtract).then_inc(pt_lo, 1)

            def masked(j, s, h):
                dve.wait_ge(s_done, 16 * j + 4 * s + h + 1)
                dve.memset(carry[:, h:h + 1], 0.0)
                dve.tensor_tensor_reduce(out=probs[:, s % 2, h, 0:SE], in0=s_bank[h % 2][0:S, 0:SE], in1=mask_s[:],
                                         scale=-1.0, scalar=BIG, op0=ALU.add, op1=ALU.min,
                                         accum_out=nmax[:, s % 2, h:h + 1]).then_inc(t_rdy, 1)

            def invert_sums(j, s, h):
                dve.wait_ge(e_rdy, 16 * j + 4 * s + h + 2)
                dve.reciprocal(rinv[:, s % 2, h:h + 2], psums[:, s % 2, h:h + 2]).then_inc(ri_set, 1)

            dve.memset(half_s[:], -0.5).then_inc(set_up, 1)
            dve.memset(rms_eps_s[:], XHD * RMS_EPS).then_inc(set_up, 1)
            dve.memset(ln_eps_s[:], LN_EPS).then_inc(set_up, 1)
            dve.memset(probs[:, :, :, SE:SEP], 0.0).then_inc(set_up, 1)
            split_lo(0)
            split_lo(1)
            dve.wait_ge(consts, 64)
            key_squares(0, 0)
            split_lo(2)
            key_squares(0, 1)
            split_lo(3)
            key_norm(0, 0)
            values_lo(0, 0)
            keys_lo(0, 0, 0)
            key_squares(0, 2)
            key_norm(0, 1)
            values_lo(0, 1)
            keys_lo(0, 1, 0)
            key_norm(0, 2)
            values_lo(0, 2)
            keys_lo(0, 2, 0)

            def body(j, par):
                first, last, past = kinds(j)
                for s in range(1 if past else 4):
                    n, before, now = 4 * j + s, not (first and s == 0), not past
                    for h in range(3):
                        if now:
                            masked(j, s, h)
                        if s == 1 and h == 0 and not first:
                            values_lo(j, 2)
                        if s == 3 and h == 0 and not last:
                            keys_lo(j + 1, 0, 1 - par)
                        if before:
                            probs_lo(n - 1, h)
                    if now:
                        masked(j, s, 3)
                        if s == 3 and not last:
                            key_squares(j + 1, 2)
                        invert_sums(j, s, 0)
                        if s in (2, 3) and not last:
                            key_norm(j + 1, s - 2)
                        invert_sums(j, s, 2)
                    if first:
                        for k in range(2):
                            split_lo(KV_PIECES + 2 * s + k)
                    if s == 1 and not first:
                        residual_norm(j - 1)
                    if s in (1, 2) and not last:
                        key_squares(j + 1, s - 1)
                    if s == 3 and not first:
                        apply_norm(j - 1)
                    if s == 3 and not last:
                        key_norm(j + 1, 2)
                    if before:
                        kv = (s + 3) % 4
                        dve.wait_ge(o_hi, n)
                        dve.scalar_tensor_tensor(out=oTl[:, kv, :], in0=o_bank[:, 0:XG * S], scalar=bv_s[:, kv:kv + 1],
                                                 in1=oTh[:, kv, :].bitcast(F32), op0=ALU.add,
                                                 op1=ALU.subtract).then_inc(o_lo, 1)
                    if s == 0 and now and not first:
                        values_lo(j, 0)
                        values_lo(j, 1)
                    if s == 3 and not last:
                        keys_lo(j + 1, 1, 1 - par)
                        keys_lo(j + 1, 2, 1 - par)
                    if s == 3 and not first:
                        dve.wait_ge(x2_out, 16 * j)
                if past:
                    residual_norm(j - 1)
                    apply_norm(j - 1)

            def residual_norm(j):
                dve.wait_ge(x1_in, 16 * (j + 1))
                dve.wait_ge(y_done, j + 1)
                dve.tensor_tensor(y_s[:], y_bank[0:S, :], x1_s[:], ALU.add).then_inc(ysum, 1)
                dve.wait_ge(ysum, j + 1)
                dve.bn_stats(stat[:], y_s[:]).then_inc(stat_set, 1)
                dve.wait_ge(stat_set, j + 1)
                dve.memset(carry[:, XG:XG + 1], 0.0)
                dve.bn_aggr(mv[:], stat[:]).then_inc(mv_set, 1)

            def apply_norm(j):
                dve.wait_ge(rstd_set, 2 * (j + 1))
                dve.tensor_scalar(y_s[:], y_s[:], mv[:, 0:1], rstd[:, 0:1], ALU.subtract,
                                  ALU.mult).then_inc(x2_rdy, 1)
            over_batches(dve, body)

        @block.gpsimd
        def _(pool):
            def carry_wait(k):
                pool.tensor_tensor(pcarry[:, k:k + 1], half_s[:, 0:1], half_s[:, 0:1], ALU.add)

            def split_ctx(jn, c):
                pool.wait_ge(ctx_in[c % 2], ctx_loads(jn, c))
                wait(pool, v_done, 3 * (jn - 1) + c + 1)
                carry_wait(c)
                pool.tensor_scalar(ctxh[:, c], ctxr[:, c % 2], 1.0, 1.0, ALU.mult, ALU.mult).then_inc(ctx_hi, 1)
                pool.wait_ge(ctx_hi, 3 * jn + c + 1)
                pool.tensor_tensor(ctxl[:, c], ctxr[:, c % 2], ctxh[:, c].bitcast(F32),
                                   ALU.subtract).then_inc(ctx_lo, 1)

            def key_rsqrt(jn, c):
                k = 3 * jn + c
                pool.wait_ge(k_ss, k + 1)
                pool.tensor_tensor(krs[:, c, :], kss[:, c, :], rms_eps_s[0:KT, :], ALU.add).then_inc(k_rs, 1)
                pool.wait_ge(k_rs, 2 * k + 1)
                pool.tensor_tensor(krs[:, c, :], krs[:, c, :], half_s[0:KT, :], ALU.pow).then_inc(k_rs, 1)

            def normalise(j, s):
                n = 4 * j + s
                for h in range(XG):
                    if h % 2 == 0:
                        pool.wait_ge(ri_set, 2 * n + 1 + h // 2)
                        carry_wait(4 + 2 * s + h // 2)
                    p = probs[:, s % 2, h, 0:SE]
                    pool.tensor_scalar(p, p, rinv[:, s % 2, h:h + 1], 1.0, ALU.mult, ALU.mult).then_inc(p_rdy, 1)

            pool.wait_ge(set_up, 4)
            for c in range(KC):
                split_ctx(0, c)
            for c in range(KC):
                key_rsqrt(0, c)

            def body(j, par):
                first, last, past = kinds(j)
                if not past:
                    normalise(j, 0)
                    if not last:
                        split_ctx(j + 1, 0)
                        split_ctx(j + 1, 1)
                    normalise(j, 1)
                    if not last:
                        key_rsqrt(j + 1, 0)
                        split_ctx(j + 1, 2)
                    normalise(j, 2)
                    if not last:
                        key_rsqrt(j + 1, 1)
                if not first:
                    pool.wait_ge(mv_set, j)
                    pool.tensor_tensor(rstd[:], mv[:, 1:2], ln_eps_s[0:S, :], ALU.add).then_inc(rstd_set, 1)
                    pool.wait_ge(rstd_set, 2 * j - 1)
                    pool.tensor_tensor(rstd[:], rstd[:], half_s[0:S, 0:1], ALU.pow).then_inc(rstd_set, 1)
                if not past:
                    if not last:
                        key_rsqrt(j + 1, 2)
                    normalise(j, 3)
            over_batches(pool, body)



def feed_forward_phase(nc, sem, x2_d, router_w, router_b, expert_w, expert_b, proj_w, proj_b, norm_w, tri, sel, ident, out):
    with ExitStack() as ctx:
        def sb(name, shape, dt=F32):
            return ctx.enter_context(nc.sbuf_tensor(name, shape, dt))

        ident_s = sb("c_ident", [P, P])
        small = sb("c_small", [P, 32])
        half_s, rms_eps_s, ln_eps_s = small[:, 0:1], small[:, 1:2], small[:, 2:3]
        ss, rr, rstd = [[small[0:S, k + t:k + t + 1] for t in range(GB)] for k in (3, 7, 11)]
        mv = [small[0:S, 15 + 2 * t:17 + 2 * t] for t in range(GB)]
        carry = small[0:S, 23:23 + GB]
        rb_s, tri_s = sb("c_rb", [S, E]), sb("c_tri", [S, E, E])
        eb_s = sb("c_eb", [P, E, DC])
        pb_s, nw_s = sb("c_pb", [S, D]), sb("c_nw", [S, D])
        rw_s = sb("c_rw", [P, DC, E])
        selr = sb("c_selr", [E, E, P], F32R)
        Eh, El = sb("c_Eh", [P, E, DC, D], F32R), sb("c_El", [P, E, DC, D], F32R)
        Ph, Pl = sb("c_Ph", [P, DC, D], F32R), sb("c_Pl", [P, DC, D], F32R)
        x2n = sb("c_x2n", [S, D])
        xTr = sb("c_xTr", [P, DC, GT])
        xTh = sb("c_xTh", [P, DC, GT], F32R)
        with nc.sbuf_tensor("c_sums", [S, GB - 1, D], F32) as sums:
            pass
        xTl = sb("c_xTl", [P, DC, GT], F32R)
        logit, dlogit, elogit = sb("c_logit", [S, GB, E]), sb("c_dlogit", [S, GB, E]), sb("c_elogit", [S, GB, E])
        lmax, rank, picked = sb("c_lmax", [S, GB]), sb("c_rank", [S, GB, E]), sb("c_picked", [S, GB, E])
        wsum, winv = sb("c_wsum", [S, GB]), sb("c_winv", [S, GB])
        above, equal = sb("c_above", [S, GB, E, E]), sb("c_equal", [S, GB, E, E])
        weight = sb("c_weight", [S, GB, E])
        wTh, wTl = sb("c_wTh", [E, GT], F32R), sb("c_wTl", [E, GT], F32R)
        act_s = sb("c_act", [P, 2, GT])
        acc = sb("c_acc", [P, DC, GT])
        with nc.sbuf_tensor("c_raw", [P, 6, D], F32) as raw:
            pass
        combh, combl = sb("c_combh", [P, DC, GT], F32R), sb("c_combl", [P, DC, GT], F32R)
        x2r = sb("c_x2r", [P, 2, D])
        u_s = sb("c_u", [S, D])
        def flat(a):
            return a.rearrange("p c t -> p (c t)")

        stage = [x2r[:, 0], x2r[:, 1]]
        stage += [raw[:, k] for k in range(6)]
        NST = len(stage)
        x2_first = [x2n[:], u_s[:], flat(act_s[:])[0:S, 0:D]]
        x2_last = [flat(xTr[:])[0:S, k * D:(k + 1) * D] for k in range(3)] + [x2n[:]]
        u_last = [u_s[:]] + [sums[:, k] for k in range(GB - 1)]

        def x2_tile(g, t):
            return x2_last[t] if isinstance(g, int) and g == G - 1 else x2r[0:S, t % 2]

        def u_tile(g, t):
            return u_last[t] if isinstance(g, int) and g == G - 1 else u_s[:]
        stat = sb("c_stat", [S, GB, 6])

        bank = [ctx.enter_context(nc.psum_tensor(f"c_bank{k}", [P, 512], F32)) for k in range(8)]
        h_bank, w_bank, x_bank, l_bank = bank[0:2], bank[2:4], bank[4], bank[6]
        p_bank = (bank[5], bank[7])

        consts, set_up = sem("c_consts"), sem("c_set_up")
        w_raw, w_hi, w_lo = [sem(f"c_w_raw{k}") for k in range(NST)], sem("c_w_hi"), sem("c_w_lo")
        rw_in, x2f_in, x2l_in = sem("rw_in"), [sem(f"x2f_in{k}") for k in range(3)], [sem(f"x2l_in{k}") for k in range(GB)]
        xt_used = sem("c_xt_used")
        x2n_in, xt_done, xt_ev, xt_hi, xt_lo = sem("x2n_in"), sem("c_xt_done"), sem("c_xt_ev"), sem("c_xt_hi"), sem("c_xt_lo")
        lg_done, route, exp_rdy = sem("lg_done"), sem("route"), sem("exp_rdy")
        wt_done, wt_hi, wt_lo, wb_done = sem("wt_done"), sem("wt_hi"), sem("wt_lo"), sem("wb_done")
        h_done, act_rdy, mul_done, acc_done = sem("h_done"), sem("act_rdy"), sem("mul_done"), sem("acc_done")
        c_hi, c_lo, p_done = sem("c_hi"), sem("c_lo"), sem("p_done")
        x2r_in, x2p_set, u_rdy, sq_done = [sem("x2r_in0"), sem("x2r_in1")], sem("x2p_set"), sem("u_rdy"), sem("sq_done")
        rr_set, v_rdy, z_rdy = sem("rr_set"), sem("v_rdy"), sem("z_rdy")
        stat_set, mv_set, rstd_set = sem("c_stat_set"), sem("c_mv_set"), sem("c_rstd_set")
        o_rdy, out_in, nw_set, sel_set = sem("c_out_rdy"), sem("out_in"), sem("nw_set"), sem("sel_set")
        NR = 13
        NE = E * DC

        pieces = [(expert_w[e, :, c], Eh[:, e, c], El[:, e, c]) for e in range(E) for c in range(DC)]
        pieces += [(proj_w[:, c], Ph[:, c], Pl[:, c]) for c in range(DC)]

        def splits_after(e, m):
            k = DC * e + m
            first = DC + k + min(e, DC)
            if e >= E - 1:
                return []
            return [first, first + 1] if m == DC - 1 and e < DC else [first]

        RESIDUAL_AT = ((2, 0), (3, 3), (5, 0), (6, 2))
        SQUARE_AT = ((2, 1), (4, 0), (5, 1), (6, 3))
        RMS_AT = ((2, 2), (4, 1), (5, 3), (7, 0))
        NORM_AT = ((3, 0), (4, 2), (6, 0), (7, 1))

        def over_groups(eng, body):
            body(0)
            with eng.Fori(1, G - 1) as g:
                body(g)
            body(G - 1)
            body(G)

        def kinds(g):
            return [not (isinstance(g, int) and g == 0), not (isinstance(g, int) and g == G),
                    not (isinstance(g, int) and g >= G - 1)]

        block = ctx.enter_context(nc.Block())

        @block.sync
        def _(sp):
            def tile(g, t):
                return x2_d[bass.ds(GB * g + t, 1)].rearrange("a t d -> t (a d)")

            def load_x2n(g, t):
                wait(sp, xt_done, 4 * g + t)
                sp.dma_start(x2n[:], tile(g, t)).then_inc(x2n_in, 16)

            def load_x2_first(t):
                if t == 3:
                    sp.wait_ge(xt_done, 1)
                sp.dma_start(x2_first[t % 3], tile(0, t)).then_inc(x2f_in[t % 3], 16)

            def load_x2r(g, t):
                sp.dma_start(x2r[0:S, t % 2], tile(g, t)).then_inc(x2r_in[t % 2], 16)

            def load_weights(n):
                if n >= NST:
                    sp.wait_ge(w_lo, n - NST + 1)
                sp.dma_start(stage[n % NST], pieces[n][0]).then_inc(w_raw[n % NST], 16)

            load_x2_first(0)
            sp.dma_start(ident_s[:], ident).then_inc(consts, 16)
            load_x2_first(1)
            load_x2_first(2)
            sp.dma_start(rw_s[:], router_w).then_inc(rw_in, 16)
            load_weights(0)
            load_weights(1)
            load_x2_first(3)
            load_weights(2)
            load_weights(3)
            half = E * P // 2
            for k in range(2):
                sp.dma_start(acc[0:E, 2 * k:2 * k + 2].rearrange("p a b -> p (a b)")[:, 0:half],
                             sel[:, k * half:(k + 1) * half]).then_inc(consts, 16)
            for a, b in ((rb_s[:], router_b.partition_broadcast(S)), (tri_s[:], tri), (eb_s[:], expert_b)):
                sp.dma_start(a, b).then_inc(consts, 16)
            for n in range(4, NST):
                load_weights(n)
            sp.dma_start(pb_s[:], proj_b.partition_broadcast(S)).then_inc(consts, 16)
            sp.dma_start(nw_s[:], norm_w.partition_broadcast(S)).then_inc(consts, 16)

            def body(g):
                back, now, front = kinds(g)
                if not back:
                    for n in range(NST, len(pieces)):
                        if n % 5 == 0 and n // 5 in range(2, 2 + GB):
                            load_x2n(1, n // 5 - 2)
                        load_weights(n)
                    sp.wait_ge(w_lo, len(pieces))
                if back and not now:
                    for t in range(GB):
                        sp.wait_ge(o_rdy, 4 * (g - 1) + t + 1)
                        sp.dma_start(out[GB * (g - 1) + t], u_last[t]).then_inc(out_in, 16)
                    return
                for t in range(GB):
                    if back and front:
                        load_x2n(g + 1, t)
                    if back and t < 2:
                        load_x2r(g - 1, t)
                for t in range(GB):
                    if back:
                        sp.wait_ge(o_rdy, 4 * (g - 1) + t + 1)
                        dst = out[bass.ds(GB * (g - 1) + t, 1)].rearrange("a t d -> t (a d)")
                        sp.dma_start(dst, u_s[:]).then_inc(out_in, 16)
                        if t < 2:
                            load_x2r(g - 1, t + 2)
                    if now and not front:
                        if t == 0:
                            sp.wait_ge(xt_lo, DC * G)
                        sp.dma_start(x2_last[t], tile(g, t)).then_inc(x2l_in[t], 16)
            over_groups(sp, body)
            sp.wait_ge(out_in, 16 * B)

        @block.tensor
        def _(pe):
            def transpose_x2(g, t):
                first = isinstance(g, int) and g == 0
                if first:
                    pe.wait_ge(x2f_in[t % 3], 16 * (t // 3 + 1))
                else:
                    pe.wait_ge(x2n_in, 16 * (4 * (g - 1) + t + 1))
                wait(pe, xt_ev, 4 * g + t)
                for c in range(DC):
                    src = x2_first[t % 3] if first else x2n[:]
                    mm = pe.transpose(x_bank[:, c * S:(c + 1) * S], src[:, c * P:(c + 1) * P], ident_s[0:S, 0:S])
                mm.then_inc(xt_done, 1)

            def logits(g):
                pe.wait_ge(xt_ev, 4 * g + 4)
                for t in range(GB):
                    for c in range(DC):
                        mm = pe.matmul(l_bank[0:S, t * E:(t + 1) * E], lhsT=xTr[:, c, t * S:(t + 1) * S],
                                       rhs=rw_s[:, c, :], start=c == 0, stop=c == DC - 1)
                mm.then_inc(lg_done, 1)

            def transpose_weights(g):
                pe.wait_ge(route, NR * (g + 1))
                for t in range(GB):
                    mm = pe.transpose(l_bank[0:E, t * S:(t + 1) * S], weight[:, t, :], ident_s[0:S, 0:S])
                mm.then_inc(wt_done, 1)

            def spread_weights(g, e):
                if e == 0:
                    pe.wait_ge(wt_lo, g + 1)
                wait(pe, mul_done, 4 * (E * g + e - 1))
                pe.matmul(w_bank[e % 2][:, 0:GT], lhsT=selr[:, e, :], rhs=wTh[:], start=True, stop=False)
                pe.matmul(w_bank[e % 2][:, 0:GT], lhsT=selr[:, e, :], rhs=wTl[:], start=False,
                          stop=True).then_inc(wb_done, 1)

            def expert(g, e, m):
                k = NE * g + DC * e + m
                wait(pe, act_rdy, k - 1)
                cols = slice(m * P, (m + 1) * P)
                for c in range(DC):
                    if e == 0 and m == 0:
                        pe.wait_ge(xt_lo, DC * g + c + 1)
                    mm = product3(pe, h_bank[m % 2][:, 0:GT], lambda c: Eh[:, e, c, cols], lambda c: El[:, e, c, cols],
                                  lambda c: xTh[:, c, :], lambda c: xTl[:, c, :], [c], first=c == 0, last=c == DC - 1)
                mm.then_inc(h_done, 1)

            def last_outputs(g):
                e = E - 1
                pe.wait_ge(act_rdy, NE * (g + 1) - DC + 1)
                pe.wait_ge(act_rdy, NE * (g + 1) - DC + 2)
                for c in range(DC):
                    for m in (2, 3):
                        cols = slice(m * P, (m + 1) * P)
                        mm = product3(pe, h_bank[m % 2][:, 0:GT], lambda c: Eh[:, e, c, cols], lambda c: El[:, e, c, cols],
                                      lambda c: xTh[:, c, :], lambda c: xTl[:, c, :], [c], first=c == 0, last=c == DC - 1)
                        if c == DC - 1:
                            mm.then_inc(h_done, 1)
                    if c < DC - 1:
                        mm.then_inc(xt_used, 1)

            def project(g, t):
                if t >= 2:
                    pe.wait_ge(sq_done, 4 * g + t - 1)
                cols = slice(t * S, (t + 1) * S)
                for m in range(DC):
                    if t == 0:
                        pe.wait_ge(c_lo, DC * g + m + 1)
                    mm = product3(pe, p_bank[t % 2][0:S, :], lambda m: combh[:, m, cols], lambda m: combl[:, m, cols],
                                  lambda m: Ph[:, m, :], lambda m: Pl[:, m, :], [m], first=m == 0, last=m == DC - 1)
                mm.then_inc(p_done, 1)

            pe.wait_ge(consts, 16)
            for t in range(GB):
                transpose_x2(0, t)
            pe.wait_ge(rw_in, 16)
            logits(0)

            def body(g):
                back, now, front = kinds(g)
                if not now:
                    for t in range(GB):
                        project(g - 1, t)
                    return
                for e in range(E):
                    if not back:
                        pe.wait_ge(w_lo, DC * (e + 1))
                    for m in range(DC):
                        if e < E - 1 or m < 2:
                            expert(g, e, m)
                        elif m == 2:
                            last_outputs(g)
                        if e == 0 and m == 1:
                            if not back:
                                pe.wait_ge(sel_set, 2)
                                transpose_weights(0)
                            spread_weights(g, 0)
                        if e and m == 0:
                            spread_weights(g, e)
                    if front:
                        if e < GB:
                            transpose_x2(g + 1, e)
                        if e == 4:
                            logits(g + 1)
                        if e == 6:
                            transpose_weights(g + 1)
                    if back and e in (1, 2, 4, 5):
                        project(g - 1, (1, 2, 4, 5).index(e))
                if not back:
                    pe.wait_ge(w_lo, len(pieces))
            over_groups(pe, body)

        @block.scalar
        def _(act):
            def split_hi(n):
                act.wait_ge(w_raw[n % NST], 16 * (n // NST + 1))
                act.activation(pieces[n][1], stage[n % NST], ACT.Copy).then_inc(w_hi, 1)

            def copy_x2(g, t):
                act.wait_ge(xt_done, 4 * g + t + 1)
                act.activation(xTr[:, :, t * S:(t + 1) * S], x_bank[:, 0:DC * S].rearrange("p (c t) -> p c t", c=DC),
                               ACT.Copy).then_inc(xt_ev, 1)

            def x2_hi(g, c):
                act.wait_ge(xt_ev, 4 * g + 4)
                if c < DC - 1:
                    wait(act, xt_used, (DC - 1) * (g - 1) + c + 1)
                else:
                    wait(act, h_done, NE * g)
                act.activation(xTh[:, c], xTr[:, c], ACT.Copy).then_inc(xt_hi, 1)

            def exponent(g):
                act.wait_ge(route, NR * g + 3)
                act.activation(elogit[:], dlogit[:], ACT.Exp).then_inc(exp_rdy, 1)

            def weights_hi(g):
                act.wait_ge(wt_done, g + 1)
                wait(act, wb_done, E * g)
                act.activation(wTh[:], l_bank[0:E, 0:GT], ACT.Copy).then_inc(wt_hi, 1)

            def silu(g, e, m):
                k = NE * g + DC * e + m
                act.wait_ge(h_done, k + 1)
                wait(act, acc_done, k - 1)
                act.activation(act_s[:, m % 2], h_bank[m % 2][:, 0:GT], ACT.Silu,
                               bias=eb_s[:, e, m:m + 1]).then_inc(act_rdy, 1)

            def combined_hi(g, m):
                act.wait_ge(acc_done, NE * (g + 1) - DC + m + 1)
                wait(act, p_done, 4 * g)
                act.activation(combh[:, m], acc[:, m], ACT.Copy).then_inc(c_hi, 1)

            def square(g, t):
                act.wait_ge(u_rdy, 4 * g + t + 1)
                act.activation(p_bank[t % 2][0:S, :], u_tile(g, t), ACT.Square, accum_out=ss[t]).then_inc(sq_done, 1)

            for t in range(GB):
                copy_x2(0, t)
            for c in range(DC):
                x2_hi(0, c)
            for n in range(DC):
                split_hi(n)
            act.wait_ge(consts, 16 * 8)
            for k in range(2):
                half = E * P // 2
                act.activation(selr[:, k * E // 2:(k + 1) * E // 2].rearrange("p a b -> p (a b)"),
                               acc[0:E, 2 * k:2 * k + 2].rearrange("p a b -> p (a b)")[:, 0:half],
                               ACT.Copy).then_inc(sel_set, 1)
            exponent(0)

            def body(g):
                back, now, front = kinds(g)
                if not now:
                    for t in range(GB):
                        square(g - 1, t)
                    return
                for e in range(E):
                    for m in range(DC):
                        if front and e == E - 1 and m == 2:
                            for c in range(DC - 1):
                                x2_hi(g + 1, c)
                        silu(g, e, m)
                        if front and e == E - 1 and m == 2:
                            x2_hi(g + 1, DC - 1)
                        if not back:
                            if (e, m) == (0, 1):
                                weights_hi(0)
                            for n in splits_after(e, m):
                                split_hi(n)
                        if front and 1 <= e <= GB and m == 0:
                            copy_x2(g + 1, e - 1)
                        if back and (e, m) in SQUARE_AT:
                            square(g - 1, SQUARE_AT.index((e, m)))
                        if front and (e, m) == (5, 3):
                            exponent(g + 1)
                if front:
                    weights_hi(g + 1)
                for m in range(DC):
                    combined_hi(g, m)
            over_groups(act, body)

        @block.vector
        def _(dve):
            def split_lo(n):
                dve.wait_ge(w_hi, n + 1)
                dve.tensor_tensor(pieces[n][2], stage[n % NST], pieces[n][1].bitcast(F32),
                                  ALU.subtract).then_inc(w_lo, 1)

            def x2_lo(g, c):
                dve.wait_ge(xt_hi, DC * g + c + 1)
                dve.tensor_tensor(xTl[:, c], xTr[:, c], xTh[:, c].bitcast(F32), ALU.subtract).then_inc(xt_lo, 1)

            def spread(a):
                return a.unsqueeze(2).to_broadcast([S, GB, E])

            def rank_logits(g):
                step = NR * g
                dve.wait_ge(lg_done, g + 1)
                dve.tensor_tensor(logit[:], l_bank[0:S, 0:GB * E].rearrange("t (b e) -> t b e", b=GB),
                                  rb_s[:].unsqueeze(1).to_broadcast([S, GB, E]), ALU.add).then_inc(route, 1)
                dve.wait_ge(route, step + 1)
                dve.tensor_reduce(lmax[:], logit[:], AX.X, ALU.max).then_inc(route, 1)
                dve.wait_ge(route, step + 2)
                dve.tensor_tensor(dlogit[:], logit[:], spread(lmax[:]), ALU.subtract).then_inc(route, 1)
                mine = logit[:].unsqueeze(3).to_broadcast([S, GB, E, E])
                other = logit[:].unsqueeze(2).to_broadcast([S, GB, E, E])
                dve.tensor_tensor(above[:], other, mine, ALU.is_gt).then_inc(route, 1)
                dve.tensor_tensor(equal[:], other, mine, ALU.is_equal).then_inc(route, 1)
                dve.wait_ge(route, step + 5)
                dve.tensor_tensor(equal[:], equal[:], tri_s[:].unsqueeze(1).to_broadcast([S, GB, E, E]),
                                  ALU.mult).then_inc(route, 1)
                dve.wait_ge(route, step + 6)
                dve.tensor_tensor(above[:], above[:], equal[:], ALU.add).then_inc(route, 1)
                dve.wait_ge(route, step + 7)
                dve.tensor_reduce(rank[:], above[:], AX.X, ALU.add).then_inc(route, 1)
                dve.wait_ge(route, step + 8)
                dve.tensor_scalar(picked[:], rank[:], 1.5, None, ALU.is_lt).then_inc(route, 1)

            def weigh(g):
                step = NR * g
                dve.wait_ge(route, step + 9)
                dve.wait_ge(exp_rdy, g + 1)
                dve.tensor_tensor(picked[:], picked[:], elogit[:], ALU.mult).then_inc(route, 1)
                dve.wait_ge(route, step + 10)
                dve.tensor_reduce(wsum[:], picked[:], AX.X, ALU.add).then_inc(route, 1)
                dve.wait_ge(route, step + 11)
                dve.reciprocal(winv[:], wsum[:]).then_inc(route, 1)
                dve.wait_ge(route, step + 12)
                dve.tensor_tensor(weight[:], picked[:], spread(winv[:]), ALU.mult).then_inc(route, 1)

            def weights_lo(g):
                dve.wait_ge(wt_hi, g + 1)
                dve.tensor_tensor(wTl[:], l_bank[0:E, 0:GT], wTh[:].bitcast(F32), ALU.subtract).then_inc(wt_lo, 1)

            def weighted_sum(g, e, m):
                k = NE * g + DC * e + m
                if m == 0:
                    dve.wait_ge(wb_done, E * g + e + 1)
                a = act_s[:, m % 2]
                dve.wait_ge(act_rdy, k + 1)
                dve.tensor_tensor(a, a, w_bank[e % 2][:, 0:GT], ALU.mult).then_inc(mul_done, 1)
                dve.wait_ge(mul_done, k + 1)
                if e == 0:
                    dve.tensor_copy(acc[:, m], a).then_inc(acc_done, 1)
                else:
                    dve.tensor_tensor(acc[:, m], acc[:, m], a, ALU.add).then_inc(acc_done, 1)

            def combined_lo(g, m):
                dve.wait_ge(c_hi, DC * g + m + 1)
                dve.tensor_tensor(combl[:, m], acc[:, m], combh[:, m].bitcast(F32), ALU.subtract).then_inc(c_lo, 1)

            def residual(g, t):
                dve.wait_ge(p_done, 4 * g + t + 1)
                dve.wait_ge(x2p_set, 4 * g + t + 1)
                u = u_tile(g, t)
                dve.tensor_tensor(u, p_bank[t % 2][0:S, :], u, ALU.add).then_inc(u_rdy, 1)

            def rms_norm(g, t):
                k, u = 4 * g + t, u_tile(g, t)
                dve.wait_ge(rr_set, 2 * (k + 1))
                dve.scalar_tensor_tensor(out=u, in0=u, scalar=rr[t], in1=nw_s[:], op0=ALU.mult,
                                         op1=ALU.mult).then_inc(v_rdy, 1)
                dve.wait_ge(v_rdy, k + 1)
                dve.tensor_tensor(u, u, x2_tile(g, t), ALU.add).then_inc(z_rdy, 1)
                dve.wait_ge(z_rdy, k + 1)
                dve.bn_stats(stat[:, t], u).then_inc(stat_set, 1)
                dve.wait_ge(stat_set, k + 1)
                dve.memset(carry[:, t:t + 1], 0.0)
                dve.bn_aggr(mv[t], stat[:, t]).then_inc(mv_set, 1)

            def layer_norm(g, t):
                u = u_tile(g, t)
                dve.wait_ge(rstd_set, 2 * (4 * g + t + 1))
                dve.tensor_scalar(u, u, mv[t][:, 0:1], rstd[t], ALU.subtract, ALU.mult).then_inc(o_rdy, 1)

            dve.memset(half_s, -0.5).then_inc(set_up, 1)
            dve.memset(rms_eps_s, D * RMS_EPS).then_inc(set_up, 1)
            dve.memset(ln_eps_s, LN_EPS).then_inc(set_up, 1)
            for c in range(DC):
                x2_lo(0, c)
            for n in range(DC):
                split_lo(n)
            dve.wait_ge(consts, 16 * 8)
            rank_logits(0)
            weigh(0)
            dve.tensor_scalar(nw_s[:], nw_s[:], float(D) ** 0.5, None, ALU.mult).then_inc(nw_set, 1)
            dve.wait_ge(sel_set, 2)
            dve.wait_ge(nw_set, 1)

            def body(g):
                back, now, front = kinds(g)
                if not now:
                    for t in range(GB + 2):
                        if t < GB:
                            residual(g - 1, t)
                        if 1 <= t <= GB:
                            rms_norm(g - 1, t - 1)
                        if t >= 2:
                            layer_norm(g - 1, t - 2)
                    return
                for e in range(E):
                    for m in range(DC):
                        if front and (e, m) == (E - 1, 2):
                            for c in range(DC):
                                x2_lo(g + 1, c)
                        if not back and (e, m) == (0, 0):
                            weights_lo(0)
                        weighted_sum(g, e, m)
                        if front and (e, m) == (E - 1, 2):
                            weights_lo(g + 1)
                        if not back:
                            for n in splits_after(e, m):
                                split_lo(n)
                        if back:
                            for at, step in ((RESIDUAL_AT, residual), (RMS_AT, rms_norm), (NORM_AT, layer_norm)):
                                if (e, m) in at:
                                    step(g - 1, at.index((e, m)))
                        if front and (e, m) == (5, 2):
                            rank_logits(g + 1)
                        if front and (e, m) == (6, 1):
                            weigh(g + 1)
                for m in range(DC):
                    combined_lo(g, m)
            over_groups(dve, body)

        @block.gpsimd
        def _(pool):
            def reciprocal_root(dst, src, eps, count, k):
                pool.tensor_tensor(dst, src, eps, ALU.add).then_inc(count, 1)
                pool.wait_ge(count, 2 * k + 1)
                pool.tensor_tensor(dst, dst, half_s[0:S, :], ALU.pow).then_inc(count, 1)

            def biased_residual(g, t):
                if isinstance(g, int) and g == G - 1:
                    pool.wait_ge(x2l_in[t], 16)
                    if t == 1:
                        pool.wait_ge(h_done, NE * G)
                else:
                    pool.wait_ge(x2r_in[t % 2], 16 * (2 * g + t // 2 + 1))
                pool.tensor_tensor(u_tile(g, t), x2_tile(g, t), pb_s[:], ALU.add).then_inc(x2p_set, 1)

            def rms(g, t):
                pool.wait_ge(sq_done, 4 * g + t + 1)
                reciprocal_root(rr[t], ss[t], rms_eps_s[0:S, :], rr_set, 4 * g + t)

            def ln(g, t):
                pool.wait_ge(mv_set, 4 * g + t + 1)
                reciprocal_root(rstd[t], mv[t][:, 1:2], ln_eps_s[0:S, :], rstd_set, 4 * g + t)

            pool.wait_ge(set_up, 3)
            pool.wait_ge(consts, 16 * 8)

            def body(g):
                back, now, front = kinds(g)
                if back and now:
                    for t in range(GB):
                        biased_residual(g - 1, t)
                        rms(g - 1, t)
                        ln(g - 1, t)
                        pool.wait_ge(out_in, 16 * (4 * (g - 1) + t + 1))
                if not now:
                    for t in range(GB):
                        biased_residual(g - 1, t)
                    for t in range(GB + 1):
                        if t < GB:
                            rms(g - 1, t)
                        if t:
                            ln(g - 1, t - 1)
            over_groups(pool, body)


def build(nc, args, out):
    x1_d = nc.dram_tensor("x1_d", (B, S, D), F32, kind="Internal").ap()
    x2_d = nc.dram_tensor("x2_d", (B, S, D), F32, kind="Internal").ap()
    q_d = nc.dram_tensor("q_d", (B * XKV, P, 2, XG * S), F32, kind="Internal").ap()
    with ExitStack() as ctx:
        def sem(name):
            return ctx.enter_context(nc.semaphore(name))

        a = args
        self_attention_phase(nc, sem, a["x"], a["xT"], a["w_q"], a["w_k"], a["w_v"], a["w_o"], a["Wq"], a["bq"],
                             a["qn_w"], a["kn_w"], a["causal"], a["ident"], x1_d, q_d)
        cross_attention_phase(nc, sem, a["ctxT"], a["Wk"], a["Wv"], a["Wo"], a["bk"], a["bv"], a["mask"],
                              a["ident"], x1_d, q_d, x2_d)
        feed_forward_phase(nc, sem, x2_d, a["router_w"], a["router_b"], a["expert_w"], a["expert_b"],
                           a["proj_w"], a["proj_b"], a["norm_w"], a["tri"], a["sel"], a["ident"], out)


def layouts(inputs):
    import numpy as np

    def chunks(w):
        return w.reshape(w.shape[0] // P, P, w.shape[1]).transpose(1, 0, 2)

    a = {k: np.asarray(v) for k, v in inputs.items()}
    x, context = a["x"], a["ctx_2048"]
    padded = np.zeros((B, SEP, D), context.dtype)
    padded[:, :SE] = context
    sel = np.zeros((E, E, P), np.float32)
    sel[range(E), range(E)] = 1.0
    arrays = {
        "x": x,
        "xT": x.reshape(B // 2, 2, S, DC, P).transpose(0, 4, 3, 1, 2).reshape(B // 2, P, DC, 2 * S),
        "w_q": chunks(a["L0_attn_w_q"].T),
        "w_k": chunks(a["L0_attn_w_k"].T),
        "w_v": chunks(a["L0_attn_w_v"].T),
        "w_o": chunks(a["L0_attn_w_o"].T),
        "Wq": a["L0_xattn_Wq"].reshape(DC, P, XKV, XG * XHD).transpose(2, 1, 0, 3),
        "bq": a["L0_xattn_bq"],
        "qn_w": a["L0_xattn_qn_w"].reshape(XHD, 1),
        "kn_w": a["L0_xattn_kn_w"].reshape(XHD, 1),
        "causal": np.triu(np.full((S, S), -BIG, np.float32), 1),
        "ident": np.eye(P, dtype=np.float32),
        "ctxT": padded.reshape(B, KC, KT, DC, P).transpose(0, 1, 4, 3, 2).reshape(B * KC, P, DC, KT),
        "Wk": chunks(a["L0_xattn_Wk"]),
        "Wv": chunks(a["L0_xattn_Wv"]),
        "Wo": chunks(a["L0_xattn_Wo"]),
        "bk": a["L0_xattn_bk"],
        "bv": a["L0_xattn_bv"].reshape(XKV, XHD).T,
        "mask": a["mask_1xSxS2_ff0"].reshape(S, SE),
        "router_w": chunks(a["L0_ffn_router_w"]),
        "router_b": a["L0_ffn_router_b"],
        "expert_w": a["L0_ffn_expert_w"].reshape(E, DC, P, D).transpose(0, 2, 1, 3),
        "expert_b": a["L0_ffn_expert_b"].reshape(E, DC, P).transpose(2, 0, 1),
        "proj_w": chunks(a["L0_ffn_proj_w"]),
        "proj_b": a["L0_ffn_proj_b"],
        "norm_w": a["L0_ffn_norm_w"],
        "tri": np.broadcast_to(np.tril(np.ones((E, E), np.float32), -1), (S, E, E)),
        "sel": sel.reshape(E, E * P),
    }
    return {k: np.ascontiguousarray(v) for k, v in arrays.items()}


def kernel(**inputs):
    import concourse.bacc as bacc
    from concourse.bass_utils import run_bass_kernel_spmd

    nc = bacc.Bacc("TRN2", target_bir_lowering=False, num_devices=1)
    arrays = {f"in_{k}": v for k, v in layouts(inputs).items()}
    args = {k[3:]: nc.dram_tensor(k, v.shape, F32, kind="ExternalInput").ap() for k, v in arrays.items()}
    out = nc.dram_tensor("out", (B, S, D), F32, kind="ExternalOutput").ap()
    build(nc, args, out)
    result = run_bass_kernel_spmd(nc, [arrays], core_ids=[0])
    return result.results[0]["out"]
```
